# Optimizing a Trainium2 kernel written in Bass

```python
import numpy as np
import jax
import jax.numpy as jnp

def _softmax(x, axis=-1):
    return jax.nn.softmax(x, axis=axis)

def _gelu(x):
    return jax.nn.gelu(x, approximate=True)

def _silu(x):
    return jax.nn.silu(x)

def _sigmoid(x):
    return jax.nn.sigmoid(x)

def _layernorm(x, axis=-1, eps=1e-05):
    m = jnp.mean(x, axis=axis, keepdims=True)
    v = jnp.var(x, axis=axis, keepdims=True)
    return (x - m) / jnp.sqrt(v + eps)

def _scatter_add(tgt, idx, src, axis=0):
    return tgt.at[idx].add(src)

def _segment_sum(src, seg, n):
    return jax.ops.segment_sum(src, seg, n)
kernel_name = 'mk_seq_preln_d2_jaxref_r8_25da86'

def setup_inputs(seed: int=0):
    np.random.seed(seed)
    _w = jnp.asarray

    def _L0_attn_setup():
        import jax, jax.numpy as jnp
        import numpy as np
        HEAD_NUM = 16
        ROPE_BASE = 10000.0

        def _rotate_half(x):
            x_even = x[..., ::2]
            x_odd = x[..., 1::2]
            return jnp.stack((-x_odd, x_even), axis=-1).reshape(x.shape)

        def _rope_cos_sin(seq_len, head_dim):
            half = head_dim // 2
            inv_freq = 1.0 / ROPE_BASE ** (jnp.arange(half, dtype=jnp.float32) / half)
            t = jnp.arange(seq_len, dtype=jnp.float32)
            freqs = t[:, None] * inv_freq[None, :]
            cos = jnp.repeat(jnp.cos(freqs), 2, axis=-1)
            sin = jnp.repeat(jnp.sin(freqs), 2, axis=-1)
            return (cos, sin)
        key = jax.random.key(seed)
        ks = jax.random.split(key, 9)
        B, S, H = (2, 256, 256)
        std = 1.0 / np.sqrt(H)
        return {'x': jax.random.normal(ks[0], (B, S, H), jnp.float32), 'Wq': jax.random.normal(ks[1], (H, H), jnp.float32) * std, 'bq': jax.random.normal(ks[2], (H,), jnp.float32) * std, 'Wk': jax.random.normal(ks[3], (H, H), jnp.float32) * std, 'bk': jax.random.normal(ks[4], (H,), jnp.float32) * std, 'Wv': jax.random.normal(ks[5], (H, H), jnp.float32) * std, 'bv': jax.random.normal(ks[6], (H,), jnp.float32) * std, 'Wo': jax.random.normal(ks[7], (H, H), jnp.float32) * std, 'bo': jax.random.normal(ks[8], (H,), jnp.float32) * std}
    _L0_attn_in = _L0_attn_setup()

    def _L0_ffn_setup():
        import jax, jax.numpy as jnp
        import numpy as np
        N_GROUPS = 4
        TOPK_GROUPS = 2
        TOPK = 4
        ROUTE_SCALE = 1.0

        def _gate(xt, gate_w):
            T = xt.shape[0]
            E = gate_w.shape[0]
            scores = jax.nn.sigmoid(xt @ gate_w.T)
            original_scores = scores
            sg = scores.reshape(T, N_GROUPS, E // N_GROUPS)
            group_scores = sg.max(axis=-1)
            _, gidx = jax.lax.top_k(group_scores, TOPK_GROUPS)
            gmask = jax.nn.one_hot(gidx, N_GROUPS, dtype=scores.dtype).sum(axis=1)
            masked = (sg * gmask[:, :, None]).reshape(T, E)
            _, idx = jax.lax.top_k(masked, TOPK)
            w = jnp.take_along_axis(original_scores, idx, axis=-1)
            w = w / w.sum(axis=-1, keepdims=True) * ROUTE_SCALE
            return (w, idx)
        key = jax.random.key(seed)
        ks = jax.random.split(key, 8)
        B, S, D = (1, 256, 256)
        E, I = (16, 176)
        SH = 2 * I
        s = 0.02
        return {'x': jax.random.normal(ks[0], (B, S, D), dtype=jnp.float32), 'gate_w': jax.random.normal(ks[1], (E, D), dtype=jnp.float32) * s, 'W1': jax.random.normal(ks[2], (E, I, D), dtype=jnp.float32) * s, 'W2': jax.random.normal(ks[3], (E, D, I), dtype=jnp.float32) * s, 'W3': jax.random.normal(ks[4], (E, I, D), dtype=jnp.float32) * s, 'Ws1': jax.random.normal(ks[5], (SH, D), dtype=jnp.float32) * s, 'Ws2': jax.random.normal(ks[6], (D, SH), dtype=jnp.float32) * s, 'Ws3': jax.random.normal(ks[7], (SH, D), dtype=jnp.float32) * s}
    _L0_ffn_in = _L0_ffn_setup()

    def _L1_attn_setup():
        import jax, jax.numpy as jnp
        import numpy as np
        D_MODEL = 256
        N_Q_HEADS = 32
        N_KV_HEADS = 8
        D_HEAD = D_MODEL // N_Q_HEADS
        N_GROUPS = N_Q_HEADS // N_KV_HEADS
        B, N = (2, 256)
        key = jax.random.key(seed)
        ks = jax.random.split(key, 9)
        d_kv = N_KV_HEADS * D_HEAD
        s = 0.02
        return {'x': jax.random.normal(ks[0], (B, N, D_MODEL), dtype=jnp.float32), 'Wq': jax.random.normal(ks[1], (D_MODEL, D_MODEL), dtype=jnp.float32) * s, 'bq': jnp.zeros((D_MODEL,), dtype=jnp.float32), 'Wk': jax.random.normal(ks[2], (d_kv, D_MODEL), dtype=jnp.float32) * s, 'bk': jnp.zeros((d_kv,), dtype=jnp.float32), 'Wv': jax.random.normal(ks[3], (d_kv, D_MODEL), dtype=jnp.float32) * s, 'bv': jnp.zeros((d_kv,), dtype=jnp.float32), 'Wo': jax.random.normal(ks[4], (D_MODEL, D_MODEL), dtype=jnp.float32) * s, 'bo': jnp.zeros((D_MODEL,), dtype=jnp.float32)}
    _L1_attn_in = _L1_attn_setup()

    def _L1_ffn_setup():
        import jax, jax.numpy as jnp
        import numpy as np
        E, K, H, F = (64, 6, 256, 96)
        G, KG = (8, 4)
        SHARED_F = 96
        SCALE = 2.5
        T = 2 * 128
        CAP = 2 * (T * K // E)

        def _grouped_topk(logits, bias):
            scores = jax.nn.sigmoid(logits.astype(jnp.float32))
            scores_b = scores + bias[None, :]
            gs = scores_b.reshape(-1, G, E // G)
            group_scores = jnp.sum(jax.lax.top_k(gs, 2)[0], axis=-1)
            gidx = jax.lax.top_k(group_scores, KG)[1]
            rows = jnp.arange(group_scores.shape[0])[:, None]
            group_mask = jnp.zeros_like(group_scores).at[rows, gidx].set(1.0)
            score_mask = jnp.repeat(group_mask, E // G, axis=-1) > 0
            tmp = jnp.where(score_mask, scores_b, -jnp.inf)
            topk_ids = jax.lax.top_k(tmp, K)[1]
            topk_w = jnp.take_along_axis(scores, topk_ids, axis=-1)
            topk_w = topk_w / jnp.sum(topk_w, axis=-1, keepdims=True)
            return (topk_w * SCALE, topk_ids)

        def _routed_moe(x, topk_w, topk_ids, w_gate, w_up, w_down):
            Tn = x.shape[0]
            flat_e = topk_ids.reshape(-1)
            order = jnp.argsort(flat_e)
            se = flat_e[order]
            pos = jnp.arange(Tn * K) - jnp.searchsorted(se, se, side='left')
            tok = order // K
            valid = pos < CAP
            slot = jnp.where(valid, pos, CAP)
            buf = jnp.zeros((E, CAP + 1, H), x.dtype).at[se, slot].set(x[tok])[:, :CAP]
            h = jax.nn.silu(jnp.einsum('ech,ehf->ecf', buf, w_gate)) * jnp.einsum('ech,ehf->ecf', buf, w_up)
            out = jnp.einsum('ecf,efh->ech', h, w_down)
            gathered = out[se, jnp.minimum(pos, CAP - 1)] * valid.astype(x.dtype)[:, None]
            w = topk_w.reshape(-1)[order].astype(x.dtype)[:, None]
            return jax.ops.segment_sum(gathered * w, tok, num_segments=Tn)
        key = jax.random.key(seed)
        ks = jax.random.split(key, 9)
        s = 0.02
        return dict(hidden_states=jax.random.normal(ks[0], (2, 128, H), jnp.float32), gate_w=jax.random.normal(ks[1], (H, E), jnp.float32) * s, bias=jax.random.normal(ks[2], (E,), jnp.float32) * s, w_gate=jax.random.normal(ks[3], (E, H, F), jnp.float32) * s, w_up=jax.random.normal(ks[4], (E, H, F), jnp.float32) * s, w_down=jax.random.normal(ks[5], (E, F, H), jnp.float32) * s, ws_gate=jax.random.normal(ks[6], (H, SHARED_F), jnp.float32) * s, ws_up=jax.random.normal(ks[7], (H, SHARED_F), jnp.float32) * s, ws_down=jax.random.normal(ks[8], (SHARED_F, H), jnp.float32) * s)
    _L1_ffn_in = _L1_ffn_setup()
    _d = {'L0_attn_x': _L0_attn_in['x'], 'L0_attn_Wq': _L0_attn_in['Wq'], 'L0_attn_bq': _L0_attn_in['bq'], 'L0_attn_Wk': _L0_attn_in['Wk'], 'L0_attn_bk': _L0_attn_in['bk'], 'L0_attn_Wv': _L0_attn_in['Wv'], 'L0_attn_bv': _L0_attn_in['bv'], 'L0_attn_Wo': _L0_attn_in['Wo'], 'L0_attn_bo': _L0_attn_in['bo'], 'L0_ffn_gate_w': _L0_ffn_in['gate_w'], 'L0_ffn_W1': _L0_ffn_in['W1'], 'L0_ffn_W2': _L0_ffn_in['W2'], 'L0_ffn_W3': _L0_ffn_in['W3'], 'L0_ffn_Ws1': _L0_ffn_in['Ws1'], 'L0_ffn_Ws2': _L0_ffn_in['Ws2'], 'L0_ffn_Ws3': _L0_ffn_in['Ws3'], 'L1_attn_Wq': _L1_attn_in['Wq'], 'L1_attn_bq': _L1_attn_in['bq'], 'L1_attn_Wk': _L1_attn_in['Wk'], 'L1_attn_bk': _L1_attn_in['bk'], 'L1_attn_Wv': _L1_attn_in['Wv'], 'L1_attn_bv': _L1_attn_in['bv'], 'L1_attn_Wo': _L1_attn_in['Wo'], 'L1_attn_bo': _L1_attn_in['bo'], 'L1_ffn_gate_w': _L1_ffn_in['gate_w'], 'L1_ffn_bias': _L1_ffn_in['bias'], 'L1_ffn_w_gate': _L1_ffn_in['w_gate'], 'L1_ffn_w_up': _L1_ffn_in['w_up'], 'L1_ffn_w_down': _L1_ffn_in['w_down'], 'L1_ffn_ws_gate': _L1_ffn_in['ws_gate'], 'L1_ffn_ws_up': _L1_ffn_in['ws_up'], 'L1_ffn_ws_down': _L1_ffn_in['ws_down']}
    _x0 = _d['L0_attn_x']
    _d['L0_attn_x'] = jax.random.normal(jax.random.fold_in(jax.random.key(seed), 1), (4, 512, 256), dtype=_x0.dtype)
    del _x0
    return _d

def reference(L0_attn_x, L0_attn_Wq, L0_attn_bq, L0_attn_Wk, L0_attn_bk, L0_attn_Wv, L0_attn_bv, L0_attn_Wo, L0_attn_bo, L0_ffn_gate_w, L0_ffn_W1, L0_ffn_W2, L0_ffn_W3, L0_ffn_Ws1, L0_ffn_Ws2, L0_ffn_Ws3, L1_attn_Wq, L1_attn_bq, L1_attn_Wk, L1_attn_bk, L1_attn_Wv, L1_attn_bv, L1_attn_Wo, L1_attn_bo, L1_ffn_gate_w, L1_ffn_bias, L1_ffn_w_gate, L1_ffn_w_up, L1_ffn_w_down, L1_ffn_ws_gate, L1_ffn_ws_up, L1_ffn_ws_down):

    def _L0_attn_ref(x, Wq, bq, Wk, bk, Wv, bv, Wo, bo):
        import jax, jax.numpy as jnp
        import numpy as np
        HEAD_NUM = 16
        ROPE_BASE = 10000.0

        def _rotate_half(x):
            x_even = x[..., ::2]
            x_odd = x[..., 1::2]
            return jnp.stack((-x_odd, x_even), axis=-1).reshape(x.shape)

        def _rope_cos_sin(seq_len, head_dim):
            half = head_dim // 2
            inv_freq = 1.0 / ROPE_BASE ** (jnp.arange(half, dtype=jnp.float32) / half)
            t = jnp.arange(seq_len, dtype=jnp.float32)
            freqs = t[:, None] * inv_freq[None, :]
            cos = jnp.repeat(jnp.cos(freqs), 2, axis=-1)
            sin = jnp.repeat(jnp.sin(freqs), 2, axis=-1)
            return (cos, sin)
        B, S, H = x.shape
        nh = HEAD_NUM
        d = H // nh
        scale = jnp.float32(np.sqrt(d))

        def proj(W, b):
            y = x @ W.T + b
            return y.reshape(B, S, nh, d).transpose(0, 2, 1, 3)
        Q = proj(Wq, bq)
        K = proj(Wk, bk)
        V = proj(Wv, bv)
        cos, sin = _rope_cos_sin(S, d)
        Q = Q * cos + _rotate_half(Q) * sin
        K = K * cos + _rotate_half(K) * sin
        scores = jnp.einsum('bhqd,bhkd->bhqk', Q, K) / scale
        causal = jnp.tril(jnp.ones((S, S), dtype=bool))
        scores = jnp.where(causal, scores, jnp.float32(-jnp.inf))
        attn = jax.nn.softmax(scores, axis=-1)
        out = jnp.einsum('bhqk,bhkd->bhqd', attn, V)
        out = out.transpose(0, 2, 1, 3).reshape(B, S, H)
        return out @ Wo.T + bo

    def _L0_ffn_ref(x, gate_w, W1, W2, W3, Ws1, Ws2, Ws3):
        import jax, jax.numpy as jnp
        import numpy as np
        N_GROUPS = 4
        TOPK_GROUPS = 2
        TOPK = 4
        ROUTE_SCALE = 1.0

        def _gate(xt, gate_w):
            T = xt.shape[0]
            E = gate_w.shape[0]
            scores = jax.nn.sigmoid(xt @ gate_w.T)
            original_scores = scores
            sg = scores.reshape(T, N_GROUPS, E // N_GROUPS)
            group_scores = sg.max(axis=-1)
            _, gidx = jax.lax.top_k(group_scores, TOPK_GROUPS)
            gmask = jax.nn.one_hot(gidx, N_GROUPS, dtype=scores.dtype).sum(axis=1)
            masked = (sg * gmask[:, :, None]).reshape(T, E)
            _, idx = jax.lax.top_k(masked, TOPK)
            w = jnp.take_along_axis(original_scores, idx, axis=-1)
            w = w / w.sum(axis=-1, keepdims=True) * ROUTE_SCALE
            return (w, idx)
        shape = x.shape
        D = shape[-1]
        xt = x.reshape(-1, D)
        E = W1.shape[0]
        weights, indices = _gate(xt, gate_w)
        combine = jnp.einsum('tk,tke->te', weights, jax.nn.one_hot(indices, E, dtype=weights.dtype))
        h1 = jnp.einsum('td,eid->tei', xt, W1)
        h3 = jnp.einsum('td,eid->tei', xt, W3)
        g = jax.nn.silu(h1) * h3 * combine[:, :, None]
        y = jnp.einsum('tei,edi->td', g, W2)
        z = jax.nn.silu(xt @ Ws1.T) * (xt @ Ws3.T) @ Ws2.T
        return (y + z).reshape(shape)

    def _L1_attn_ref(x, Wq, bq, Wk, bk, Wv, bv, Wo, bo):
        import jax, jax.numpy as jnp
        import numpy as np
        D_MODEL = 256
        N_Q_HEADS = 32
        N_KV_HEADS = 8
        D_HEAD = D_MODEL // N_Q_HEADS
        N_GROUPS = N_Q_HEADS // N_KV_HEADS
        B, N = (2, 256)
        b, n, _ = x.shape
        scale = D_HEAD ** (-0.5)
        q = x @ Wq.T + bq
        k = x @ Wk.T + bk
        v = x @ Wv.T + bv
        q = q.reshape(b, n, N_Q_HEADS, D_HEAD).transpose(0, 2, 1, 3)
        k = k.reshape(b, n, N_KV_HEADS, D_HEAD).transpose(0, 2, 1, 3)
        v = v.reshape(b, n, N_KV_HEADS, D_HEAD).transpose(0, 2, 1, 3)
        k = jnp.repeat(k, N_GROUPS, axis=1)
        v = jnp.repeat(v, N_GROUPS, axis=1)
        scores = jnp.einsum('bhqd,bhkd->bhqk', q, k) * scale
        attn = jax.nn.softmax(scores, axis=-1)
        out = jnp.einsum('bhqk,bhkd->bhqd', attn, v)
        out = out.transpose(0, 2, 1, 3).reshape(b, n, D_MODEL)
        return out @ Wo.T + bo

    def _L1_ffn_ref(hidden_states, gate_w, bias, w_gate, w_up, w_down, ws_gate, ws_up, ws_down):
        import jax, jax.numpy as jnp
        import numpy as np
        E, K, H, F = (64, 6, 256, 96)
        G, KG = (8, 4)
        SHARED_F = 96
        SCALE = 2.5
        T = 2 * 128
        CAP = 2 * (T * K // E)

        def _grouped_topk(logits, bias):
            scores = jax.nn.sigmoid(logits.astype(jnp.float32))
            scores_b = scores + bias[None, :]
            gs = scores_b.reshape(-1, G, E // G)
            group_scores = jnp.sum(jax.lax.top_k(gs, 2)[0], axis=-1)
            gidx = jax.lax.top_k(group_scores, KG)[1]
            rows = jnp.arange(group_scores.shape[0])[:, None]
            group_mask = jnp.zeros_like(group_scores).at[rows, gidx].set(1.0)
            score_mask = jnp.repeat(group_mask, E // G, axis=-1) > 0
            tmp = jnp.where(score_mask, scores_b, -jnp.inf)
            topk_ids = jax.lax.top_k(tmp, K)[1]
            topk_w = jnp.take_along_axis(scores, topk_ids, axis=-1)
            topk_w = topk_w / jnp.sum(topk_w, axis=-1, keepdims=True)
            return (topk_w * SCALE, topk_ids)

        def _routed_moe(x, topk_w, topk_ids, w_gate, w_up, w_down):
            Tn = x.shape[0]
            flat_e = topk_ids.reshape(-1)
            order = jnp.argsort(flat_e)
            se = flat_e[order]
            pos = jnp.arange(Tn * K) - jnp.searchsorted(se, se, side='left')
            tok = order // K
            valid = pos < CAP
            slot = jnp.where(valid, pos, CAP)
            buf = jnp.zeros((E, CAP + 1, H), x.dtype).at[se, slot].set(x[tok])[:, :CAP]
            h = jax.nn.silu(jnp.einsum('ech,ehf->ecf', buf, w_gate)) * jnp.einsum('ech,ehf->ecf', buf, w_up)
            out = jnp.einsum('ecf,efh->ech', h, w_down)
            gathered = out[se, jnp.minimum(pos, CAP - 1)] * valid.astype(x.dtype)[:, None]
            w = topk_w.reshape(-1)[order].astype(x.dtype)[:, None]
            return jax.ops.segment_sum(gathered * w, tok, num_segments=Tn)
        orig_shape = hidden_states.shape
        x = hidden_states.reshape(-1, H)
        router_logits = x @ gate_w
        topk_w, topk_ids = _grouped_topk(router_logits, bias)
        y = _routed_moe(x, topk_w, topk_ids, w_gate, w_up, w_down)
        shared = jax.nn.silu(x @ ws_gate) * (x @ ws_up) @ ws_down
        return (y + shared).reshape(orig_shape)
    x = L0_attn_x
    x = x + _L0_attn_ref(_layernorm(x, axis=-1), L0_attn_Wq, L0_attn_bq, L0_attn_Wk, L0_attn_bk, L0_attn_Wv, L0_attn_bv, L0_attn_Wo, L0_attn_bo)
    x = x + _L0_ffn_ref(_layernorm(x, axis=-1), L0_ffn_gate_w, L0_ffn_W1, L0_ffn_W2, L0_ffn_W3, L0_ffn_Ws1, L0_ffn_Ws2, L0_ffn_Ws3)
    x = x + _L1_attn_ref(_layernorm(x, axis=-1), L1_attn_Wq, L1_attn_bq, L1_attn_Wk, L1_attn_bk, L1_attn_Wv, L1_attn_bv, L1_attn_Wo, L1_attn_bo)
    x = x + _L1_ffn_ref(_layernorm(x, axis=-1), L1_ffn_gate_w, L1_ffn_bias, L1_ffn_w_gate, L1_ffn_w_up, L1_ffn_w_down, L1_ffn_ws_gate, L1_ffn_ws_up, L1_ffn_ws_down)
    return x

_drawn_inputs = setup_inputs


def setup_inputs(seed=0):
    import zlib

    import numpy as np

    out = dict(_drawn_inputs(seed))
    spreads = {'L1_attn_bq': (0.0, 0.8),
     'L1_attn_bk': (0.0, 0.8),
     'L1_attn_bv': (0.0, 0.1),
     'L1_attn_bo': (0.0, 0.1)}
    factors = {'L0_attn_bq': 6.157,
     'L0_attn_bk': 7.734,
     'L0_ffn_gate_w': 8.0,
     'L0_ffn_W1': 8.0,
     'L0_ffn_W2': 8.0,
     'L0_ffn_W3': 8.0,
     'L0_ffn_Ws1': 2.951,
     'L0_ffn_Ws2': 2.939,
     'L0_ffn_Ws3': 2.934,
     'L1_attn_Wq': 8.0,
     'L1_attn_Wk': 8.0,
     'L1_attn_Wv': 4.129,
     'L1_ffn_gate_w': 8.0,
     'L1_ffn_bias': 8.0,
     'L1_ffn_w_gate': 8.0,
     'L1_ffn_w_up': 8.0,
     'L1_ffn_w_down': 8.0,
     'L1_ffn_ws_gate': 5.704,
     'L1_ffn_ws_up': 5.615,
     'L1_ffn_ws_down': 5.627}
    for name, (base, spread) in spreads.items():
        noise = np.random.default_rng([zlib.crc32(name.encode()), seed]).standard_normal(out[name].shape)
        drawn = base * np.exp(spread * noise) if base else spread * noise
        out[name] = jnp.asarray(drawn.astype(out[name].dtype))
    for name, factor in factors.items():
        out[name] = (out[name] * factor).astype(out[name].dtype)
    return out
```

```python
from contextlib import ExitStack

import concourse.bass as bass
import numpy as np
from concourse import mybir

ALU = mybir.AluOpType
ACT = mybir.ActivationFunctionType
AX = mybir.AxisListType
F32 = mybir.dt.float32
BF16 = mybir.dt.bfloat16
I32 = mybir.dt.int32
U32 = mybir.dt.uint32
ds = bass.ds

P = 128
B, S, H = 4, 512, 256
T = B * S
NT = T // P
TB = S // P
KH = H // P
HQ = 4
HB = 16
QUAD = 32
M_ROW = 96
NEG = -1.0e30

PAIRS_L0 = [(0, 0), (0, 1), (0, 2), (1, 0), (1, 1), (2, 0)]
PAIRS_L1 = [(i, j) for i in range(3) for j in range(3)]


class Layer:

    def __init__(self, name, d, nq, nkv, causal, scale, pairs):
        self.name, self.d, self.nq, self.nkv, self.causal, self.scale, self.pairs = (
            name, d, nq, nkv, causal, scale, pairs)
        self.rows = len(pairs) * d
        self.blocks = B * nq // HB
        self.groups = self.blocks * HB // HQ
        self.kv_of_block = HB * nkv // nq
        self.kv_of_group = HQ * nkv // nq
        self.vw = self.kv_of_group * QUAD


L0 = Layer("l0", 16, 16, 16, True, 0.25, PAIRS_L0)
L1 = Layer("l1", 8, 32, 8, False, 8 ** -0.5, PAIRS_L1)


def runs(parts):
    out = []
    for n, p in enumerate(parts):
        if out and out[-1][0] == p:
            out[-1][2] += 1
        else:
            out.append([p, n, 1])
    return out


def climbs(parts):
    out = []
    for n, p in enumerate(parts):
        if p == 0:
            out.append([n, 0])
        out[-1][1] += 1
    return out


def semaphore(nc, c, name):
    s = nc.alloc_semaphore(name=name)
    c["semaphores"].append(s)
    return s


def retire_semaphores(nc, c):
    nc.all_engine_barrier()
    nc.clear_and_free_semaphores(c["semaphores"])
    nc.all_engine_barrier()
    c["semaphores"] = []


def layernorm_statistics(nc, c, tag):
    with ExitStack() as ctx:
        stats = ctx.enter_context(nc.sbuf_tensor(f"stats_{tag}", [P, NT * 6], F32))
        var = ctx.enter_context(nc.sbuf_tensor(f"var_{tag}", [P, NT], F32))
        root = ctx.enter_context(nc.sbuf_tensor(f"root_{tag}", [P, NT], F32))
        work = ctx.enter_context(nc.sbuf_tensor(f"work_{tag}", [P, NT], F32))
        stats_done, mean_done, var_done, root_done, step_done = (
            semaphore(nc, c, f"{n}_{tag}")
            for n in ("stats_done", "mean_done", "var_done", "root_done", "step_done"))
        block = ctx.enter_context(nc.Block())
        mean_var = c["mean_var"][:, :].rearrange("p (t s) -> p t s", s=2)

        @block.vector
        def _(dve):
            with dve.Fori(0, NT) as t:
                nc.vector.bn_stats(stats[:, ds(t * 6, 6)], c["resid"][:, ds(t * H, H)]).then_inc(stats_done, 1)
            dve.wait_ge(stats_done, NT)
            for t in range(NT):
                nc.vector.bn_aggr(c["mean_var"][:, t * 2:t * 2 + 2], stats[:, t * 6:t * 6 + 6]).then_inc(mean_done, 1)
            dve.wait_ge(mean_done, NT)
            nc.vector.tensor_scalar(var[:, :], mean_var[:, :, 1], 1e-5, None, ALU.add).then_inc(var_done, 1)
            dve.wait_ge(root_done, 1)
            nc.vector.reciprocal(c["rstd"][:, :], root[:, :]).then_inc(step_done, 1)
            dve.wait_ge(step_done, 1)
            nc.vector.tensor_tensor(work[:, :], c["rstd"][:, :], c["rstd"][:, :], ALU.mult).then_inc(step_done, 1)
            dve.wait_ge(step_done, 2)
            nc.vector.tensor_tensor(work[:, :], work[:, :], var[:, :], ALU.mult).then_inc(step_done, 1)
            dve.wait_ge(step_done, 3)
            nc.vector.tensor_scalar(work[:, :], work[:, :], -0.5, 1.5, ALU.mult, ALU.add).then_inc(step_done, 1)
            dve.wait_ge(step_done, 4)
            nc.vector.tensor_tensor(c["rstd"][:, :], c["rstd"][:, :], work[:, :], ALU.mult).then_inc(step_done, 1)

        @block.scalar
        def _(act):
            act.wait_ge(var_done, 1)
            nc.scalar.activation(root[:, :], var[:, :], ACT.Sqrt).then_inc(root_done, 1)


def load_constants(nc, c, d):
    with ExitStack() as ctx:
        masks = ctx.enter_context(nc.sbuf_tensor("masks_f32", [P, 5, P], F32))
        loaded = semaphore(nc, c, "constants_loaded")
        block = ctx.enter_context(nc.Block())

        @block.sync
        def _(sp):
            for tt in range(B):
                sp.dma_start(c["resid"][:, tt * TB * H:(tt + 1) * TB * H].rearrange("p (t f) -> p t f", f=H),
                             d["x"][tt * S:(tt + 1) * S, :].rearrange("(t p) f -> p t f", p=P)).then_inc(loaded, 16)
            sp.dma_start(masks[:, :, :], d["masks"]).then_inc(loaded, 16)
            sp.dma_start(c["ident"][:, :], d["ident"]).then_inc(loaded, 16)
            sp.wait_ge(loaded, 16 * (B + 2))

        @block.vector
        def _(dve):
            dve.wait_ge(loaded, 16 * (B + 2))
            nc.vector.tensor_copy(c["masks"][:, :, :], masks[:, :, :])


def project(nc, c, d, L):
    rope = L.causal
    n = L.name
    kf = L.nkv * L.d
    KT = -(-kf // P)
    kp = min(kf, P)
    NF = KH + KT
    with ExitStack() as ctx:
        def sb(name, shape, dt=F32):
            return ctx.enter_context(nc.sbuf_tensor(f"{name}_{n}", shape, dt))

        def sem(name):
            return semaphore(nc, c, f"{name}_{n}")

        wq, wk, wv = sb("wq_sb", [P, KH, H]), sb("wk_sb", [P, KH, kf]), sb("wv_sb", [P, KH, kf])
        bqk, bv = sb("bqk_sb", [P, NF]), sb("bv_sb", [P, kf])
        if rope:
            cos, sin = sb("cos_sb", [P, S]), sb("sin_sb", [P, S])
            swapped = sb("swapped", [P, NF, S])
        xn = sb("xn", [P, 2, TB, H])
        xnt = sb("xnt", [P, KH, S])
        qk = sb("qk", [P, NF, S])
        rest = sb("rest", [P, NF, S])
        parts = sb("parts", [P, 3, NF, S], BF16)
        vaug = sb("vaug", [P, TB, L.nkv, QUAD])
        ps_t = ctx.enter_context(nc.psum_tensor(f"ps_t_{n}", [P, KH, S], F32))
        ps_qk = ctx.enter_context(nc.psum_tensor(f"ps_qk_{n}", [P, NF, S], F32))
        ps_v = ctx.enter_context(nc.psum_tensor(f"ps_v_{n}", [P, TB, 256], F32))

        weights_in, xn_ready, t_ready, xnt_ready, qk_ready, v_ready = (
            sem(x) for x in ("weights_in", "xn_ready", "t_ready", "xnt_ready", "qk_ready", "v_ready"))
        qk_biased, rope_swapped, rope_cos, rope_sin, roped = (
            sem(x) for x in ("qk_biased", "rope_swapped", "rope_cos", "rope_sin", "roped"))
        part0, rest1, part1, part2, v_out, parts_stored, v_stored, ones_set = (
            sem(x) for x in ("part0", "rest1", "part1", "part2", "v_out", "parts_stored", "v_stored", "ones_set"))
        dve_passed = sem("dve_passed")
        n_weights = 7 + 2 * rope
        q_stores = KH
        k_stores = KT if rope else 2
        n_parts = 3 * (q_stores + k_stores)
        hg = L.nkv // L.kv_of_group
        block = ctx.enter_context(nc.Block())

        @block.sync
        def _(sp):
            for dst, src in [(wq, "wq"), (wk, "wk"), (wv, "wv")]:
                sp.dma_start(dst[:, :, :], d[f"{n}_{src}"]).then_inc(weights_in, 16)
            sp.dma_start(bqk[:, 0:KH], d[f"{n}_bq"]).then_inc(weights_in, 16)
            sp.dma_start(bqk[0:kp, KH:NF], d[f"{n}_bk"]).then_inc(weights_in, 16)
            sp.dma_start(bv[:, :], d[f"{n}_bv"].rearrange("(a n) -> a n", a=1).to_broadcast([P, kf])).then_inc(
                weights_in, 16)
            sp.dma_start(c["bo"][:, :], d[f"{n}_bo"].rearrange("(a n) -> a n", a=1).to_broadcast([P, H])).then_inc(
                weights_in, 16)
            if rope:
                sp.dma_start(cos[:, :], d["cos"]).then_inc(weights_in, 16)
                sp.dma_start(sin[:, :], d["sin"]).then_inc(weights_in, 16)
            with sp.Fori(0, B) as b:
                sp.wait_ge(v_out, b + 1)
                for g in range(hg):
                    w = L.kv_of_group
                    sp.dma_start(d[f"{n}_vd"][ds(b * hg + g, 1)].rearrange("o (t p) w -> p (o t) w", p=P),
                                 vaug[:, :, g * w:(g + 1) * w, :].rearrange("p t h w -> p t (h w)")).then_inc(
                        v_stored, 16)
                for part, ready in ((0, part0), (1, part1), (2, part2)):
                    sp.wait_ge(ready, b + 1)
                    qd, kd = d[f"{n}_qd"], d[f"{n}_kd"]
                    for m in range(KH):
                        h8 = P // L.d
                        blk = b if rope else b * 2 + m
                        dst = qd[part, ds(blk, 1), :, (m * h8 if rope else 0):(m + 1) * h8 if rope else HB, :]
                        sp.dma_start(dst.rearrange("o e h t -> (o h) e t"), parts[:, part, m, :]).then_inc(
                            parts_stored, 16)
                    for m in range(k_stores):
                        if rope:
                            dst, src = kd[part, ds(b, 1), :, m * 8:(m + 1) * 8, :], parts[:, part, KH + m, :]
                        else:
                            dst, src = kd[part, ds(b * 2 + m, 1)], parts[m * 32:(m + 1) * 32, part, KH, :]
                        sp.dma_start(dst.rearrange("o e h t -> (o h) e t"), src).then_inc(parts_stored, 16)
            sp.wait_ge(parts_stored, 16 * n_parts * B)
            sp.wait_ge(v_stored, 16 * hg * B)

        def normalise(dve, b, slot):
            for t in range(TB):
                at = b * TB + t
                op = nc.vector.tensor_scalar(
                    xn[:, slot, t, :], c["resid"][:, ds(at * H, H)], c["mean_var"][:, ds(at * 2, 1)],
                    c["rstd"][:, ds(at, 1)], ALU.subtract, ALU.mult)
            op.then_inc(xn_ready, 1)

        @block.tensor
        def _(pe):
            pe.wait_ge(weights_in, 16 * n_weights)
            with pe.Fori(0, B // 2) as b2:
                for half in range(2):
                    b = b2 * 2 + half
                    pe.wait_ge(xn_ready, b + 1)
                    pe.wait_ge(xnt_ready, b)
                    for k in range(KH):
                        for t in range(TB):
                            op = nc.tensor.transpose(ps_t[:, k, t * P:(t + 1) * P],
                                                     xn[:, half, t, k * P:(k + 1) * P], c["ident"][:, :])
                    op.then_inc(t_ready, 1)
                    pe.wait_ge(xnt_ready, b + 1)
                    pe.wait_ge(qk_biased, b)
                    for m in range(NF):
                        w, lo, width = (wq, m * P, P) if m < KH else (wk, (m - KH) * P, kp)
                        for k in range(KH):
                            op = nc.tensor.matmul(ps_qk[0:width, m, :], w[:, k, lo:lo + width], xnt[:, k, :],
                                                  start=k == 0, stop=k == KH - 1)
                    op.then_inc(qk_ready, 1)
                    pe.wait_ge(v_out, b)
                    for t in range(TB):
                        for k in range(KH):
                            op = nc.tensor.matmul(ps_v[:, t, 0:kf], xnt[:, k, t * P:(t + 1) * P], wv[:, k, :],
                                                  start=k == 0, stop=k == KH - 1)
                    op.then_inc(v_ready, 1)

        @block.scalar
        def _(act):
            act.wait_ge(weights_in, 16 * n_weights)
            with act.Fori(0, B) as b:
                act.wait_ge(t_ready, b + 1)
                act.wait_ge(v_ready, b)
                nc.scalar.copy(xnt[:, :, :], ps_t[:, :, :]).then_inc(xnt_ready, 1)
                act.wait_ge(qk_ready, b + 1)
                act.wait_ge(part2, b)
                for m in range(NF):
                    w = P if m < KH else kp
                    op = nc.scalar.activation(qk[0:w, m, :], ps_qk[0:w, m, :], ACT.Identity,
                                              bias=bqk[0:w, m:m + 1])
                op.then_inc(qk_biased, 1)
                if rope:
                    act.wait_ge(roped, b + 1)
                else:
                    act.wait_ge(qk_biased, b + 1)
                act.wait_ge(parts_stored, 16 * n_parts * b)
                nc.scalar.copy(parts[:, 0, 0:KH, :], qk[:, 0:KH, :])
                nc.scalar.copy(parts[0:kp, 0, KH:NF, :], qk[0:kp, KH:NF, :]).then_inc(part0, 1)
                act.wait_ge(rest1, b + 1)
                nc.scalar.copy(parts[:, 1, 0:KH, :], rest[:, 0:KH, :])
                nc.scalar.copy(parts[0:kp, 1, KH:NF, :], rest[0:kp, KH:NF, :]).then_inc(part1, 1)

        if rope:
            @block.gpsimd
            def _(pool):
                pool.wait_ge(weights_in, 16 * n_weights)
                with pool.Fori(0, B) as b:
                    pool.wait_ge(qk_biased, b + 1)
                    pool.wait_ge(part1, b)
                    pool.wait_ge(part2, b)
                    nc.gpsimd.tensor_tensor(rest[:, :, :], qk[:, :, :],
                                            cos[:, :].unsqueeze(1).to_broadcast([P, NF, S]), ALU.mult).then_inc(
                        rope_cos, 1)

        @block.vector
        def _(dve):
            dve.wait_ge(weights_in, 16 * n_weights)
            nc.vector.memset(vaug[:, :, :, :], 1.0).then_inc(ones_set, 1)
            dve.wait_ge(ones_set, 1)
            with dve.Fori(0, B // 2) as b2:
                dve.wait_ge(t_ready, b2 * 2)
                for half in range(2):
                    normalise(dve, b2 * 2 + half, half)
                for half in range(2):
                    b = b2 * 2 + half
                    if rope:
                        dve.wait_ge(qk_biased, b + 1)
                        dve.sem_inc(dve_passed, 1)
                        nc.vector.stream_shuffle(swapped[:, :, :], qk[:, :, :],
                                                 [i ^ 1 for i in range(32)]).then_inc(rope_swapped, 1)
                        dve.wait_ge(rope_swapped, b + 1)
                        nc.vector.tensor_tensor(swapped[:, :, :], swapped[:, :, :],
                                                sin[:, :].unsqueeze(1).to_broadcast([P, NF, S]),
                                                ALU.mult).then_inc(rope_sin, 1)
                        dve.wait_ge(rope_sin, b + 1)
                        dve.wait_ge(rope_cos, b + 1)
                        nc.vector.tensor_tensor(qk[:, :, :], rest[:, :, :], swapped[:, :, :], ALU.add).then_inc(
                            roped, 1)
                    dve.wait_ge(v_ready, b + 1)
                    dve.wait_ge(v_stored, 16 * hg * b)
                    for t in range(TB):
                        op = nc.vector.tensor_tensor(
                            vaug[:, t, :, 0:L.d], ps_v[:, t, 0:kf].rearrange("p (h e) -> p h e", e=L.d),
                            bv[:, :].rearrange("p (h e) -> p h e", e=L.d), ALU.add)
                    op.then_inc(v_out, 1)
                    dve.wait_ge(part0, b + 1)
                    dve.wait_ge(parts_stored, 16 * n_parts * b)
                    nc.vector.tensor_tensor(rest[:, 0:KH, :], qk[:, 0:KH, :], parts[:, 0, 0:KH, :], ALU.subtract)
                    nc.vector.tensor_tensor(rest[0:kp, KH:NF, :], qk[0:kp, KH:NF, :], parts[0:kp, 0, KH:NF, :],
                                            ALU.subtract).then_inc(rest1, 1)
                    dve.wait_ge(part1, b + 1)
                    nc.vector.tensor_tensor(parts[:, 2, 0:KH, :], rest[:, 0:KH, :], parts[:, 1, 0:KH, :],
                                            ALU.subtract)
                    nc.vector.tensor_tensor(parts[0:kp, 2, KH:NF, :], rest[0:kp, KH:NF, :],
                                            parts[0:kp, 1, KH:NF, :], ALU.subtract).then_inc(part2, 1)


def attend(nc, c, d, L):
    n = L.name
    G, U = L.groups, 4
    R = L.rows
    KW = L.kv_of_group * S
    q_parts, k_parts = [q for q, _ in L.pairs], [k for _, k in L.pairs]
    q_runs, k_climbs = runs(q_parts), climbs(k_parts)
    n_loads = len(q_runs) + len(k_climbs) + 1
    with ExitStack() as ctx:
        def sb(name, shape, dt=F32):
            return ctx.enter_context(nc.sbuf_tensor(f"{name}_{n}", shape, dt))

        def sem(name):
            return semaphore(nc, c, f"{name}_{n}")

        q = [sb(f"q{u}", [P, HQ, S], BF16) for u in range(U)]
        k = [sb(f"k{u}", [P, KW], BF16) for u in range(U)]
        v = [sb(f"v{u}", [P, TB, L.vw]) for u in range(U)]
        probs = [sb(f"probs{t}", [P, HQ, S]) for t in range(TB)]
        row_max = sb("row_max", [P, 2, HQ * TB])
        neg_rest = sb("neg_rest", [P, 2, HQ * TB])
        neg_parts = sb("neg_parts", [P, 2, 3, HQ * TB], BF16)
        neg_rows = sb("neg_rows", [3 * HQ * TB, 2, P], BF16)
        mixed = sb("mixed", [P, 2, S])
        ps_max = ctx.enter_context(nc.psum_tensor(f"ps_max_{n}", [P, 2, S], F32))
        ps_s = ctx.enter_context(nc.psum_tensor(f"ps_s_{n}", [P, 2, 2, S], F32))
        ps_o = ctx.enter_context(nc.psum_tensor(f"ps_o_{n}", [P, S], F32))
        ps_m = ctx.enter_context(nc.psum_tensor(f"ps_m_{n}", [P, S], F32))

        loaded = [sem(f"loaded{u}") for u in range(U)]
        ones_set, pool_passed = sem("ones_set_k"), sem("pool_passed")
        max_scores, max_taken = sem("max_scores"), sem("max_taken")
        neg0, neg_r1, neg1, neg_split = sem("neg0"), sem("neg_r1"), sem("neg1"), sem("neg_split")
        neg_turned, neg_copied, neg_stored, neg_loaded = (
            sem("neg_turned"), sem("neg_copied"), sem("neg_stored"), sem("neg_loaded"))
        scores, exps, values_used, mixed_copied, mixed_stored = (
            sem("scores"), sem("exps"), sem("values_used"), sem("mixed_copied"), sem("mixed_stored"))
        block = ctx.enter_context(nc.Block())

        def body_of_groups(eng, one):
            for u in range(U):
                one(eng, 0, u, u)
            with eng.Fori(1, G // U - 1) as i:
                for u in range(U):
                    one(eng, i, u, 99)
            for u in range(U):
                one(eng, G // U - 1, u, G - U + u)

        @block.sync
        def _(sp):
            sp.wait_ge(ones_set, 3 * U)

            def load(i, u):
                for part, at, count in q_runs:
                    src = d[f"{n}_qd"][part, ds(i, 1), :, u * HQ:(u + 1) * HQ, :].rearrange(
                        "o e h t -> o e (h t)").to_broadcast([count, L.d, HQ * S])
                    sp.dma_start(q[u][at * L.d:(at + count) * L.d, :, :].rearrange("p h t -> p (h t)"),
                                 src).then_inc(loaded[u], 16)
                w = L.kv_of_group
                for at, count in k_climbs:
                    src = d[f"{n}_kd"][0:count, ds(i, 1), :, u * w:(u + 1) * w, :].rearrange(
                        "c o e h t -> (o c) e (h t)")
                    sp.dma_start(k[u][at * L.d:(at + count) * L.d, :], src).then_inc(loaded[u], 16)
                sp.dma_start(v[u][:, :, :], d[f"{n}_vd"][ds(i * U + u, 1)].rearrange(
                    "o (t p) w -> p (o t) w", p=P)).then_inc(loaded[u], 16)

            for u in range(U):
                load(0, u)
            with sp.Fori(1, G // U) as i:
                for u in range(U):
                    sp.wait_ge(values_used, (i * U + u - 3) * TB)
                    load(i, u)

        @block.gpsimd
        def _(pool):
            for u in range(U):
                nc.gpsimd.memset(k[u][64:P, :], 0.0).then_inc(ones_set, 1)
                nc.gpsimd.memset(q[u][64:M_ROW, :, :], 0.0).then_inc(ones_set, 1)
            pool.wait_ge(ones_set, 2 * U)
            for u in range(U):
                nc.gpsimd.memset(k[u][M_ROW:M_ROW + 3, :], 1.0).then_inc(ones_set, 1)

            def step(pool, i, u, known):
                g = i * U + u
                pool.wait_ge(neg_copied, g + 1)
                pool.wait_ge(neg_loaded, g * 16)
                pool.sem_inc(pool_passed, 1)
                pool.dma_start(d["neg_d"][u], neg_rows[:, u % 2, :]).then_inc(neg_stored, 16)
                pool.wait_ge(neg_stored, (g + 1) * 16)
                pool.sem_inc(pool_passed, 1)
                pool.dma_start(q[u][M_ROW:M_ROW + 3, :, :],
                               d["neg_d"][u].rearrange("(c h) t -> c (h t)", c=3)).then_inc(neg_loaded, 16)
                if known > 1:
                    pool.wait_ge(mixed_copied, g - 1)
                    pool.wait_ge(mixed_stored, (g - 2) * 16)
                    pool.sem_inc(pool_passed, 1)
                    pool.dma_start(d[f"{n}_od"][ds((g - 2) * P, P), :], mixed[:, u % 2, :]).then_inc(mixed_stored, 16)

            body_of_groups(pool, step)
            for g in (G - 2, G - 1):
                pool.wait_ge(mixed_copied, g + 1)
                pool.wait_ge(mixed_stored, g * 16)
                pool.dma_start(d[f"{n}_od"][g * P:(g + 1) * P, :], mixed[:, g % 2, :]).then_inc(mixed_stored, 16)
            pool.wait_ge(mixed_stored, 16 * G)

        @block.vector
        def _(dve):
            def step(dve, i, u, known):
                g = i * U + u
                s = u % 2
                if known > 1:
                    dve.wait_ge(neg_turned, g - 1)
                for t in range(TB):
                    for h in range(HQ):
                        x = t * HQ + h
                        dve.wait_ge(max_scores, g * 16 + x + 1)
                        width = (t + 1) * P if L.causal else S
                        nc.vector.tensor_reduce(row_max[:, s, h * TB + t:h * TB + t + 1], ps_max[:, x % 2, 0:width],
                                                AX.X, ALU.max).then_inc(max_taken, 1)
                dve.wait_ge(max_taken, (g + 1) * 16)
                nc.vector.tensor_scalar(neg_parts[:, s, 0, :], row_max[:, s, :], -1.0, None, ALU.mult).then_inc(
                    neg0, 1)
                dve.wait_ge(neg0, g + 1)
                nc.vector.scalar_tensor_tensor(neg_rest[:, s, :], row_max[:, s, :], -1.0, neg_parts[:, s, 0, :],
                                               ALU.mult, ALU.subtract).then_inc(neg_r1, 1)
                dve.wait_ge(neg_r1, g + 1)
                nc.vector.tensor_copy(neg_parts[:, s, 1, :], neg_rest[:, s, :]).then_inc(neg1, 1)
                dve.wait_ge(neg1, g + 1)
                nc.vector.tensor_tensor(neg_parts[:, s, 2, :], neg_rest[:, s, :], neg_parts[:, s, 1, :],
                                        ALU.subtract).then_inc(neg_split, 1)

            body_of_groups(dve, step)

        @block.scalar
        def _(act):
            def copy_negated(g, s):
                act.wait_ge(neg_turned, g + 1)
                if not isinstance(g, int) or g > 1:
                    act.wait_ge(neg_stored, (g - 1) * 16)
                nc.scalar.copy(neg_rows[:, s, :], ps_m[0:3 * HQ * TB, 0:P]).then_inc(neg_copied, 1)

            def copy_mixed(g, s):
                act.wait_ge(values_used, (g + 1) * TB)
                if not isinstance(g, int) or g > 1:
                    act.wait_ge(mixed_stored, (g - 1) * 16)
                nc.scalar.copy(mixed[:, s, :], ps_o[:, :]).then_inc(mixed_copied, 1)

            def step(act, i, u, known):
                g = i * U + u
                for x in range(8):
                    kt, pair = x // 2, x % 2
                    lo = kt * P if L.causal else 0
                    act.wait_ge(scores, g * 8 + x + 1)
                    if known > 0 and pair == 0:
                        act.wait_ge(values_used, g * TB + kt - 3)
                    nc.scalar.activation(probs[kt][:, 2 * pair:2 * pair + 2, lo:S], ps_s[:, pair, :, lo:S], ACT.Exp,
                                         scale=L.scale).then_inc(exps, 1)
                    if x == 1 and known != G - 1:
                        copy_negated(g + 1, (u + 1) % 2)
                    if x == 2 and known > 0:
                        copy_mixed(g - 1, (u + 1) % 2)

            copy_negated(0, 0)
            body_of_groups(act, step)
            copy_mixed(G - 1, (G - 1) % 2)

        @block.tensor
        def _(pe):
            def top(g, u, x):
                t, h = x // HQ, x % HQ
                if not isinstance(g, int) or g * 16 + x >= 2:
                    pe.wait_ge(max_taken, g * 16 + x - 1)
                kc = h * S if L.kv_of_group > 1 else 0
                width = (t + 1) * P if L.causal else S
                op = nc.tensor.matmul(ps_max[:, x % 2, 0:width], q[u][0:R, h, t * P:(t + 1) * P],
                                      k[u][0:R, kc:kc + width], start=True, stop=not L.causal)
                if L.causal:
                    op = nc.tensor.matmul(ps_max[:, x % 2, t * P:width], c["masks"][:, 0, :], c["masks"][:, 1, :],
                                          start=False, stop=True)
                op.then_inc(max_scores, 1)

            def turn(g, u):
                pe.wait_ge(neg_split, g + 1)
                if not isinstance(g, int) or g > 0:
                    pe.wait_ge(neg_copied, g)
                nc.tensor.matmul(ps_m[0:3 * HQ * TB, 0:P],
                                 neg_parts[:, u % 2, :, :].rearrange("p c n -> p (c n)"),
                                 c["masks"][:, 0, :], start=True, stop=True).then_inc(neg_turned, 1)

            def weigh(g, u, kt):
                pe.wait_ge(exps, g * 8 + 2 * kt + 2)
                if kt == 0 and (not isinstance(g, int) or g > 0):
                    pe.wait_ge(mixed_copied, g)
                lo = kt * P if L.causal else 0
                for h in range(HQ):
                    vc = h * QUAD if L.kv_of_group > 1 else 0
                    op = nc.tensor.matmul(ps_o[h * QUAD:(h + 1) * QUAD, lo:S], v[u][:, kt, vc:vc + QUAD],
                                          probs[kt][:, h, lo:S], start=kt == 0, stop=kt == TB - 1)
                op.then_inc(values_used, 1)

            def step(pe, i, u, known):
                g = i * U + u
                ahead = known == 99 or known < G - 2
                for x in range(8):
                    kt, pair = x // 2, x % 2
                    lo = kt * P if L.causal else 0
                    if x == 0:
                        pe.wait_ge(neg_loaded, (g + 1) * 16)
                        if ahead:
                            pe.wait_ge(loaded[(u + 2) % U], (i + u // 2 + 1) * (16 * n_loads))
                    if ahead:
                        top(g + 2, (u + 2) % U, 2 * x)
                        top(g + 2, (u + 2) % U, 2 * x + 1)
                    if not isinstance(g, int) or g * 8 + x >= 2:
                        pe.wait_ge(exps, g * 8 + x - 1)
                    for h in (2 * pair, 2 * pair + 1):
                        kc = h * S if L.kv_of_group > 1 else 0
                        op = nc.tensor.matmul(ps_s[:, pair, h % 2, lo:S], k[u][0:M_ROW + 3, kc + kt * P:kc + (kt + 1) * P],
                                              q[u][0:M_ROW + 3, h, lo:S], start=True, stop=not L.causal)
                        if L.causal:
                            op = nc.tensor.matmul(ps_s[:, pair, h % 2, lo:lo + P], c["masks"][:, 0, :],
                                                  c["masks"][:, 2, :], start=False, stop=True)
                    op.then_inc(scores, 1)
                    if x == 1:
                        if known > 0:
                            weigh(g - 1, (u - 1) % U, TB - 1)
                        if known != G - 1:
                            turn(g + 1, (u + 1) % U)
                    if x in (3, 5, 7):
                        weigh(g, u, x // 2 - 1)

            pe.wait_ge(ones_set, 3 * U)
            pe.wait_ge(loaded[0], 16 * n_loads)
            for x in range(16):
                top(0, 0, x)
            pe.wait_ge(loaded[1], 16 * n_loads)
            for x in range(16):
                top(1, 1, x)
                if x == 3:
                    turn(0, 0)
            body_of_groups(pe, step)
            weigh(G - 1, U - 1, TB - 1)


def join(nc, c, d, L):
    n = L.name
    with ExitStack() as ctx:
        def sb(name, shape, dt=F32):
            return ctx.enter_context(nc.sbuf_tensor(f"{name}_{n}", shape, dt))

        def sem(name):
            return semaphore(nc, c, f"{name}_{n}")

        wo = sb("wo_sb", [P, KH, H])
        num = sb("num", [P, 2, KH, S])
        den = sb("den", [P, 2, KH, S])
        ps_y = ctx.enter_context(nc.psum_tensor(f"ps_y_{n}", [P, 2, TB, H], F32))
        wo_in, biased = sem("wo_in"), sem("biased")
        rows_in = [sem("rows_in0"), sem("rows_in1")]
        inverted, divided, projected, added = sem("inverted"), sem("divided"), sem("projected"), sem("added")
        heads = P // L.d
        block = ctx.enter_context(nc.Block())

        @block.sync
        def _(sp):
            sp.dma_start(wo[:, :, :], d[f"{n}_wo"]).then_inc(wo_in, 16)
            od = d[f"{n}_od"].rearrange("(h r) t -> h r t", r=QUAD)
            for b in range(B):
                if b >= 2:
                    sp.wait_ge(projected, b - 1)
                for m in range(KH):
                    h0 = (b * KH + m) * heads
                    sp.dma_start(num[:, b % 2, m, :], od[h0:h0 + heads, 0:L.d, :]).then_inc(rows_in[b % 2], 16)
                    sp.dma_start(den[:, b % 2, m, :], od[h0:h0 + heads, L.d:2 * L.d, :]).then_inc(rows_in[b % 2], 16)

        @block.gpsimd
        def _(pool):
            with pool.Fori(0, NT) as t:
                nc.gpsimd.tensor_tensor(c["resid"][:, ds(t * H, H)], c["resid"][:, ds(t * H, H)], c["bo"][:, :],
                                        ALU.add).then_inc(biased, 1)

        @block.vector
        def _(dve):
            dve.wait_ge(biased, NT)

            def add(b):
                dve.wait_ge(projected, b + 1)
                r = c["resid"][:, b * TB * H:(b + 1) * TB * H]
                nc.vector.tensor_tensor(r, r, ps_y[:, b % 2, :, :].rearrange("p t f -> p (t f)"),
                                        ALU.add).then_inc(added, 1)

            for b in range(B):
                dve.wait_ge(rows_in[b % 2], 16 * 2 * KH * (b // 2 + 1))
                nc.vector.reciprocal(den[:, b % 2, :, :], den[:, b % 2, :, :]).then_inc(inverted, 1)
                dve.wait_ge(inverted, b + 1)
                nc.vector.tensor_tensor(num[:, b % 2, :, :], num[:, b % 2, :, :], den[:, b % 2, :, :],
                                        ALU.mult).then_inc(divided, 1)
                if b:
                    add(b - 1)
            add(B - 1)

        @block.tensor
        def _(pe):
            pe.wait_ge(wo_in, 16)
            for b in range(B):
                pe.wait_ge(divided, b + 1)
                if b >= 2:
                    pe.wait_ge(added, b - 1)
                for t in range(TB):
                    for m in range(KH):
                        op = nc.tensor.matmul(ps_y[:, b % 2, t, :], num[:, b % 2, m, t * P:(t + 1) * P], wo[:, m, :],
                                              start=m == 0, stop=m == KH - 1)
                op.then_inc(projected, 1)


def normalised_rows(nc, c, d, n, experts):
    shared = n == "l1"
    F = 96
    with ExitStack() as ctx:
        def sb(name, shape, dt=F32):
            return ctx.enter_context(nc.sbuf_tensor(f"{name}_{n}f", shape, dt))

        def sem(name):
            return semaphore(nc, c, f"{name}_{n}f")

        wr = sb("wr", [P, KH, experts])
        xn = sb("xn", [P, 2, TB, H])
        xnt = sb("xnt", [P, KH, S])
        ps_t = ctx.enter_context(nc.psum_tensor(f"ps_t_{n}f", [P, KH, S], F32))
        ps_l = ctx.enter_context(nc.psum_tensor(f"ps_l_{n}f", [P, TB, experts], F32))
        weights_in, xn_ready, t_ready, xnt_ready, l_ready, l_out, rows_kept, rows_used = (
            sem(x) for x in ("weights_in", "xn_ready", "t_ready", "xnt_ready", "l_ready", "l_out", "rows_kept",
                             "rows_used"))
        if shared:
            wsg, wsu, wsd = sb("wsg", [P, KH, F]), sb("wsu", [P, KH, F]), sb("wsd", [F, H])
            gate, hidden = sb("gate", [F, S]), sb("hidden", [F, S])
            ps_g = ctx.enter_context(nc.psum_tensor("ps_g_sh", [P, 2, S], F32))
            ps_y = ctx.enter_context(nc.psum_tensor("ps_y_sh", [P, TB, H], F32))
            up_ready, gated, hidden_ready, y_ready, y_added = (
                sem(x) for x in ("up_ready", "gated", "hidden_ready", "y_ready", "y_added"))
        sp_passed = sem("sp_passed")
        n_weights = 1 + 3 * shared
        block = ctx.enter_context(nc.Block())

        @block.sync
        def _(sp):
            sp.dma_start(wr[:, :, :], d[f"{n}_router"]).then_inc(weights_in, 16)
            if shared:
                sp.dma_start(wsg[:, :, :], d["l1_wsg"]).then_inc(weights_in, 16)
                sp.dma_start(wsu[:, :, :], d["l1_wsu"]).then_inc(weights_in, 16)
                sp.dma_start(wsd[:, :], d["l1_wsd"]).then_inc(weights_in, 16)
                with sp.Fori(0, B // 2) as b2:
                    for half in range(2):
                        sp.wait_ge(xn_ready, b2 * 2 + half + 1)
                        sp.dma_start(d["xn_d"][ds((b2 * 2 + half) * S, S), :].rearrange("(t p) f -> p t f", p=P),
                                     xn[:, half, :, :]).then_inc(rows_kept, 16)
                        sp.wait_ge(rows_kept, (b2 * 2 + half + 1) * 16)
                        sp.sem_inc(sp_passed, 1)

        @block.tensor
        def _(pe):
            pe.wait_ge(weights_in, 16 * n_weights)
            with pe.Fori(0, B // 2) as b2:
                for half in range(2):
                    b = b2 * 2 + half
                    pe.wait_ge(xn_ready, b + 1)
                    pe.wait_ge(xnt_ready, b)
                    for k in range(KH):
                        for t in range(TB):
                            op = nc.tensor.transpose(ps_t[:, k, t * P:(t + 1) * P],
                                                     xn[:, half, t, k * P:(k + 1) * P], c["ident"][:, :])
                    op.then_inc(t_ready, 1)
                    pe.wait_ge(xnt_ready, b + 1)
                    if shared:
                        pe.wait_ge(hidden_ready, b)
                        for i, w in enumerate((wsg, wsu)):
                            for k in range(KH):
                                op = nc.tensor.matmul(ps_g[0:F, i, :], w[:, k, :], xnt[:, k, :],
                                                      start=k == 0, stop=k == KH - 1)
                        op.then_inc(up_ready, 1)
                    pe.wait_ge(l_out, b)
                    for t in range(TB):
                        for k in range(KH):
                            op = nc.tensor.matmul(ps_l[:, t, :], xnt[:, k, t * P:(t + 1) * P], wr[:, k, :],
                                                  start=k == 0, stop=k == KH - 1)
                    op.then_inc(l_ready, 1)
                    if shared:
                        pe.wait_ge(hidden_ready, b + 1)
                        pe.wait_ge(y_added, b)
                        for t in range(TB):
                            op = nc.tensor.matmul(ps_y[:, t, :], hidden[:, t * P:(t + 1) * P], wsd[:, :],
                                                  start=True, stop=True)
                        op.then_inc(y_ready, 1)

        @block.scalar
        def _(act):
            with act.Fori(0, B) as b:
                act.wait_ge(t_ready, b + 1)
                act.wait_ge(l_ready, b)
                act.wait_ge(rows_used, b)
                nc.scalar.copy(xnt[:, :, :], ps_t[:, :, :]).then_inc(xnt_ready, 1)
                if shared:
                    act.wait_ge(up_ready, b + 1)
                    act.wait_ge(hidden_ready, b)
                    nc.scalar.activation(gate[:, :], ps_g[0:F, 0, :], ACT.Silu).then_inc(gated, 1)
                act.wait_ge(l_ready, b + 1)
                nc.scalar.copy(c["logits"][:, ds(b * (TB * experts), TB * experts)],
                               ps_l[:, :, :].rearrange("p t e -> p (t e)")).then_inc(l_out, 1)

        @block.gpsimd
        def _(pool):
            with pool.Fori(0, B) as b:
                pool.wait_ge(xnt_ready, b + 1)
                if shared:
                    nc.gpsimd.nop().then_inc(rows_used, 1)
                else:
                    for k in range(KH):
                        op = nc.gpsimd.tensor_copy(c["xnt"][:, k, ds(b * S, S)], xnt[:, k, :])
                    op.then_inc(rows_used, 1)

        @block.vector
        def _(dve):
            with dve.Fori(0, B // 2) as b2:
                dve.wait_ge(t_ready, b2 * 2)
                if shared:
                    dve.wait_ge(rows_kept, b2 * 32)
                for half in range(2):
                    for t in range(TB):
                        at = b2 * (2 * TB) + (half * TB + t)
                        op = nc.vector.tensor_scalar(
                            xn[:, half, t, :], c["resid"][:, ds(at * H, H)], c["mean_var"][:, ds(at * 2, 1)],
                            c["rstd"][:, ds(at, 1)], ALU.subtract, ALU.mult)
                    op.then_inc(xn_ready, 1)
                if shared:
                    for half in range(2):
                        b = b2 * 2 + half
                        dve.wait_ge(gated, b + 1)
                        dve.wait_ge(y_ready, b)
                        nc.vector.tensor_tensor(hidden[:, :], gate[:, :], ps_g[0:F, 1, :], ALU.mult).then_inc(
                            hidden_ready, 1)
                        dve.wait_ge(y_ready, b + 1)
                        r = c["resid"][:, ds(b * (TB * H), TB * H)]
                        nc.vector.tensor_tensor(r, r, ps_y[:, :, :].rearrange("p t f -> p (t f)"),
                                                ALU.add).then_inc(y_added, 1)


def chosen_groups(nc, dve, step, gs, ge, gt, lower, keep, G, take):
    a = gs[:, :, :].unsqueeze(3).to_broadcast([P, NT, G, G])
    b = gs[:, :, :].unsqueeze(2).to_broadcast([P, NT, G, G])
    low = lower.unsqueeze(1).to_broadcast([P, NT, G, G])
    step(nc.vector.tensor_tensor(ge, b, a, ALU.is_ge))
    step(nc.vector.tensor_tensor(gt, b, a, ALU.is_gt))
    step(nc.vector.tensor_tensor(ge, ge, low, ALU.mult))
    step(nc.vector.tensor_tensor(gt, gt, ge, ALU.max))
    step(nc.vector.tensor_reduce(keep, gt, AX.X, ALU.add))
    step(nc.vector.tensor_scalar(keep, keep, float(take), NEG, ALU.is_ge, ALU.mult))


def dense_experts(nc, c, d):
    E, G, TOPG, K, I = 16, 4, 2, 4, 176
    FT = c["FT"]
    ER = 32
    with ExitStack() as outer:
        def sbo(name, shape, dt=F32):
            return outer.enter_context(nc.sbuf_tensor(name, shape, dt))

        c["xnt"] = sbo("xnt_all", [P, KH, T])
        c["logits"] = sbo("logits0", [P, NT * E])
        normalised_rows(nc, c, d, "l0", E)
        weights_t = sbo("weights_t", [3 * ER, T], BF16)

        with ExitStack() as ctx:
            def sb(name, shape, dt=F32):
                return ctx.enter_context(nc.sbuf_tensor(f"{name}_r0", shape, dt))

            logit = c["logits"][:, :].rearrange("p (t e) -> p t e", e=E)
            key, sig = sb("key", [P, NT, E]), sb("sig", [P, NT, E])
            gs, keep = sb("gs", [P, NT, G]), sb("keep", [P, NT, G])
            ge, gt = sb("ge", [P, NT, G, G]), sb("gt", [P, NT, G, G])
            best, place = sb("best", [P, NT, 8]), sb("place", [P, NT, 8], U32)
            placef = sb("placef", [P, NT, 8])
            hot, mask = sb("hot", [P, K, NT, E]), sb("mask", [P, NT, E])
            total = sb("total", [P, NT, 1])
            weight = sb("weight", [P, NT, ER])
            rest = sb("rest", [P, NT, ER])
            wparts = sb("wparts", [P, NT, 3, ER], BF16)
            low, numbers = sb("low", [P, G, G]), sb("numbers", [P, E])
            ps_w = ctx.enter_context(nc.psum_tensor("ps_w", [3 * ER, T], F32))
            tables_in, sigmoid_done, dve_step, split_done, turned, top_done, index_done = (
                semaphore(nc, c, x + "_r0") for x in (
                    "tables_in", "sigmoid_done", "dve_step", "split_done", "turned", "top_done", "index_done"))
            block = ctx.enter_context(nc.Block())

            @block.sync
            def _(sp):
                sp.dma_start(low[:, :, :], d["lower4"]).then_inc(tables_in, 16)
                sp.dma_start(numbers[:, :], d["numbers"][:, 0:E]).then_inc(tables_in, 16)

            @block.scalar
            def _(act):
                nc.scalar.activation(sig[:, :, :], logit, ACT.Sigmoid).then_inc(sigmoid_done, 1)
                act.wait_ge(turned, 1)
                nc.scalar.copy(weights_t[:, :], ps_w[:, :])

            @block.vector
            def _(dve):
                count = [0]

                def step(op):
                    count[0] += 1
                    op.then_inc(dve_step, 1)
                    dve.wait_ge(dve_step, count[0])

                dve.wait_ge(tables_in, 32)
                step(nc.vector.tensor_scalar(key[:, :, :], logit, 17.0, None, ALU.min))
                step(nc.vector.tensor_reduce(gs[:, :, :], key[:, :, :].rearrange("p t (g e) -> p t g e", g=G), AX.X,
                                             ALU.max))
                chosen_groups(nc, dve, step, gs, ge[:, :, :, :], gt[:, :, :, :], low[:, :, :], keep[:, :, :], G, TOPG)
                step(nc.vector.tensor_tensor(key[:, :, :].rearrange("p t (g e) -> p t g e", g=G),
                                             key[:, :, :].rearrange("p t (g e) -> p t g e", g=G),
                                             keep[:, :, :].unsqueeze(3).to_broadcast([P, NT, G, E // G]), ALU.add))
                keys = key[:, :, :].rearrange("p t e -> p (t e)")
                bests = best[:, :, :].rearrange("p t e -> p (t e)")
                places = place[:, :, :].rearrange("p t e -> p (t e)")
                for t in range(NT):
                    nc.vector.max(bests[:, t * 8:t * 8 + 8], keys[:, t * E:(t + 1) * E]).then_inc(top_done, 1)
                dve.wait_ge(top_done, NT)
                for t in range(NT):
                    nc.vector.max_index(places[:, t * 8:t * 8 + 8], bests[:, t * 8:t * 8 + 8],
                                        keys[:, t * E:(t + 1) * E]).then_inc(index_done, 1)
                dve.wait_ge(index_done, NT)
                step(nc.vector.tensor_copy(placef[:, :, :], place[:, :, :]))
                for k in range(K):
                    op = nc.vector.tensor_tensor(hot[:, k, :, :], numbers[:, :].unsqueeze(1).to_broadcast([P, NT, E]),
                                                 placef[:, :, k:k + 1].to_broadcast([P, NT, E]), ALU.is_equal)
                step(op)
                step(nc.vector.tensor_tensor(hot[:, 0:2], hot[:, 0:2], hot[:, 2:4], ALU.add))
                step(nc.vector.tensor_tensor(mask[:, :, :], hot[:, 0], hot[:, 1], ALU.add))
                dve.wait_ge(sigmoid_done, 1)
                step(nc.vector.tensor_tensor(sig[:, :, :], sig[:, :, :], mask[:, :, :], ALU.mult))
                step(nc.vector.tensor_reduce(total[:, :, 0], sig[:, :, :], AX.X, ALU.add))
                step(nc.vector.reciprocal(total[:, :, :], total[:, :, :]))
                step(nc.vector.memset(weight[:, :, :], 0.0))
                step(nc.vector.tensor_tensor(weight[:, :, 0:E], sig[:, :, :],
                                             total[:, :, :].to_broadcast([P, NT, E]), ALU.mult))
                step(nc.vector.memset(weight[:, :, E:E + 1], 1.0))
                step(nc.vector.tensor_copy(wparts[:, :, 0, :], weight[:, :, :]))
                step(nc.vector.tensor_tensor(rest[:, :, :], weight[:, :, :], wparts[:, :, 0, :], ALU.subtract))
                step(nc.vector.tensor_copy(wparts[:, :, 1, :], rest[:, :, :]))
                nc.vector.tensor_tensor(wparts[:, :, 2, :], rest[:, :, :], wparts[:, :, 1, :],
                                        ALU.subtract).then_inc(split_done, 1)

            @block.tensor
            def _(pe):
                pe.wait_ge(split_done, 1)
                for t in range(NT):
                    op = nc.tensor.matmul(ps_w[:, t * P:(t + 1) * P], wparts[:, t, :, :].rearrange("p c e -> p (c e)"),
                                          c["masks"][:, 0, :], start=True, stop=True)
                op.then_inc(turned, 1)

        with ExitStack() as ctx:
            def sb(name, shape, dt=F32):
                return ctx.enter_context(nc.sbuf_tensor(f"{name}_e0", shape, dt))

            def sem(name):
                return semaphore(nc, c, f"{name}_e0")

            NW = 5
            FW = FT // NW
            w1, w3 = sb("w1", [P, FT, KH, P]), sb("w3", [P, FT, KH, P])
            w2 = sb("w2", [P, FT, H])
            spread = sb("spread", [3 * ER, FT * P], BF16)
            spread_f = sb("spread_f", [3 * ER, P * FW])
            gate, hidden = sb("gate", [P, 2, S]), sb("hidden", [P, 2, S])
            hidden_w = sb("hidden_w", [P, 2, S])
            zero = sb("zero", [P, 6 * H])
            ps_g = ctx.enter_context(nc.psum_tensor("ps_g_e0", [P, 2, S], F32))
            ps_u = ctx.enter_context(nc.psum_tensor("ps_u_e0", [P, 2, S], F32))
            ps_w = ctx.enter_context(nc.psum_tensor("ps_w_e0", [P, 2, S], F32))
            ps_y = ctx.enter_context(nc.psum_tensor("ps_y_e0", [P, TB, H], F32))
            w_in = [sem(f"w_in{i}") for i in range(NW)]
            spread_in, spread_cast, zero_set, zeros_out = (
                sem("spread_in"), sem("spread_cast"), sem("zero_set"), sem("zeros_out"))
            up_ready, gated, multiplied, weighted, down_done, added = (
                sem("up_ready"), sem("gated"), sem("multiplied"), sem("weighted"), sem("down_done"), sem("added"))
            block = ctx.enter_context(nc.Block())

            @block.sync
            def _(sp):
                for i in range(NW):
                    f = slice(i * FW, (i + 1) * FW)
                    sp.dma_start(w1[:, f, :, :], d["l0_w1"][:, f]).then_inc(w_in[i], 16)
                    sp.dma_start(w3[:, f, :, :], d["l0_w3"][:, f]).then_inc(w_in[i], 16)
                    sp.dma_start(w2[:, f, :], d["l0_w2"][:, f]).then_inc(w_in[i], 16)
                sp.wait_ge(zero_set, 1)
                for t in range(NT):
                    sp.dma_start(d["y6_d"][t * P * 6:(t + 1) * P * 6, :].rearrange("(p k) f -> p (k f)", k=6),
                                 zero[:, :]).then_inc(zeros_out, 16)
                sp.wait_ge(zeros_out, 16 * NT)

            @block.gpsimd
            def _(pool):
                nc.gpsimd.memset(zero[:, :], 0.0).then_inc(zero_set, 1)
                for i in range(NW):
                    pool.wait_ge(spread_cast, i)
                    pool.dma_start(spread_f[:, :], d["spread"][:, i * FW * P:(i + 1) * FW * P]).then_inc(spread_in, 16)
                    pool.wait_ge(spread_in, 16 * (i + 1))
                    nc.gpsimd.tensor_copy(spread[:, i * FW * P:(i + 1) * FW * P], spread_f[:, :]).then_inc(
                        spread_cast, 1)

            def place(f):
                return f % 2

            @block.tensor
            def _(pe):
                def up(cc, f):
                    s = f % 2
                    if isinstance(cc, int):
                        if f % FW == 0:
                            pe.wait_ge(w_in[f // FW], 48)
                            pe.wait_ge(spread_cast, f // FW + 1)
                    n = cc * FT + f
                    if not isinstance(cc, int) or cc > 0 or f >= 1:
                        pe.wait_ge(weighted, n - 1 if f else n)
                    for ps, w in ((ps_g, w1), (ps_u, w3)):
                        for k in range(KH):
                            op = nc.tensor.matmul(ps[:, s, :], w[:, f, k, :], c["xnt"][:, k, ds(cc * S, S)],
                                                  start=k == 0, stop=k == KH - 1)
                    op = nc.tensor.matmul(ps_w[:, s, :], spread[:, f * P:(f + 1) * P],
                                          weights_t[:, ds(cc * S, S)], start=True, stop=True)
                    op.then_inc(up_ready, 1)

                def down(cc, f):
                    pe.wait_ge(weighted, cc * FT + f + 1)
                    if f == 0 and (not isinstance(cc, int) or cc > 0):
                        pe.wait_ge(added, cc)
                    for t in range(TB):
                        op = nc.tensor.matmul(ps_y[:, t, :], hidden_w[:, f % 2, t * P:(t + 1) * P], w2[:, f, :],
                                              start=f == 0 and t % 2 == 0, stop=f == FT - 1, skip_group_check=True)
                    op.then_inc(down_done, 1)

                def row(cc):
                    for f in range(FT):
                        up(cc, f)
                        if f:
                            down(cc, f - 1)
                    down(cc, FT - 1)

                row(0)
                with pe.Fori(1, B) as cc:
                    row(cc)

            @block.scalar
            def _(act):
                with act.Fori(0, B) as cc:
                    for f in range(FT):
                        n = cc * FT + f
                        act.wait_ge(up_ready, n + 1)
                        if f:
                            act.wait_ge(multiplied, n - 1)
                        else:
                            act.wait_ge(multiplied, n)
                        nc.scalar.activation(gate[:, f % 2, :], ps_g[:, f % 2, :], ACT.Silu).then_inc(gated, 1)

            @block.vector
            def _(dve):
                with dve.Fori(0, B) as cc:
                    for f in range(FT):
                        n, s = cc * FT + f, f % 2
                        dve.wait_ge(gated, n + 1)
                        nc.vector.tensor_tensor(hidden[:, s, :], gate[:, s, :], ps_u[:, s, :], ALU.mult).then_inc(
                            multiplied, 1)
                        dve.wait_ge(multiplied, n + 1)
                        dve.wait_ge(down_done, n - 1 if f else n)
                        nc.vector.tensor_tensor(hidden_w[:, s, :], hidden[:, s, :], ps_w[:, s, :],
                                                ALU.mult).then_inc(weighted, 1)
                    dve.wait_ge(down_done, (cc + 1) * FT)
                    r = c["resid"][:, ds(cc * (TB * H), TB * H)]
                    nc.vector.tensor_tensor(r, r, ps_y[:, :, :].rearrange("p t f -> p (t f)"), ALU.add).then_inc(
                        added, 1)


def sparse_experts(nc, c, d):
    E, G, TOPG, K, F = 64, 8, 4, 6, 96
    CAP, SLOTS = 2 * (256 * K // E), 64
    PAIRS = E // 2
    SCALE = 2.5
    with ExitStack() as outer:
        def sbo(name, shape, dt=F32):
            return outer.enter_context(nc.sbuf_tensor(name, shape, dt))

        c["logits"] = sbo("logits1", [P, NT * E])
        normalised_rows(nc, c, d, "l1", E)
        gather_at = sbo("gather_at", [P, PAIRS], I32)
        scatter_at = sbo("scatter_at", [P, PAIRS], I32)
        wk = sbo("wk", [P, NT, K])

        with ExitStack() as ctx:
            def sb(name, shape, dt=F32):
                return ctx.enter_context(nc.sbuf_tensor(f"{name}_r1", shape, dt))

            logit = c["logits"][:, :].rearrange("p (t e) -> p t e", e=E)
            bias, numbers = sb("bias", [P, E]), sb("numbers", [P, E])
            low, pnum, tnum = sb("low", [P, G, G]), sb("pnum", [P, 1]), sb("tnum", [P, NT])
            sig, tanh, key = sb("sig", [P, NT, E]), sb("tanh", [P, NT, E]), sb("key", [P, NT, E])
            work = sb("work", [P, NT, E])
            gs, keep, second = sb("gs", [P, NT, G]), sb("keep", [P, NT, G]), sb("second", [P, NT, G])
            ge, gt = sb("ge", [P, NT, G, G]), sb("gt", [P, NT, G, G])
            best, place = sb("best", [P, NT, 8]), sb("place", [P, NT, 8], U32)
            placef = sb("placef", [P, NT, 8])
            hot = sb("hot", [P, K, NT, E], BF16)
            mask = sb("mask", [P, NT, E], BF16)
            before = sb("before", [P, NT, E], BF16)
            seat = sb("seat", [P, NT, E])
            total, ck = sb("total", [P, NT, 1]), sb("ck", [P, NT, 1])
            values = sb("values", [P, 2, NT, 3, E], BF16)
            seats = sb("seats", [P, 2, NT, SLOTS], BF16)
            table = sb("table", [P, 3, E])
            ps_p = ctx.enter_context(nc.psum_tensor("ps_p", [P, NT, E], F32))
            ps_s = ctx.enter_context(nc.psum_tensor("ps_s_r1", [P, 512], F32))
            tables_in, scores_done, dve_step, top_done, index_done, before_done, places_done, lists_ready, used = (
                semaphore(nc, c, x + "_r1") for x in (
                    "tables_in", "scores_done", "dve_step", "top_done", "index_done", "before_done", "places_done",
                    "lists_ready", "used"))
            block = ctx.enter_context(nc.Block())

            @block.sync
            def _(sp):
                sp.dma_start(low[:, :, :], d["lower8"]).then_inc(tables_in, 16)
                sp.dma_start(numbers[:, :], d["numbers"]).then_inc(tables_in, 16)
                sp.dma_start(pnum[:, :], d["pnum"]).then_inc(tables_in, 16)
                sp.dma_start(tnum[:, :], d["numbers"][:, 0:NT]).then_inc(tables_in, 16)
                sp.dma_start(bias[:, :], d["l1_bias"].rearrange("(a n) -> a n", a=1).to_broadcast([P, E])).then_inc(
                    tables_in, 16)

            @block.scalar
            def _(act):
                nc.scalar.activation(sig[:, :, :], logit, ACT.Sigmoid).then_inc(scores_done, 1)
                nc.scalar.activation(tanh[:, :, :], logit, ACT.Tanh, scale=0.5).then_inc(scores_done, 1)

            @block.vector
            def _(dve):
                count = [0]

                def step(op):
                    count[0] += 1
                    op.then_inc(dve_step, 1)
                    dve.wait_ge(dve_step, count[0])

                tt, tsc = nc.vector.tensor_tensor, nc.vector.tensor_scalar
                all_ = (slice(None),) * 3
                dve.wait_ge(tables_in, 16 * 5)
                dve.wait_ge(scores_done, 2)
                step(tsc(tanh[all_], tanh[all_], 0.5, 0.5, ALU.mult, ALU.add))
                step(tsc(work[all_], logit, -2.0, None, ALU.is_gt))
                step(tt(tanh[all_], tanh[all_], work[all_], ALU.mult))
                step(tsc(work[all_], logit, -2.0, None, ALU.is_le))
                step(tt(work[all_], work[all_], sig[all_], ALU.mult))
                step(tt(key[all_], tanh[all_], work[all_], ALU.add))
                step(nc.vector.tensor_copy(sig[all_], key[all_]))
                step(tt(key[all_], key[all_], bias[:, :].unsqueeze(1).to_broadcast([P, NT, E]), ALU.add))

                def grouped(x):
                    return x[all_].rearrange("p t (g e) -> p t g e", g=G)

                def spread(x):
                    return x[all_].unsqueeze(3).to_broadcast([P, NT, G, E // G])

                step(nc.vector.tensor_reduce(gs[all_], grouped(key), AX.X, ALU.max))
                step(tt(grouped(work), grouped(key), spread(gs), ALU.is_equal))
                step(nc.vector.tensor_reduce(keep[all_], grouped(work), AX.X, ALU.add))
                step(tsc(work[all_], work[all_], NEG, None, ALU.mult))
                step(tt(work[all_], work[all_], key[all_], ALU.add))
                step(nc.vector.tensor_reduce(second[all_], grouped(work), AX.X, ALU.max))
                step(tsc(keep[all_], keep[all_], 2.0, NEG, ALU.is_lt, ALU.mult))
                step(tt(keep[all_], keep[all_], gs[all_], ALU.add))
                step(tt(second[all_], second[all_], keep[all_], ALU.max))
                step(tt(gs[all_], gs[all_], second[all_], ALU.add))
                chosen_groups(nc, dve, step, gs, ge[:, :, :, :], gt[:, :, :, :], low[all_], keep[all_], G, TOPG)
                step(tt(grouped(key), grouped(key), spread(keep), ALU.add))
                keys = key[all_].rearrange("p t e -> p (t e)")
                bests = best[all_].rearrange("p t e -> p (t e)")
                places = place[all_].rearrange("p t e -> p (t e)")
                for t in range(NT):
                    nc.vector.max(bests[:, t * 8:t * 8 + 8], keys[:, t * E:(t + 1) * E]).then_inc(top_done, 1)
                dve.wait_ge(top_done, NT)
                for t in range(NT):
                    nc.vector.max_index(places[:, t * 8:t * 8 + 8], bests[:, t * 8:t * 8 + 8],
                                        keys[:, t * E:(t + 1) * E]).then_inc(index_done, 1)
                dve.wait_ge(index_done, NT)
                step(nc.vector.tensor_copy(placef[all_], place[all_]))
                for k in range(K):
                    op = tt(hot[:, k, :, :], numbers[:, :].unsqueeze(1).to_broadcast([P, NT, E]),
                            placef[:, :, k:k + 1].to_broadcast([P, NT, E]), ALU.is_equal)
                step(op)
                step(tt(hot_a := work[all_], hot[:, 0], hot[:, 1], ALU.add))
                for k in range(2, K - 1):
                    step(tt(hot_a, hot_a, hot[:, k], ALU.add))
                step(tt(mask[all_], hot_a, hot[:, K - 1], ALU.add))
                step(nc.vector.memset(before[:, 0, :], 0.0))
                for t in range(1, NT):
                    step(tt(before[:, t, :], before[:, t - 1, :], mask[:, t - 1, :], ALU.add))
                nc.vector.tensor_copy(work[all_], mask[all_]).then_inc(before_done, 1)
                dve.wait_ge(before_done, 1)
                step(tt(sig[all_], sig[all_], mask[all_], ALU.mult))
                step(nc.vector.tensor_reduce(total[:, :, 0], sig[all_], AX.X, ALU.add))
                step(nc.vector.reciprocal(total[all_], total[all_]))
                step(tt(sig[all_], sig[all_], total[all_].to_broadcast([P, NT, E]), ALU.mult))
                step(tsc(sig[all_], sig[all_], SCALE, None, ALU.mult))
                dve.wait_ge(places_done, 1)
                step(tsc(work[all_], ps_p[all_], float(CAP), None, ALU.is_lt))
                step(tt(sig[all_], sig[all_], work[all_], ALU.mult))
                step(tsc(seat[all_], ps_p[all_], float(CAP), None, ALU.min))
                step(tsc(work[all_], ps_p[all_], float(CAP), 16.0, ALU.is_ge, ALU.mult))
                step(tt(seat[all_], seat[all_], work[all_], ALU.add))
                for k in range(K):
                    s = k % 2
                    if k >= 2:
                        dve.wait_ge(used, k - 1)
                    step(tt(work[all_], seat[all_], hot[:, k], ALU.mult))
                    step(nc.vector.tensor_reduce(ck[:, :, 0], work[all_], AX.X, ALU.add))
                    step(tt(seats[:, s], numbers[:, :].unsqueeze(1).to_broadcast([P, NT, SLOTS]),
                            ck[all_].to_broadcast([P, NT, SLOTS]), ALU.is_equal))
                    nc.vector.tensor_scalar(values[:, s, :, 0, :], hot[:, k], pnum[:, 0:1], None, ALU.mult)
                    tt(values[:, s, :, 1, :], hot[:, k], tnum[:, :].unsqueeze(2).to_broadcast([P, NT, E]), ALU.mult)
                    tsc(values[:, s, :, 2, :], hot[:, k], float(k + 1), None, ALU.mult).then_inc(lists_ready, 1)
                for k in range(K):
                    step(tt(work[all_], sig[all_], hot[:, k], ALU.mult))
                    step(nc.vector.tensor_reduce(wk[:, :, k], work[all_], AX.X, ALU.add))
                dve.wait_ge(used, K)
                step(nc.vector.tensor_copy(table[all_], ps_s[:, 0:3 * E].rearrange("p (c e) -> p c e", c=3)))
                step(nc.vector.scalar_tensor_tensor(table[:, 1], table[:, 1], float(P), table[:, 0], ALU.mult, ALU.add))
                step(nc.vector.scalar_tensor_tensor(table[:, 0], table[:, 1], float(K), table[:, 2], ALU.mult, ALU.add))
                step(tsc(table[:, 2], table[:, 2], 0.5, 65536.0, ALU.is_lt, ALU.mult))
                step(nc.vector.scalar_tensor_tensor(table[:, 0], table[:, 0], -1.0, table[:, 2], ALU.add, ALU.add))
                step(tsc(table[:, 0], table[:, 0], 0.0, None, ALU.max))
                for half in range(2):
                    rows = slice(half * SLOTS, (half + 1) * SLOTS)
                    for dst, i in ((gather_at, 1), (scatter_at, 0)):
                        src = table[rows, i, :].rearrange("p (n h) -> p n h", h=2)[:, :, half]
                        step(nc.vector.tensor_copy(dst[rows, :], src))

            @block.tensor
            def _(pe):
                pe.wait_ge(before_done, 1)
                for t in range(NT):
                    nc.tensor.matmul(ps_p[:, t, :], c["masks"][:, 3, :], mask[:, t, :], start=True, stop=False)
                    op = nc.tensor.matmul(ps_p[:, t, :], c["masks"][:, 4, :], before[:, t, :], start=False, stop=True)
                op.then_inc(places_done, 1)
                for k in range(K):
                    pe.wait_ge(lists_ready, k + 1)
                    for t in range(NT):
                        for half in range(2):
                            op = nc.tensor.matmul(ps_s[half * SLOTS:(half + 1) * SLOTS, 0:3 * E], seats[:, k % 2, t, :],
                                                  values[:, k % 2, t, :, :].rearrange("p c e -> p (c e)"),
                                                  start=k == 0 and t == 0, stop=k == K - 1 and t == NT - 1)
                    op.then_inc(used, 1)

        expert_pairs(nc, c, d, gather_at, scatter_at)
        combine(nc, c, d, wk)


def expert_pairs(nc, c, d, gather_at, scatter_at):
    PAIRS, SLOTS, F, U = 32, 64, 96, 4
    with ExitStack() as ctx:
        def sb(name, shape, dt=F32):
            return ctx.enter_context(nc.sbuf_tensor(f"{name}_p1", shape, dt))

        def sem(name):
            return semaphore(nc, c, f"{name}_p1")

        w_up = [sb(f"w_up{u}", [P, 2, KH, 2 * F]) for u in range(U)]
        w_down = [sb(f"w_down{u}", [F, 2, H]) for u in range(U)]
        at = [sb(f"at{u}", [P, 1], I32) for u in range(U)]
        to = [sb(f"to{u}", [P, 1], I32) for u in range(U)]
        rows = [sb(f"rows{u}", [P, H]) for u in range(U)]
        rows_t = sb("rows_t", [P, 2, KH, P])
        gate, hidden, hidden_t = sb("gate", [P, 2, F]), sb("hidden", [P, 2, F]), sb("hidden_t", [F, 2, P])
        result = [sb(f"result{u}", [P, H]) for u in range(U)]
        ps_x = [ctx.enter_context(nc.psum_tensor(f"ps_x{i}", [P, KH, P], F32)) for i in range(2)]
        ps_h = [ctx.enter_context(nc.psum_tensor(f"ps_h{i}", [P, 2 * F], F32)) for i in range(2)]
        ps_t = [ctx.enter_context(nc.psum_tensor(f"ps_ht{i}", [F, P], F32)) for i in range(2)]
        ps_o = [ctx.enter_context(nc.psum_tensor(f"ps_o{i}", [P, H], F32)) for i in range(2)]
        w_in = [sem(f"w_in{u}") for u in range(U)]
        gathered = [sem(f"gathered{u}") for u in range(U)]
        scattered = [sem(f"scattered{u}") for u in range(U)]
        at_ready, to_ready, pool_passed = sem("at_ready"), sem("to_ready"), sem("pool_passed")
        x_turned, x_copied, up_done, gated, hidden_done, h_turned, h_copied, down_done, result_done = (
            sem(x) for x in ("x_turned", "x_copied", "up_done", "gated", "hidden_done", "h_turned", "h_copied",
                             "down_done", "result_done"))
        block = ctx.enter_context(nc.Block())

        def steps(eng, one, lag):
            for u in range(U):
                for j in range(lag + 1):
                    if u - j >= 0:
                        one(0, u - j, j, u - j)
            with eng.Fori(1, PAIRS // U) as i:
                for u in range(U):
                    for j in range(lag + 1):
                        one(i if u >= j else i - 1, (u - j) % U, j, 99)
            for u in range(lag):
                for j in range(u + 1, lag + 1):
                    one(PAIRS // U - 1, U + u - j, j, 99)

        @block.sync
        def _(sp):
            def load(i, u):
                sp.dma_start(w_up[u][:, :, :, :], d["l1_w_up"][ds(i * U + u, 1)].rearrange(
                    "o p a k f -> (o p) a k f")).then_inc(w_in[u], 16)
                sp.dma_start(w_down[u][:, :, :], d["l1_w_down"][ds(i * U + u, 1)].rearrange(
                    "o p a f -> (o p) a f")).then_inc(w_in[u], 16)

            for u in range(U):
                load(0, u)
            with sp.Fori(1, PAIRS // U) as i:
                for u in range(U):
                    sp.wait_ge(down_done, i * U + (u - 3))
                    load(i, u)

        @block.gpsimd
        def _(pool):
            def one(i, u, j, known):
                n = i * U + u
                if j == 0:
                    if known >= U:
                        pool.wait_ge(x_turned, n - 3)
                    nc.gpsimd.tensor_copy(at[u][:, :], gather_at[:, ds(n, 1)]).then_inc(at_ready, 1)
                    pool.wait_ge(at_ready, n + 1)
                    pool.sem_inc(pool_passed, 1)
                    pool.indirect_dma_start(rows[u][:, :], None, d["xn_d"],
                                            bass.IndirectOffsetOnAxis(ap=at[u][:, 0:1], axis=0)).then_inc(
                        gathered[u], 16)
                if j == 4:
                    pool.wait_ge(result_done, n + 1)
                    if known >= U:
                        pool.wait_ge(scattered[u], i * 16)
                    nc.gpsimd.tensor_copy(to[u][:, :], scatter_at[:, ds(n, 1)]).then_inc(to_ready, 1)
                    pool.wait_ge(to_ready, n + 1)
                    pool.sem_inc(pool_passed, 1)
                    pool.indirect_dma_start(d["y6_d"], bass.IndirectOffsetOnAxis(ap=to[u][:, 0:1], axis=0),
                                            result[u][:, :], None, bounds_check=T * 6 - 1,
                                            oob_is_err=False).then_inc(scattered[u], 16)

            def both(eng, lag):
                for u in range(U):
                    one(0, u, 0, u)
                with eng.Fori(1, PAIRS // U) as i:
                    for u in range(U):
                        one(i, u, 0, 99)
                        one(i - 1, u, 4, 99)
                for u in range(U):
                    one(PAIRS // U - 1, u, 4, 99)

            both(pool, 4)
            for u in range(U):
                pool.wait_ge(scattered[u], 16 * (PAIRS // U))

        @block.tensor
        def _(pe):
            def one(i, u, j, known):
                n, s = i * U + u, u % 2
                if j == 0:
                    pe.wait_ge(gathered[u], (i + 1) * 16)
                    if known >= 2:
                        pe.wait_ge(x_copied, n - 1)
                    for k in range(KH):
                        op = nc.tensor.transpose(ps_x[s][:, k, :], rows[u][:, k * P:(k + 1) * P], c["ident"][:, :])
                    op.then_inc(x_turned, 1)
                if j == 1:
                    pe.wait_ge(x_copied, n + 1)
                    pe.wait_ge(w_in[u], (i + 1) * 32)
                    if known >= 2:
                        pe.wait_ge(hidden_done, n - 1)
                    for k in range(KH):
                        for a in range(2):
                            op = nc.tensor.matmul(ps_h[s][a * SLOTS:(a + 1) * SLOTS, :],
                                                  rows_t[:, s, k, a * SLOTS:(a + 1) * SLOTS], w_up[u][:, a, k, :],
                                                  start=k == 0, stop=k == KH - 1)
                    op.then_inc(up_done, 1)
                if j == 2:
                    pe.wait_ge(hidden_done, n + 1)
                    if known >= 2:
                        pe.wait_ge(h_copied, n - 1)
                    nc.tensor.transpose(ps_t[s][:, :], hidden[:, s, :], c["ident"][:, :]).then_inc(h_turned, 1)
                if j == 3:
                    pe.wait_ge(h_copied, n + 1)
                    if known >= 2:
                        pe.wait_ge(result_done, n - 1)
                    for a in range(2):
                        op = nc.tensor.matmul(ps_o[s][a * SLOTS:(a + 1) * SLOTS, :],
                                              hidden_t[:, s, a * SLOTS:(a + 1) * SLOTS], w_down[u][:, a, :],
                                              start=True, stop=True)
                    op.then_inc(down_done, 1)

            steps(pe, one, 3)

        @block.scalar
        def _(act):
            def one(i, u, j, known):
                n, s = i * U + u, u % 2
                if j == 0:
                    act.wait_ge(x_turned, n + 1)
                    if known >= 2:
                        act.wait_ge(up_done, n - 1)
                    nc.scalar.copy(rows_t[:, s, :, :], ps_x[s][:, :, :]).then_inc(x_copied, 1)
                if j == 1:
                    act.wait_ge(up_done, n + 1)
                    if known >= 2:
                        act.wait_ge(hidden_done, n - 1)
                    nc.scalar.activation(gate[:, s, :], ps_h[s][:, 0:F], ACT.Silu).then_inc(gated, 1)

            steps(act, one, 1)

        @block.vector
        def _(dve):
            def one(i, u, j, known):
                n, s = i * U + u, u % 2
                if j == 0:
                    dve.wait_ge(gated, n + 1)
                    if known >= 2:
                        dve.wait_ge(h_turned, n - 1)
                    nc.vector.tensor_tensor(hidden[:, s, :], gate[:, s, :], ps_h[s][:, F:2 * F], ALU.mult).then_inc(
                        hidden_done, 1)
                if j == 1:
                    dve.wait_ge(h_turned, n + 1)
                    if known >= 2:
                        dve.wait_ge(down_done, n - 1)
                    nc.vector.tensor_copy(hidden_t[:, s, :], ps_t[s][:, :]).then_inc(h_copied, 1)
                if j == 2:
                    dve.wait_ge(down_done, n + 1)
                    if known >= U:
                        dve.wait_ge(scattered[u], i * 16)
                    nc.vector.tensor_copy(result[u][:, :], ps_o[s][:, :]).then_inc(result_done, 1)

            steps(dve, one, 2)


def combine(nc, c, d, wk):
    K = 6
    with ExitStack() as ctx:
        R = 4
        y = ctx.enter_context(nc.sbuf_tensor("y_choices", [P, R, K, H], F32))
        y_in = [semaphore(nc, c, f"y_in{r}") for r in range(R)]
        y_added = semaphore(nc, c, "y_added")
        stored = semaphore(nc, c, "out_stored")
        block = ctx.enter_context(nc.Block())

        @block.sync
        def _(sp):
            def load(t, r):
                sp.dma_start(y[:, r, :, :].rearrange("p k f -> p (k f)"),
                             d["y6_d"][ds(t * (P * K), P * K), :].rearrange("(p k) f -> p (k f)", k=K)).then_inc(
                    y_in[r], 16)

            for r in range(R):
                load(r, r)
            with sp.Fori(1, NT // R) as i:
                for r in range(R):
                    sp.wait_ge(y_added, (i * R + (r - 3)) * K)
                    load(i * R + r, r)

        @block.vector
        def _(dve):
            with dve.Fori(0, NT // R) as i:
                for r in range(R):
                    dve.wait_ge(y_in[r], (i + 1) * 16)
                    for k in range(K):
                        x = c["resid"][:, ds((i * R + r) * H, H)]
                        nc.vector.scalar_tensor_tensor(
                            x, y[:, r, k, :], wk[:, :, :].rearrange("p t k -> p (t k)")[:, ds((i * R + r) * K + k, 1)],
                            x, ALU.mult, ALU.add).then_inc(y_added, 1)
                        dve.wait_ge(y_added, (i * R + r) * K + (k + 1))

        @block.scalar
        def _(act):
            with act.Fori(0, NT) as t:
                act.wait_ge(y_added, (t + 1) * K)
                act.dma_start(d["out"][ds(t * P, P), :], c["resid"][:, ds(t * H, H)]).then_inc(stored, 16)
            act.wait_ge(stored, 16 * NT)


def build(nc, d, upto=99):
    for L in (L0, L1):
        d[f"{L.name}_qd"] = nc.dram_tensor(f"{L.name}_qd", [3, L.blocks, L.d, HB, S], BF16, kind="Internal").ap()
        d[f"{L.name}_kd"] = nc.dram_tensor(f"{L.name}_kd", [3, L.blocks, L.d, L.kv_of_block, S], BF16,
                                           kind="Internal").ap()
        d[f"{L.name}_vd"] = nc.dram_tensor(f"{L.name}_vd", [L.groups, S, L.vw], F32, kind="Internal").ap()
        d[f"{L.name}_od"] = nc.dram_tensor(f"{L.name}_od", [L.groups * P, S], F32, kind="Internal").ap()
    d["xn_d"] = nc.dram_tensor("xn_d", [T, H], F32, kind="Internal").ap()
    d["y6_d"] = nc.dram_tensor("y6_d", [T * 6, H], F32, kind="Internal").ap()
    d["neg_d"] = nc.dram_tensor("neg_d", [4, 3 * HQ * TB, P], BF16, kind="Internal").ap()
    with ExitStack() as ctx:
        def sb(name, shape, dt=F32):
            return ctx.enter_context(nc.sbuf_tensor(name, shape, dt))

        c = {
            "semaphores": [], "resid": sb("resid_f32", [P, NT * H]), "mean_var": sb("mean_var", [P, NT * 2]), "rstd": sb("rstd", [P, NT]),
            "masks": sb("masks_bf16", [P, 5, P], BF16), "ident": sb("ident_f32", [P, P]), "bo": sb("bo", [P, H]),
        }
        c["FT"] = d["l0_w2"].shape[1]
        load_constants(nc, c, d)
        for L in (L0, L1):
            layernorm_statistics(nc, c, f"a{L.name}")
            project(nc, c, d, L)
            attend(nc, c, d, L)
            join(nc, c, d, L)
            if L is L0:
                if upto < 1: break
                layernorm_statistics(nc, c, "f0")
                dense_experts(nc, c, d)
                retire_semaphores(nc, c)
            else:
                if upto < 3: break
                layernorm_statistics(nc, c, "f1")
                sparse_experts(nc, c, d)
            if upto < 2: break
        if upto < 99:
            store_residual(nc, c, d)


def store_residual(nc, c, d):
    with ExitStack() as ctx:
        stored = semaphore(nc, c, "stored")
        block = ctx.enter_context(nc.Block())

        @block.sync
        def _(sp):
            for b in range(B):
                sp.dma_start(d["out"][b * S:(b + 1) * S, :].rearrange("(t p) f -> p t f", p=P),
                             c["resid"][:, b * TB * H:(b + 1) * TB * H].rearrange("p (t f) -> p t f", f=H)).then_inc(
                    stored, 16)
            sp.wait_ge(stored, 16 * B)


def shape_constants():
    half = L0.d // 2
    inv = np.float32(1.0) / (np.float32(10000.0) ** (np.arange(half, dtype=np.float32) / np.float32(half)))
    freq = (np.arange(S, dtype=np.float32)[:, None] * inv[None, :].astype(np.float32)).astype(np.float64)
    dim = (np.arange(P) % L0.d) // 2
    sign = np.where(np.arange(P) % 2 == 0, -1.0, 1.0)[:, None]
    cos = np.cos(freq).T[dim].astype(np.float32)
    sin = (np.sin(freq).T[dim] * sign).astype(np.float32)
    i = np.arange(P)
    masks = np.zeros((P, 5, P), np.float32)
    masks[:, 0] = i[:, None] == i[None, :]
    masks[:, 1] = np.where(i[None, :] > i[:, None], NEG, 0)
    masks[:, 2] = np.where(i[:, None] > i[None, :], NEG, 0)
    masks[:, 3] = i[:, None] < i[None, :]
    masks[:, 4] = 1
    expert = np.minimum(np.arange(25 * P) // 176, 16)
    spread = np.zeros((3, 32, 25 * P), np.float32)
    spread[:, expert, np.arange(25 * P)] = 1

    def lower(n):
        x = np.arange(n)[None, :] < np.arange(n)[:, None]
        return np.broadcast_to(x.astype(np.float32), (P, n, n)).copy()

    return {"cos": cos, "sin": sin, "masks": masks, "ident": np.eye(P, dtype=np.float32),
            "spread": spread.reshape(96, 25 * P), "lower4": lower(4), "lower8": lower(8),
            "numbers": np.broadcast_to(np.arange(64, dtype=np.float32), (P, 64)).copy(),
            "pnum": np.arange(P, dtype=np.float32)[:, None]}


def lay_out(inputs):
    a = {k: np.asarray(v) for k, v in inputs.items()}

    def columns(w):
        return np.ascontiguousarray(w.T.reshape(-1, P, w.shape[0]).transpose(1, 0, 2))

    out = {"x": a["L0_attn_x"].reshape(T, H)}
    for L in (L0, L1):
        for w in "qkvo":
            out[f"{L.name}_w{w}"] = columns(a[f"L{L.name[1]}_attn_W{w}"])
            b = a[f"L{L.name[1]}_attn_b{w}"]
            out[f"{L.name}_b{w}"] = np.ascontiguousarray(b.reshape(-1, min(P, b.size)).T) if w in "qk" else b
    out["l0_router"] = columns(a["L0_ffn_gate_w"])
    out["l1_router"] = np.ascontiguousarray(a["L1_ffn_gate_w"].reshape(KH, P, 64).transpose(1, 0, 2))
    out["l1_bias"] = a["L1_ffn_bias"]
    pad = np.zeros((25 * P - 18 * 176, H), np.float32)
    for dst, w, ws in (("l0_w1", "L0_ffn_W1", "L0_ffn_Ws1"), ("l0_w3", "L0_ffn_W3", "L0_ffn_Ws3")):
        x = np.concatenate([a[w].reshape(-1, H), a[ws], pad])
        out[dst] = np.ascontiguousarray(x.reshape(25, P, KH, P).transpose(3, 0, 2, 1))
    x = np.concatenate([a["L0_ffn_W2"].transpose(0, 2, 1).reshape(-1, H), a["L0_ffn_Ws2"].T, pad])
    out["l0_w2"] = np.ascontiguousarray(x.reshape(25, P, H).transpose(1, 0, 2))
    gu = np.concatenate([a["L1_ffn_w_gate"], a["L1_ffn_w_up"]], -1)
    out["l1_w_up"] = np.ascontiguousarray(gu.reshape(32, 2, KH, P, 192).transpose(0, 3, 1, 2, 4))
    out["l1_w_down"] = np.ascontiguousarray(a["L1_ffn_w_down"].reshape(32, 2, 96, H).transpose(0, 2, 1, 3))
    for dst, w in (("l1_wsg", "L1_ffn_ws_gate"), ("l1_wsu", "L1_ffn_ws_up")):
        out[dst] = np.ascontiguousarray(a[w].reshape(KH, P, 96).transpose(1, 0, 2))
    out["l1_wsd"] = a["L1_ffn_ws_down"]
    out.update(shape_constants())
    return out


def kernel(**inputs):
    import concourse.bacc as _bacc
    from concourse.bass_utils import run_bass_kernel_spmd as _run

    nc = _bacc.Bacc("TRN2", target_bir_lowering=False, num_devices=1)
    arrays, d = {}, {}
    for name, a in lay_out(inputs).items():
        a = np.ascontiguousarray(a)
        arrays[f"in_{name}"] = a
        d[name] = nc.dram_tensor(f"in_{name}", a.shape, mybir.dt.from_np(a.dtype), kind="ExternalInput").ap()
    d["out"] = nc.dram_tensor("out_0", [T, H], F32, kind="ExternalOutput").ap()
    build(nc, d)
    r = _run(nc, [arrays], core_ids=[0])
    return r.results[0]["out_0"].reshape(B, S, H)
```

```python
from contextlib import ExitStack

import concourse.bass as bass
import numpy as np
from concourse import mybir

ALU = mybir.AluOpType
ACT = mybir.ActivationFunctionType
AX = mybir.AxisListType
F32 = mybir.dt.float32
BF16 = mybir.dt.bfloat16
I32 = mybir.dt.int32
F32R = mybir.dt.float32r
U32 = mybir.dt.uint32
ds = bass.ds

P = 128
B, S, H = 4, 512, 256
T = B * S
NT = T // P
TB = S // P
KH = H // P
HQ = 4
HB = 16
QUAD = 32
M_ROW = 96
NEG = -1.0e30
HIGH_BITS = -(1 << 12)

PAIRS_L0 = [(0, 0), (0, 1), (0, 2), (1, 0), (1, 1), (2, 0)]
PAIRS_L1 = [(i, j) for i in range(3) for j in range(3)]


class Layer:

    def __init__(self, name, d, nq, nkv, causal, scale, pairs):
        self.name, self.d, self.nq, self.nkv, self.causal, self.scale, self.pairs = (
            name, d, nq, nkv, causal, scale, pairs)
        self.rows = len(pairs) * d
        self.blocks = B * nq // HB
        self.groups = self.blocks * HB // HQ
        self.kv_of_block = HB * nkv // nq
        self.kv_of_group = HQ * nkv // nq
        self.vw = self.kv_of_group * QUAD


L0 = Layer("l0", 16, 16, 16, True, 0.25, PAIRS_L0)
L1 = Layer("l1", 8, 32, 8, False, 8 ** -0.5, PAIRS_L1)


def runs(parts):
    out = []
    for n, p in enumerate(parts):
        if out and out[-1][0] == p:
            out[-1][2] += 1
        else:
            out.append([p, n, 1])
    return out


def climbs(parts):
    out = []
    for n, p in enumerate(parts):
        if p == 0:
            out.append([n, 0])
        out[-1][1] += 1
    return out


def semaphore(nc, c, name):
    s = nc.alloc_semaphore(name=name)
    c["semaphores"].append(s)
    return s


def retire_semaphores(nc, c):
    nc.all_engine_barrier()
    nc.clear_and_free_semaphores(c["semaphores"])
    nc.all_engine_barrier()
    c["semaphores"] = []


def wait_above_zero(eng, sem, value):
    if value > 0:
        eng.wait_ge(sem, value)


def layernorm_statistics(nc, c, tag):
    with ExitStack() as ctx:
        stats = ctx.enter_context(nc.sbuf_tensor(f"stats_{tag}", [P, NT * 6], F32))
        var = ctx.enter_context(nc.sbuf_tensor(f"var_{tag}", [P, NT], F32))
        root = ctx.enter_context(nc.sbuf_tensor(f"root_{tag}", [P, NT], F32))
        work = ctx.enter_context(nc.sbuf_tensor(f"work_{tag}", [P, NT], F32))
        stats_done, mean_done, var_done, root_done, step_done = (
            semaphore(nc, c, f"{n}_{tag}")
            for n in ("stats_done", "mean_done", "var_done", "root_done", "step_done"))
        block = ctx.enter_context(nc.Block())
        mean_var = c["mean_var"][:, :].rearrange("p (t s) -> p t s", s=2)

        @block.vector
        def _(dve):
            with dve.Fori(0, NT // 8) as i:
                for j in range(8):
                    nc.vector.bn_stats(stats[:, ds(i * (8 * 6) + j * 6, 6)],
                                       c["resid"][:, ds(i * (8 * H) + j * H, H)]).then_inc(stats_done, 1)
            dve.wait_ge(stats_done, NT)
            for t in range(NT):
                nc.vector.bn_aggr(c["mean_var"][:, t * 2:t * 2 + 2], stats[:, t * 6:t * 6 + 6]).then_inc(mean_done, 1)
            dve.wait_ge(mean_done, NT)
            nc.vector.tensor_scalar(var[:, :], mean_var[:, :, 1], 1e-5, None, ALU.add).then_inc(var_done, 1)
            dve.wait_ge(root_done, 1)
            nc.vector.reciprocal(c["rstd"][:, :], root[:, :]).then_inc(step_done, 1)
            dve.wait_ge(step_done, 1)
            nc.vector.tensor_tensor(work[:, :], c["rstd"][:, :], c["rstd"][:, :], ALU.mult).then_inc(step_done, 1)
            dve.wait_ge(step_done, 2)
            nc.vector.tensor_tensor(work[:, :], work[:, :], var[:, :], ALU.mult).then_inc(step_done, 1)
            dve.wait_ge(step_done, 3)
            nc.vector.tensor_scalar(work[:, :], work[:, :], -0.5, 1.5, ALU.mult, ALU.add).then_inc(step_done, 1)
            dve.wait_ge(step_done, 4)
            nc.vector.tensor_tensor(c["rstd"][:, :], c["rstd"][:, :], work[:, :], ALU.mult).then_inc(step_done, 1)

        @block.scalar
        def _(act):
            act.wait_ge(var_done, 1)
            nc.scalar.activation(root[:, :], var[:, :], ACT.Sqrt).then_inc(root_done, 1)


def load_constants(nc, c, d):
    with ExitStack() as ctx:
        masks = ctx.enter_context(nc.sbuf_tensor("masks_f32", [P, 5, P], F32))
        loaded = semaphore(nc, c, "constants_loaded")
        block = ctx.enter_context(nc.Block())

        @block.sync
        def _(sp):
            for tt in range(B):
                sp.dma_start(c["resid"][:, tt * TB * H:(tt + 1) * TB * H].rearrange("p (t f) -> p t f", f=H),
                             d["x"][tt * S:(tt + 1) * S, :].rearrange("(t p) f -> p t f", p=P)).then_inc(loaded, 16)
            sp.dma_start(masks[:, :, :], d["masks"]).then_inc(loaded, 16)
            sp.dma_start(c["ident"][:, :], d["ident"]).then_inc(loaded, 16)
            sp.wait_ge(loaded, 16 * (B + 2))

        @block.vector
        def _(dve):
            dve.wait_ge(loaded, 16 * (B + 2))
            nc.vector.tensor_copy(c["masks"][:, :, :], masks[:, :, :])


def project(nc, c, d, L):
    rope = L.causal
    n = L.name
    kf = L.nkv * L.d
    KT = -(-kf // P)
    kp = min(kf, P)
    NF = KH + KT
    with ExitStack() as ctx:
        def sb(name, shape, dt=F32):
            return ctx.enter_context(nc.sbuf_tensor(f"{name}_{n}", shape, dt))

        def sem(name):
            return semaphore(nc, c, f"{name}_{n}")

        wq, wk, wv = sb("wq_sb", [P, KH, H]), sb("wk_sb", [P, KH, kf]), sb("wv_sb", [P, KH, kf])
        bqk, bv = sb("bqk_sb", [P, NF]), sb("bv_sb", [P, kf])
        if rope:
            cos, sin = sb("cos_sb", [P, S]), sb("sin_sb", [P, S])
            swapped = sb("swapped", [P, NF, S])
        xn = sb("xn", [P, 2, TB, H])
        xnt = sb("xnt", [P, 2, KH, S])
        qk = sb("qk", [P, NF, S])
        rest = sb("rest", [P, NF, S])
        parts = sb("parts", [P, 2, 3, NF, S], BF16)
        vaug = sb("vaug", [P, TB, L.nkv, QUAD])
        ps_t = ctx.enter_context(nc.psum_tensor(f"ps_t_{n}", [P, KH, S], F32))
        ps_qk = ctx.enter_context(nc.psum_tensor(f"ps_qk_{n}", [P, NF, S], F32))
        ps_v = ctx.enter_context(nc.psum_tensor(f"ps_v_{n}", [P, TB, 256], F32))

        weights_in, xn_ready, t_ready, xnt_ready, qk_ready, v_ready = (
            sem(x) for x in ("weights_in", "xn_ready", "t_ready", "xnt_ready", "qk_ready", "v_ready"))
        qk_biased, rope_swapped, rope_cos, rope_sin, roped = (
            sem(x) for x in ("qk_biased", "rope_swapped", "rope_cos", "rope_sin", "roped"))
        part0, rest1, part1, part2, v_out, v_stored, ones_set = (
            sem(x) for x in ("part0", "rest1", "part1", "part2", "v_out", "v_stored", "ones_set"))
        parts_stored = [sem("parts_stored0"), sem("parts_stored1")]
        n_weights = 7 + 2 * rope
        q_stores = KH
        k_stores = KT if rope else 2
        n_parts = 3 * (q_stores + k_stores)
        hg = L.nkv // L.kv_of_group
        block = ctx.enter_context(nc.Block())

        @block.sync
        def _(sp):
            for dst, src in [(wq, "wq"), (wk, "wk"), (wv, "wv")]:
                sp.dma_start(dst[:, :, :], d[f"{n}_{src}"]).then_inc(weights_in, 16)
            sp.dma_start(bqk[:, 0:KH], d[f"{n}_bq"]).then_inc(weights_in, 16)
            sp.dma_start(bqk[0:kp, KH:NF], d[f"{n}_bk"]).then_inc(weights_in, 16)
            sp.dma_start(bv[:, :], d[f"{n}_bv"].rearrange("(a n) -> a n", a=1).to_broadcast([P, kf])).then_inc(
                weights_in, 16)
            sp.dma_start(c["bo"][:, :], d[f"{n}_bo"].rearrange("(a n) -> a n", a=1).to_broadcast([P, H])).then_inc(
                weights_in, 16)
            if rope:
                sp.dma_start(cos[:, :], d["cos"]).then_inc(weights_in, 16)
                sp.dma_start(sin[:, :], d["sin"]).then_inc(weights_in, 16)
            for b in range(B):
                sp.wait_ge(v_out, b + 1)
                for g in range(hg):
                    w = L.kv_of_group
                    sp.dma_start(d[f"{n}_vd"][ds(b * hg + g, 1)].rearrange("o (t p) w -> p (o t) w", p=P),
                                 vaug[:, :, g * w:(g + 1) * w, :].rearrange("p t h w -> p t (h w)")).then_inc(
                        v_stored, 16)
                for part, ready in ((0, part0), (1, part1), (2, part2)):
                    sp.wait_ge(ready, b + 1)
                    qd, kd = d[f"{n}_qd"], d[f"{n}_kd"]
                    for m in range(KH):
                        h8 = P // L.d
                        blk = b if rope else b * 2 + m
                        dst = qd[part, ds(blk, 1), :, (m * h8 if rope else 0):(m + 1) * h8 if rope else HB, :]
                        sp.dma_start(dst.rearrange("o e h t -> (o h) e t"), parts[:, b % 2, part, m, :]).then_inc(
                            parts_stored[b % 2], 16)
                    for m in range(k_stores):
                        if rope:
                            dst, src = kd[part, ds(b, 1), :, m * 8:(m + 1) * 8, :], parts[:, b % 2, part, KH + m, :]
                        else:
                            dst, src = kd[part, ds(b * 2 + m, 1)], parts[m * 32:(m + 1) * 32, b % 2, part, KH, :]
                        sp.dma_start(dst.rearrange("o e h t -> (o h) e t"), src).then_inc(parts_stored[b % 2], 16)
            for slot in range(2):
                sp.wait_ge(parts_stored[slot], 16 * n_parts * B // 2)
            sp.wait_ge(v_stored, 16 * hg * B)

        def normalise(dve, b):
            wait_above_zero(dve, t_ready, b - 1)
            for t in range(TB):
                at = b * TB + t
                op = nc.vector.tensor_scalar(
                    xn[:, b % 2, t, :], c["resid"][:, ds(at * H, H)], c["mean_var"][:, ds(at * 2, 1)],
                    c["rstd"][:, ds(at, 1)], ALU.subtract, ALU.mult)
            op.then_inc(xn_ready, 1)

        @block.tensor
        def _(pe):
            def turn(b):
                pe.wait_ge(xn_ready, b + 1)
                wait_above_zero(pe, xnt_ready, b)
                for k in range(KH):
                    for t in range(TB):
                        op = nc.tensor.transpose(ps_t[:, k, t * P:(t + 1) * P],
                                                 xn[:, b % 2, t, k * P:(k + 1) * P], c["ident"][:, :])
                op.then_inc(t_ready, 1)

            turn(0)
            pe.wait_ge(weights_in, 16 * n_weights)
            for b in range(B):
                if b + 1 < B:
                    turn(b + 1)
                pe.wait_ge(xnt_ready, b + 1)
                wait_above_zero(pe, qk_biased, b)
                for m in range(NF):
                    w, lo, width = (wq, m * P, P) if m < KH else (wk, (m - KH) * P, kp)
                    for k in range(KH):
                        op = nc.tensor.matmul(ps_qk[0:width, m, :], w[:, k, lo:lo + width], xnt[:, b % 2, k, :],
                                              start=k == 0, stop=k == KH - 1)
                op.then_inc(qk_ready, 1)
                wait_above_zero(pe, v_out, b)
                for t in range(TB):
                    for k in range(KH):
                        op = nc.tensor.matmul(ps_v[:, t, 0:kf], xnt[:, b % 2, k, t * P:(t + 1) * P], wv[:, k, :],
                                              start=k == 0, stop=k == KH - 1)
                op.then_inc(v_ready, 1)

        @block.scalar
        def _(act):
            def keep_turned(b):
                act.wait_ge(t_ready, b + 1)
                wait_above_zero(act, v_ready, b - 1)
                nc.scalar.copy(xnt[:, b % 2, :, :], ps_t[:, :, :]).then_inc(xnt_ready, 1)

            keep_turned(0)
            act.wait_ge(weights_in, 16 * n_weights)
            for b in range(B):
                if b + 1 < B:
                    keep_turned(b + 1)
                act.wait_ge(qk_ready, b + 1)
                wait_above_zero(act, rest1, b)
                for m in range(NF):
                    w = P if m < KH else kp
                    op = nc.scalar.activation(qk[0:w, m, :], ps_qk[0:w, m, :], ACT.Identity,
                                              bias=bqk[0:w, m:m + 1])
                op.then_inc(qk_biased, 1)
                act.wait_ge(roped if rope else qk_biased, b + 1)
                wait_above_zero(act, parts_stored[b % 2], 16 * n_parts * (b // 2))
                nc.scalar.copy(parts[:, b % 2, 0, 0:KH, :], qk[:, 0:KH, :])
                nc.scalar.copy(parts[0:kp, b % 2, 0, KH:NF, :], qk[0:kp, KH:NF, :]).then_inc(part0, 1)
                act.wait_ge(rest1, b + 1)
                nc.scalar.copy(parts[:, b % 2, 1, 0:KH, :], rest[:, 0:KH, :])
                nc.scalar.copy(parts[0:kp, b % 2, 1, KH:NF, :], rest[0:kp, KH:NF, :]).then_inc(part1, 1)

        if rope:
            @block.gpsimd
            def _(pool):
                pool.wait_ge(weights_in, 16 * n_weights)
                for b in range(B):
                    pool.wait_ge(qk_biased, b + 1)
                    wait_above_zero(pool, part1, b)
                    wait_above_zero(pool, part2, b)
                    nc.gpsimd.tensor_tensor(rest[:, :, :], qk[:, :, :],
                                            cos[:, :].unsqueeze(1).to_broadcast([P, NF, S]), ALU.mult).then_inc(
                        rope_cos, 1)

        @block.vector
        def _(dve):
            normalise(dve, 0)
            normalise(dve, 1)
            nc.vector.memset(vaug[:, :, :, :], 1.0).then_inc(ones_set, 1)
            dve.wait_ge(ones_set, 1)
            dve.wait_ge(weights_in, 16 * n_weights)
            for b in range(B):
                if rope:
                    dve.wait_ge(qk_biased, b + 1)
                    nc.vector.stream_shuffle(swapped[:, :, :], qk[:, :, :],
                                             [i ^ 1 for i in range(32)]).then_inc(rope_swapped, 1)
                    dve.wait_ge(rope_swapped, b + 1)
                    nc.vector.tensor_tensor(swapped[:, :, :], swapped[:, :, :],
                                            sin[:, :].unsqueeze(1).to_broadcast([P, NF, S]),
                                            ALU.mult).then_inc(rope_sin, 1)
                    dve.wait_ge(rope_sin, b + 1)
                    dve.wait_ge(rope_cos, b + 1)
                    nc.vector.tensor_tensor(qk[:, :, :], rest[:, :, :], swapped[:, :, :], ALU.add).then_inc(
                        roped, 1)
                if b + 2 < B:
                    normalise(dve, b + 2)
                dve.wait_ge(v_ready, b + 1)
                wait_above_zero(dve, v_stored, 16 * hg * b)
                for t in range(TB):
                    op = nc.vector.tensor_tensor(
                        vaug[:, t, :, 0:L.d], ps_v[:, t, 0:kf].rearrange("p (h e) -> p h e", e=L.d),
                        bv[:, :].rearrange("p (h e) -> p h e", e=L.d), ALU.add)
                op.then_inc(v_out, 1)
                dve.wait_ge(part0, b + 1)
                if not rope:
                    wait_above_zero(dve, part1, b)
                    wait_above_zero(dve, part2, b)
                now = parts[:, b % 2]
                nc.vector.tensor_tensor(rest[:, 0:KH, :], qk[:, 0:KH, :], now[:, 0, 0:KH, :], ALU.subtract)
                nc.vector.tensor_tensor(rest[0:kp, KH:NF, :], qk[0:kp, KH:NF, :], now[0:kp, 0, KH:NF, :],
                                        ALU.subtract).then_inc(rest1, 1)
                dve.wait_ge(part1, b + 1)
                wait_above_zero(dve, parts_stored[b % 2], 16 * n_parts * (b // 2))
                nc.vector.tensor_tensor(now[:, 2, 0:KH, :], rest[:, 0:KH, :], now[:, 1, 0:KH, :],
                                        ALU.subtract)
                nc.vector.tensor_tensor(now[0:kp, 2, KH:NF, :], rest[0:kp, KH:NF, :],
                                        now[0:kp, 1, KH:NF, :], ALU.subtract).then_inc(part2, 1)


def attend(nc, c, d, L):
    n = L.name
    G, U = L.groups, 4
    R = L.rows
    KW = L.kv_of_group * S
    q_parts, k_parts = [q for q, _ in L.pairs], [k for _, k in L.pairs]
    q_runs, k_climbs = runs(q_parts), climbs(k_parts)
    q_loads, kv_loads = len(q_runs), len(k_climbs) + 1
    with ExitStack() as ctx:
        def sb(name, shape, dt=F32):
            return ctx.enter_context(nc.sbuf_tensor(f"{name}_{n}", shape, dt))

        def sem(name):
            return semaphore(nc, c, f"{name}_{n}")

        q = [sb(f"q{u}", [P, HQ, S], BF16) for u in range(U)]
        k = [sb(f"k{u}", [P, KW], BF16) for u in range(U)]
        v = [sb(f"v{u}", [P, TB, L.vw]) for u in range(U)]
        probs = [sb(f"probs{t}", [P, HQ, S]) for t in range(TB)]
        row_max = sb("row_max", [P, 2, HQ * TB])
        neg_rest = sb("neg_rest", [P, 2, HQ * TB])
        neg_parts = sb("neg_parts", [P, 2, 4, HQ * TB], BF16)
        neg_turned = sb("neg_turned", [P, 2, 4 * HQ * TB], BF16)
        mixed = sb("mixed", [P, 2, S])
        ps_max = ctx.enter_context(nc.psum_tensor(f"ps_max_{n}", [P, 3, S], F32))
        ps_s = ctx.enter_context(nc.psum_tensor(f"ps_s_{n}", [P, 2, 2, S], F32))
        ps_o = ctx.enter_context(nc.psum_tensor(f"ps_o_{n}", [P, S], F32))

        q_loaded = [sem(f"q_loaded{u}") for u in range(U)]
        kv_loaded = [sem(f"kv_loaded{u}") for u in range(U)]
        fill_set = sem("fill_set")
        ones_set, pool_passed = sem("ones_set_k"), sem("pool_passed")
        max_scores, max_taken = sem("max_scores"), sem("max_taken")
        neg0, neg_r1, neg1, neg_split = sem("neg0"), sem("neg_r1"), sem("neg1"), sem("neg_split")
        turned, neg_stored, neg_loaded = sem("turned"), sem("neg_stored"), sem("neg_loaded")
        scores, exps, values_used, mixed_copied, mixed_stored = (
            sem("scores"), sem("exps"), sem("values_used"), sem("mixed_copied"), sem("mixed_stored"))
        block = ctx.enter_context(nc.Block())

        LEAD = 2

        def max_slot(y):
            return 1 if y == U * HQ * TB - 1 else y % 3

        def body_of_groups(eng, one):
            for u in range(U):
                one(eng, 0, u, u)
            with eng.Fori(1, G // U - 1) as i:
                for u in range(U):
                    one(eng, i, u, 99)
            for u in range(U):
                one(eng, G // U - 1, u, G - U + u)

        @block.sync
        def _(sp):
            sp.wait_ge(ones_set, 3 * U)

            def load_queries(i, u):
                for part, at, count in q_runs:
                    src = d[f"{n}_qd"][part, ds(i, 1), :, u * HQ:(u + 1) * HQ, :].rearrange(
                        "o e h t -> o e (h t)").to_broadcast([count, L.d, HQ * S])
                    sp.dma_start(q[u][at * L.d:(at + count) * L.d, :, :].rearrange("p h t -> p (h t)"),
                                 src).then_inc(q_loaded[u], 16)
            def negated(g, u):
                sp.wait_ge(turned, g + 1)
                sp.dma_start(d["neg_d"][u], neg_turned[:, u % 2, :]).then_inc(neg_stored, 16)
                sp.wait_ge(neg_stored, (g + 1) * 16)
                blocks = d["neg_d"][u].rearrange("(b c) (n e) -> n c b e", b=TB, n=2)
                for part in range(3):
                    c0 = part % 2 * HQ * TB
                    sp.dma_start(q[u][M_ROW + part:M_ROW + part + 1, :, :].rearrange(
                        "o h (t b e) -> o (h t) b e", b=TB, e=QUAD), blocks[part // 2, c0:c0 + HQ * TB]).then_inc(
                        neg_loaded, 16)

            def step(sp, i, u, known):
                g = i * U + u
                if known == 99 or 0 < known < G - 3:
                    sp.wait_ge(values_used, g * TB)
                    load_queries(i if u == 0 else i + 1, (u + 3) % U)
                if known < G - 1 or known == 99:
                    negated(g + 1, (u + 1) % U)

            for u in range(U):
                load_queries(0, u)
            negated(0, 0)
            body_of_groups(sp, step)

        @block.gpsimd
        def _(pool):
            for u in range(U):
                nc.gpsimd.memset(k[u][64:P, :], 0.0).then_inc(ones_set, 1)
                nc.gpsimd.memset(q[u][64:M_ROW, :, :], 0.0).then_inc(ones_set, 1)
            pool.wait_ge(ones_set, 2 * U)
            for u in range(U):
                nc.gpsimd.memset(k[u][M_ROW:M_ROW + 3, :], 1.0).then_inc(ones_set, 1)

            pool.wait_ge(ones_set, 3 * U)

            def load_keys_and_values(i, u):
                w = L.kv_of_group
                for at, count in k_climbs:
                    src = d[f"{n}_kd"][0:count, ds(i, 1), :, u * w:(u + 1) * w, :].rearrange(
                        "c o e h t -> (o c) e (h t)")
                    pool.dma_start(k[u][at * L.d:(at + count) * L.d, :], src).then_inc(kv_loaded[u], 16)
                pool.dma_start(v[u][:, :, :], d[f"{n}_vd"][ds(i * U + u, 1)].rearrange(
                    "o (t p) w -> p (o t) w", p=P)).then_inc(kv_loaded[u], 16)

            for u in range(U):
                load_keys_and_values(0, u)

            def step(pool, i, u, known):
                g = i * U + u
                if known == 99 or 0 < known < G - 3:
                    pool.wait_ge(values_used, g * TB)
                    pool.sem_inc(pool_passed, 1)
                    load_keys_and_values(i if u == 0 else i + 1, (u + 3) % U)
                if known > 1:
                    pool.wait_ge(mixed_copied, g - 1)
                    pool.wait_ge(mixed_stored, (g - 2) * 16)
                    pool.sem_inc(pool_passed, 1)
                    pool.dma_start(d[f"{n}_od"][ds((g - 2) * P, P), :], mixed[:, u % 2, :]).then_inc(mixed_stored, 16)

            body_of_groups(pool, step)
            for g in (G - 2, G - 1):
                pool.wait_ge(mixed_copied, g + 1)
                pool.wait_ge(mixed_stored, g * 16)
                pool.dma_start(d[f"{n}_od"][g * P:(g + 1) * P, :], mixed[:, g % 2, :]).then_inc(mixed_stored, 16)
            pool.wait_ge(mixed_stored, 16 * G)

        @block.vector
        def _(dve):
            def split(g, s, part, known):
                if part == 0:
                    dve.wait_ge(max_taken, (g + 1) * 16)
                    nc.vector.tensor_scalar(neg_parts[:, s, 0, :], row_max[:, s, :], -1.0, None, ALU.mult).then_inc(
                        neg0, 1)
                if part == 1:
                    dve.wait_ge(neg0, g + 1)
                    nc.vector.scalar_tensor_tensor(neg_rest[:, s, :], row_max[:, s, :], -1.0, neg_parts[:, s, 0, :],
                                                   ALU.mult, ALU.subtract).then_inc(neg_r1, 1)
                if part == 2:
                    dve.wait_ge(neg_r1, g + 1)
                    nc.vector.tensor_copy(neg_parts[:, s, 1, :], neg_rest[:, s, :]).then_inc(neg1, 1)
                if part == 3:
                    dve.wait_ge(neg1, g + 1)
                    nc.vector.tensor_tensor(neg_parts[:, s, 2, :], neg_rest[:, s, :], neg_parts[:, s, 1, :],
                                            ALU.subtract).then_inc(neg_split, 1)
                if part == 4:
                    dve.wait_ge(neg_split, g + 1)
                    if known > 1:
                        dve.wait_ge(neg_stored, (g - 1) * 16)
                    nc.vector.transpose(neg_turned[:, s, :],
                                        neg_parts[:, s, :, :].rearrange("p c n -> p (c n)")).then_inc(turned, 1)

            def step(dve, i, u, known):
                g = i * U + u
                s, first = u % 2, u * HQ * TB
                for t in range(TB):
                    for h in range(HQ):
                        x = t * HQ + h
                        dve.wait_ge(max_scores, g * 16 + x + 1)
                        width = (t + 1) * P if L.causal else S
                        nc.vector.tensor_reduce(row_max[:, s, h * TB + t:h * TB + t + 1],
                                                ps_max[:, max_slot(first + x), 0:width], AX.X, ALU.max).then_inc(
                            max_taken, 1)
                        if known > 0 and x < 5:
                            split(g - 1, 1 - s, x, known - 1)

            nc.vector.memset(neg_parts[:, :, 3, :], 0.0).then_inc(fill_set, 1)
            dve.wait_ge(fill_set, 1)
            body_of_groups(dve, step)
            for part in range(5):
                split(G - 1, 1, part, G - 1)

        @block.scalar
        def _(act):
            def copy_mixed(g, s):
                act.wait_ge(values_used, (g + 1) * TB)
                if not isinstance(g, int) or g > 1:
                    act.wait_ge(mixed_stored, (g - 1) * 16)
                nc.scalar.copy(mixed[:, s, :], ps_o[:, :]).then_inc(mixed_copied, 1)

            def step(act, i, u, known):
                g = i * U + u
                for x in range(8):
                    kt, pair = x // 2, x % 2
                    lo = kt * P if L.causal else 0
                    act.wait_ge(scores, g * 8 + x + 1)
                    if known > 0 and pair == 0:
                        act.wait_ge(values_used, g * TB + kt - 3)
                    nc.scalar.activation(probs[kt][:, 2 * pair:2 * pair + 2, lo:S], ps_s[:, pair, :, lo:S], ACT.Exp,
                                         scale=L.scale).then_inc(exps, 1)
                    if x == 1 and known > 0:
                        copy_mixed(g - 1, (u + 1) % 2)

            body_of_groups(act, step)
            copy_mixed(G - 1, (G - 1) % 2)

        @block.tensor
        def _(pe):
            def top(g, u, x):
                t, h = x // HQ, x % HQ
                y = u * HQ * TB + x
                slot = max_slot(y)
                back = {0: 4, 1: 2, 2: 4, U * HQ * TB - 1: 2}.get(y, 3)
                if not isinstance(g, int) or g * 16 + x >= 3:
                    pe.wait_ge(max_taken, g * 16 + (x + 1 - back))
                kc = h * S if L.kv_of_group > 1 else 0
                width = (t + 1) * P if L.causal else S
                op = nc.tensor.matmul(ps_max[:, slot, 0:width], q[u][0:R, h, t * P:(t + 1) * P],
                                      k[u][0:R, kc:kc + width], start=True, stop=not L.causal)
                if L.causal:
                    op = nc.tensor.matmul(ps_max[:, slot, t * P:width], c["masks"][:, 0, :], c["masks"][:, 1, :],
                                          start=False, stop=True)
                op.then_inc(max_scores, 1)

            def weigh(g, u, kt):
                pe.wait_ge(exps, g * 8 + 2 * kt + 2)
                if kt == 0 and (not isinstance(g, int) or g > 0):
                    pe.wait_ge(mixed_copied, g)
                lo = kt * P if L.causal else 0
                for h in range(HQ):
                    vc = h * QUAD if L.kv_of_group > 1 else 0
                    op = nc.tensor.matmul(ps_o[h * QUAD:(h + 1) * QUAD, lo:S], v[u][:, kt, vc:vc + QUAD],
                                          probs[kt][:, h, lo:S], start=kt == 0, stop=kt == TB - 1)
                op.then_inc(values_used, 1)

            def step(pe, i, u, known):
                g = i * U + u

                def top_ahead(x):
                    over, x = divmod(x + LEAD, HQ * TB)
                    ahead = 2 + over
                    if known != 99 and known + ahead >= G:
                        return
                    if x == 0:
                        loads = i + ((u + ahead) // U + 1)
                        pe.wait_ge(q_loaded[(u + ahead) % U], loads * (16 * q_loads))
                        pe.wait_ge(kv_loaded[(u + ahead) % U], loads * (16 * kv_loads))
                    top(g + ahead, (u + ahead) % U, x)

                for x in range(8):
                    kt, pair = x // 2, x % 2
                    lo = kt * P if L.causal else 0
                    if x == 0:
                        pe.wait_ge(neg_loaded, (g + 1) * 48)
                    for h in (2 * pair, 2 * pair + 1):
                        top_ahead(2 * x + h % 2)
                        if h % 2 == 0 and (not isinstance(g, int) or g * 8 + x >= 2):
                            pe.wait_ge(exps, g * 8 + x - 1)
                        kc = h * S if L.kv_of_group > 1 else 0
                        op = nc.tensor.matmul(ps_s[:, pair, h % 2, lo:S], k[u][0:M_ROW + 3, kc + kt * P:kc + (kt + 1) * P],
                                              q[u][0:M_ROW + 3, h, lo:S], start=True, stop=not L.causal)
                        if L.causal:
                            op = nc.tensor.matmul(ps_s[:, pair, h % 2, lo:lo + P], c["masks"][:, 0, :],
                                                  c["masks"][:, 2, :], start=False, stop=True)
                    op.then_inc(scores, 1)
                    if x == 1:
                        if known > 0:
                            weigh(g - 1, (u - 1) % U, TB - 1)
                    if x in (3, 5, 7):
                        weigh(g, u, x // 2 - 1)

            pe.wait_ge(ones_set, 3 * U)
            for u in range(3):
                pe.wait_ge(q_loaded[u], 16 * q_loads)
                pe.wait_ge(kv_loaded[u], 16 * kv_loads)
                for x in range(HQ * TB if u < 2 else LEAD):
                    top(u, u, x)
            body_of_groups(pe, step)
            weigh(G - 1, U - 1, TB - 1)


def join(nc, c, d, L):
    n = L.name
    with ExitStack() as ctx:
        def sb(name, shape, dt=F32):
            return ctx.enter_context(nc.sbuf_tensor(f"{name}_{n}", shape, dt))

        def sem(name):
            return semaphore(nc, c, f"{name}_{n}")

        wo = sb("wo_sb", [P, KH, H])
        num = sb("num", [P, 2, KH, S])
        den = sb("den", [P, 2, KH, S])
        ps_y = ctx.enter_context(nc.psum_tensor(f"ps_y_{n}", [P, 2, TB, H], F32))
        wo_in, biased = sem("wo_in"), sem("biased")
        rows_in = [sem("rows_in0"), sem("rows_in1")]
        inverted, divided, projected, added = sem("inverted"), sem("divided"), sem("projected"), sem("added")
        heads = P // L.d
        block = ctx.enter_context(nc.Block())

        @block.sync
        def _(sp):
            sp.dma_start(wo[:, :, :], d[f"{n}_wo"]).then_inc(wo_in, 16)
            od = d[f"{n}_od"].rearrange("(h r) t -> h r t", r=QUAD)
            for b in range(B):
                if b >= 2:
                    sp.wait_ge(projected, b - 1)
                for m in range(KH):
                    h0 = (b * KH + m) * heads
                    sp.dma_start(num[:, b % 2, m, :], od[h0:h0 + heads, 0:L.d, :]).then_inc(rows_in[b % 2], 16)
                    sp.dma_start(den[:, b % 2, m, :], od[h0:h0 + heads, L.d:2 * L.d, :]).then_inc(rows_in[b % 2], 16)

        @block.gpsimd
        def _(pool):
            for b in range(B):
                r = c["resid"][:, b * TB * H:(b + 1) * TB * H].rearrange("p (t f) -> p t f", f=H)
                nc.gpsimd.tensor_tensor(r, r, c["bo"][:, :].unsqueeze(1).to_broadcast([P, TB, H]),
                                        ALU.add).then_inc(biased, 1)

        @block.vector
        def _(dve):
            def add(b):
                dve.wait_ge(projected, b + 1)
                dve.wait_ge(biased, b + 1)
                r = c["resid"][:, b * TB * H:(b + 1) * TB * H]
                nc.vector.tensor_tensor(r, r, ps_y[:, b % 2, :, :].rearrange("p t f -> p (t f)"),
                                        ALU.add).then_inc(added, 1)

            for b in range(B):
                dve.wait_ge(rows_in[b % 2], 16 * 2 * KH * (b // 2 + 1))
                nc.vector.reciprocal(den[:, b % 2, :, :], den[:, b % 2, :, :]).then_inc(inverted, 1)
                dve.wait_ge(inverted, b + 1)
                nc.vector.tensor_tensor(num[:, b % 2, :, :], num[:, b % 2, :, :], den[:, b % 2, :, :],
                                        ALU.mult).then_inc(divided, 1)
                if b:
                    add(b - 1)
            add(B - 1)

        @block.tensor
        def _(pe):
            pe.wait_ge(wo_in, 16)
            for b in range(B):
                pe.wait_ge(divided, b + 1)
                if b >= 2:
                    pe.wait_ge(added, b - 1)
                for t in range(TB):
                    for m in range(KH):
                        op = nc.tensor.matmul(ps_y[:, b % 2, t, :], num[:, b % 2, m, t * P:(t + 1) * P], wo[:, m, :],
                                              start=m == 0, stop=m == KH - 1)
                op.then_inc(projected, 1)


def normalised_rows(nc, c, d, n, experts):
    shared = n == "l1"
    F = 96
    with ExitStack() as ctx:
        def sb(name, shape, dt=F32):
            return ctx.enter_context(nc.sbuf_tensor(f"{name}_{n}f", shape, dt))

        def sem(name):
            return semaphore(nc, c, f"{name}_{n}f")

        wr = sb("wr", [P, KH, experts])
        xn = sb("xn", [P, 2, TB, H])
        xnt, xnt_cut = sb("xnt", [P, 2, KH, S]), sb("xnt_cut", [P, KH, S])
        ps_t = ctx.enter_context(nc.psum_tensor(f"ps_t_{n}f", [P, KH, S], F32))
        ps_l = ctx.enter_context(nc.psum_tensor(f"ps_l_{n}f", [P, TB, experts], F32))
        weights_in, xn_ready, t_ready, xnt_ready, l_ready, l_out, low_kept = (
            sem(x) for x in ("weights_in", "xn_ready", "t_ready", "xnt_ready", "l_ready", "l_out", "low_kept"))
        rows_kept = [sem("rows_kept0"), sem("rows_kept1")]
        if shared:
            wsg, wsu, wsd = sb("wsg", [P, KH, F]), sb("wsu", [P, KH, F]), sb("wsd", [F, H])
            gate, hidden = sb("gate", [F, S]), sb("hidden", [F, S])
            ps_g = ctx.enter_context(nc.psum_tensor("ps_g_sh", [P, 2, S], F32))
            ps_y = ctx.enter_context(nc.psum_tensor("ps_y_sh", [P, TB, H], F32))
            up_ready, gated, hidden_ready, y_ready, y_added = (
                sem(x) for x in ("up_ready", "gated", "hidden_ready", "y_ready", "y_added"))
        cut_done, high_kept = sem("cut_done"), sem("high_kept")
        n_weights = 1 + 3 * shared
        block = ctx.enter_context(nc.Block())

        @block.sync
        def _(sp):
            sp.dma_start(wr[:, :, :], d[f"{n}_router"]).then_inc(weights_in, 16)
            if shared:
                sp.dma_start(wsg[:, :, :], d["l1_wsg"]).then_inc(weights_in, 16)
                sp.dma_start(wsu[:, :, :], d["l1_wsu"]).then_inc(weights_in, 16)
                sp.dma_start(wsd[:, :], d["l1_wsd"]).then_inc(weights_in, 16)
                for b in range(B):
                    sp.wait_ge(xn_ready, b + 1)
                    sp.dma_start(d["xn_d"][b * S:(b + 1) * S, :].rearrange("(t p) f -> p t f", p=P),
                                 xn[:, b % 2, :, :]).then_inc(rows_kept[b % 2], 16)
                for slot in range(2):
                    sp.wait_ge(rows_kept[slot], 16 * B // 2)

        @block.tensor
        def _(pe):
            def turn(b):
                pe.wait_ge(xn_ready, b + 1)
                wait_above_zero(pe, xnt_ready, b)
                for k in range(KH):
                    for t in range(TB):
                        op = nc.tensor.transpose(ps_t[:, k, t * P:(t + 1) * P],
                                                 xn[:, b % 2, t, k * P:(k + 1) * P], c["ident"][:, :])
                op.then_inc(t_ready, 1)

            turn(0)
            pe.wait_ge(weights_in, 16 * n_weights)
            for b in range(B):
                if b + 1 < B:
                    turn(b + 1)
                pe.wait_ge(xnt_ready, b + 1)
                if shared:
                    wait_above_zero(pe, hidden_ready, b)
                    for i, w in enumerate((wsg, wsu)):
                        for k in range(KH):
                            op = nc.tensor.matmul(ps_g[0:F, i, :], w[:, k, :], xnt[:, b % 2, k, :],
                                                  start=k == 0, stop=k == KH - 1)
                    op.then_inc(up_ready, 1)
                wait_above_zero(pe, l_out, b)
                for t in range(TB):
                    for k in range(KH):
                        op = nc.tensor.matmul(ps_l[:, t, :], xnt[:, b % 2, k, t * P:(t + 1) * P], wr[:, k, :],
                                              start=k == 0, stop=k == KH - 1)
                op.then_inc(l_ready, 1)
                if shared:
                    pe.wait_ge(hidden_ready, b + 1)
                    wait_above_zero(pe, y_added, b)
                    for t in range(TB):
                        op = nc.tensor.matmul(ps_y[:, t, :], hidden[:, t * P:(t + 1) * P], wsd[:, :],
                                              start=True, stop=True)
                    op.then_inc(y_ready, 1)

        @block.scalar
        def _(act):
            def keep_turned(b):
                act.wait_ge(t_ready, b + 1)
                wait_above_zero(act, l_ready, b - 1)
                if not shared:
                    wait_above_zero(act, low_kept, b - 1)
                nc.scalar.copy(xnt[:, b % 2, :, :], ps_t[:, :, :]).then_inc(xnt_ready, 1)

            keep_turned(0)
            for b in range(B):
                if b + 1 < B:
                    keep_turned(b + 1)
                if shared:
                    act.wait_ge(up_ready, b + 1)
                    wait_above_zero(act, hidden_ready, b)
                    nc.scalar.activation(gate[:, :], ps_g[0:F, 0, :], ACT.Silu).then_inc(gated, 1)
                else:
                    act.wait_ge(cut_done, b + 1)
                    nc.scalar.copy(c["xh"][:, :, b * S:(b + 1) * S], xnt_cut[:, :, :]).then_inc(high_kept, 1)
                act.wait_ge(l_ready, b + 1)
                nc.scalar.copy(c["logits"][:, b * (TB * experts):(b + 1) * (TB * experts)],
                               ps_l[:, :, :].rearrange("p t e -> p (t e)")).then_inc(l_out, 1)

        @block.gpsimd
        def _(pool):
            if not shared:
                for b in range(B):
                    pool.wait_ge(cut_done, b + 1)
                    nc.gpsimd.tensor_tensor(c["xl"][:, :, b * S:(b + 1) * S], xnt[:, b % 2, :, :], xnt_cut[:, :, :],
                                            ALU.subtract).then_inc(low_kept, 1)

        @block.vector
        def _(dve):
            def normalise(b):
                wait_above_zero(dve, t_ready, b - 1)
                if shared:
                    wait_above_zero(dve, rows_kept[b % 2], 16 * (b // 2))
                for t in range(TB):
                    at = b * TB + t
                    op = nc.vector.tensor_scalar(
                        xn[:, b % 2, t, :], c["resid"][:, at * H:(at + 1) * H], c["mean_var"][:, at * 2:at * 2 + 1],
                        c["rstd"][:, at:at + 1], ALU.subtract, ALU.mult)
                op.then_inc(xn_ready, 1)

            normalise(0)
            normalise(1)
            for b in range(B):
                if shared:
                    dve.wait_ge(gated, b + 1)
                    wait_above_zero(dve, y_ready, b)
                    nc.vector.tensor_tensor(hidden[:, :], gate[:, :], ps_g[0:F, 1, :], ALU.mult).then_inc(
                        hidden_ready, 1)
                else:
                    dve.wait_ge(xnt_ready, b + 1)
                    wait_above_zero(dve, high_kept, b)
                    wait_above_zero(dve, low_kept, b)
                    cut_bits(nc, xnt_cut[:, :, :], xnt[:, b % 2, :, :]).then_inc(cut_done, 1)
                if b + 2 < B:
                    normalise(b + 2)
                if shared:
                    dve.wait_ge(y_ready, b + 1)
                    r = c["resid"][:, b * (TB * H):(b + 1) * (TB * H)]
                    nc.vector.tensor_tensor(r, r, ps_y[:, :, :].rearrange("p t f -> p (t f)"),
                                            ALU.add).then_inc(y_added, 1)


def chosen_groups(nc, dve, step, gs, ge, gt, lower, keep, G, take):
    a = gs[:, :, :].unsqueeze(3).to_broadcast([P, NT, G, G])
    b = gs[:, :, :].unsqueeze(2).to_broadcast([P, NT, G, G])
    low = lower.unsqueeze(1).to_broadcast([P, NT, G, G])
    step(nc.vector.tensor_tensor(ge, b, a, ALU.is_ge))
    step(nc.vector.tensor_tensor(gt, b, a, ALU.is_gt))
    step(nc.vector.tensor_tensor(ge, ge, low, ALU.mult))
    step(nc.vector.tensor_tensor(gt, gt, ge, ALU.max))
    step(nc.vector.tensor_reduce(keep, gt, AX.X, ALU.add))
    step(nc.vector.tensor_scalar(keep, keep, float(take), NEG, ALU.is_ge, ALU.mult))


def cut_bits(nc, out, x):
    return nc.vector.tensor_scalar(out.bitcast(I32), x.bitcast(I32), HIGH_BITS, None, ALU.bitwise_and)


def dense_experts(nc, c, d):
    E, G, TOPG, K, I = 16, 4, 2, 4, 176
    FT = c["FT"]
    ER = 32
    with ExitStack() as outer:
        def sbo(name, shape, dt=F32):
            return outer.enter_context(nc.sbuf_tensor(name, shape, dt))

        c["xh"], c["xl"] = sbo("xh", [P, KH, T], F32R), sbo("xl", [P, KH, T], F32R)
        c["logits"] = sbo("logits0", [P, NT * E])
        normalised_rows(nc, c, d, "l0", E)
        weights_t = sbo("weights_t", [3 * ER, T], BF16)

        with ExitStack() as ctx:
            def sb(name, shape, dt=F32):
                return ctx.enter_context(nc.sbuf_tensor(f"{name}_r0", shape, dt))

            logit = c["logits"][:, :].rearrange("p (t e) -> p t e", e=E)
            key, sig = sb("key", [P, NT, E]), sb("sig", [P, NT, E])
            gs, keep = sb("gs", [P, NT, G]), sb("keep", [P, NT, G])
            ge, gt = sb("ge", [P, NT, G, G]), sb("gt", [P, NT, G, G])
            best, place = sb("best", [P, NT, 8]), sb("place", [P, NT, 8], U32)
            placef = sb("placef", [P, NT, 8])
            hot, mask = sb("hot", [P, K, NT, E]), sb("mask", [P, NT, E])
            total = sb("total", [P, NT, 1])
            weight = sb("weight", [P, NT, ER])
            rest = sb("rest", [P, NT, ER])
            wparts = sb("wparts", [P, NT, 3, ER], BF16)
            low, numbers = sb("low", [P, G, G]), sb("numbers", [P, E])
            ps_w = ctx.enter_context(nc.psum_tensor("ps_w", [3 * ER, T], F32))
            tables_in, sigmoid_done, dve_step, split_done, turned, top_done, index_done = (
                semaphore(nc, c, x + "_r0") for x in (
                    "tables_in", "sigmoid_done", "dve_step", "split_done", "turned", "top_done", "index_done"))
            block = ctx.enter_context(nc.Block())

            @block.sync
            def _(sp):
                sp.dma_start(low[:, :, :], d["lower4"]).then_inc(tables_in, 16)
                sp.dma_start(numbers[:, :], d["numbers"][:, 0:E]).then_inc(tables_in, 16)

            @block.scalar
            def _(act):
                nc.scalar.activation(sig[:, :, :], logit, ACT.Sigmoid).then_inc(sigmoid_done, 1)
                act.wait_ge(turned, 1)
                nc.scalar.copy(weights_t[:, :], ps_w[:, :])

            @block.vector
            def _(dve):
                count = [0]

                def step(op):
                    count[0] += 1
                    op.then_inc(dve_step, 1)
                    dve.wait_ge(dve_step, count[0])

                dve.wait_ge(tables_in, 32)
                step(nc.vector.tensor_scalar(key[:, :, :], logit, 17.0, None, ALU.min))
                step(nc.vector.tensor_reduce(gs[:, :, :], key[:, :, :].rearrange("p t (g e) -> p t g e", g=G), AX.X,
                                             ALU.max))
                chosen_groups(nc, dve, step, gs, ge[:, :, :, :], gt[:, :, :, :], low[:, :, :], keep[:, :, :], G, TOPG)
                step(nc.vector.tensor_tensor(key[:, :, :].rearrange("p t (g e) -> p t g e", g=G),
                                             key[:, :, :].rearrange("p t (g e) -> p t g e", g=G),
                                             keep[:, :, :].unsqueeze(3).to_broadcast([P, NT, G, E // G]), ALU.add))
                keys = key[:, :, :].rearrange("p t e -> p (t e)")
                bests = best[:, :, :].rearrange("p t e -> p (t e)")
                places = place[:, :, :].rearrange("p t e -> p (t e)")
                for t in range(NT):
                    nc.vector.max(bests[:, t * 8:t * 8 + 8], keys[:, t * E:(t + 1) * E]).then_inc(top_done, 1)
                dve.wait_ge(top_done, NT)
                for t in range(NT):
                    nc.vector.max_index(places[:, t * 8:t * 8 + 8], bests[:, t * 8:t * 8 + 8],
                                        keys[:, t * E:(t + 1) * E]).then_inc(index_done, 1)
                dve.wait_ge(index_done, NT)
                step(nc.vector.tensor_copy(placef[:, :, :], place[:, :, :]))
                for k in range(K):
                    op = nc.vector.tensor_tensor(hot[:, k, :, :], numbers[:, :].unsqueeze(1).to_broadcast([P, NT, E]),
                                                 placef[:, :, k:k + 1].to_broadcast([P, NT, E]), ALU.is_equal)
                step(op)
                step(nc.vector.tensor_tensor(hot[:, 0:2], hot[:, 0:2], hot[:, 2:4], ALU.add))
                step(nc.vector.tensor_tensor(mask[:, :, :], hot[:, 0], hot[:, 1], ALU.add))
                dve.wait_ge(sigmoid_done, 1)
                step(nc.vector.tensor_tensor(sig[:, :, :], sig[:, :, :], mask[:, :, :], ALU.mult))
                step(nc.vector.tensor_reduce(total[:, :, 0], sig[:, :, :], AX.X, ALU.add))
                step(nc.vector.reciprocal(total[:, :, :], total[:, :, :]))
                step(nc.vector.memset(weight[:, :, :], 0.0))
                step(nc.vector.tensor_tensor(weight[:, :, 0:E], sig[:, :, :],
                                             total[:, :, :].to_broadcast([P, NT, E]), ALU.mult))
                step(nc.vector.memset(weight[:, :, E:E + 1], 1.0))
                step(nc.vector.tensor_copy(wparts[:, :, 0, :], weight[:, :, :]))
                step(nc.vector.tensor_tensor(rest[:, :, :], weight[:, :, :], wparts[:, :, 0, :], ALU.subtract))
                step(nc.vector.tensor_copy(wparts[:, :, 1, :], rest[:, :, :]))
                nc.vector.tensor_tensor(wparts[:, :, 2, :], rest[:, :, :], wparts[:, :, 1, :],
                                        ALU.subtract).then_inc(split_done, 1)

            @block.tensor
            def _(pe):
                pe.wait_ge(split_done, 1)
                for t in range(NT):
                    op = nc.tensor.matmul(ps_w[:, t * P:(t + 1) * P], wparts[:, t, :, :].rearrange("p c e -> p (c e)"),
                                          c["masks"][:, 0, :], start=True, stop=True)
                op.then_inc(turned, 1)

        with ExitStack() as ctx:
            def sb(name, shape, dt=F32):
                return ctx.enter_context(nc.sbuf_tensor(f"{name}_e0", shape, dt))

            def sem(name):
                return semaphore(nc, c, f"{name}_e0")

            NW = 5
            FW = FT // NW
            STEPS = B * FW
            parts = ("w1", "w3", "w2")
            w_raw = {part: sb(f"{part}_raw", [P, FW * H]) for part in parts}
            w_cut = {part: sb(f"{part}_cut", [P, FW * H]) for part in parts}
            w_low = {part: sb(f"{part}_low", [P, 2, FW * H], F32R) for part in parts}
            w_high = {part: sb(f"{part}_high", [P, 2, FW * H], F32R) for part in parts}
            spread = sb("spread", [3 * ER, FT * P], BF16)
            spread_f = sb("spread_f", [3 * ER, P * FW])
            gate, product, hidden = sb("gate", [P, 2, S]), sb("product", [P, 2, S]), sb("hidden", [P, 2, S])
            hidden_cut = sb("hidden_cut", [P, 2, S])
            hidden_high, hidden_low = sb("hidden_high", [P, 2, S], F32R), sb("hidden_low", [P, 2, S], F32R)
            zero = sb("zero", [P, 6 * H])
            ps_g = ctx.enter_context(nc.psum_tensor("ps_g_e0", [P, 2, S], F32))
            ps_u = ctx.enter_context(nc.psum_tensor("ps_u_e0", [P, 2, S], F32))
            ps_w = ctx.enter_context(nc.psum_tensor("ps_w_e0", [P, 2, S], F32))
            ps_y = ctx.enter_context(nc.psum_tensor("ps_y_e0", [P, TB, H], F32))
            w_in, cut_done, high_ready, low_ready, sp_passed = (
                sem("w_in"), sem("cut_done"), sem("high_ready"), sem("low_ready"), sem("sp_passed"))
            spread_in, spread_cast, zero_set, zeros_out = (
                sem("spread_in"), sem("spread_cast"), sem("zero_set"), sem("zeros_out"))
            up_ready, gated, multiplied, weighted, hidden_cut_done, hidden_high_done, hidden_low_done = (
                sem(x) for x in ("up_ready", "gated", "multiplied", "weighted", "hidden_cut_done",
                                 "hidden_high_done", "hidden_low_done"))
            down_done, added = sem("down_done"), sem("added")
            FREE = 2
            FREE_Y = 1
            CUT_AT = (6, 11, 16)
            block = ctx.enter_context(nc.Block())

            def over_groups(eng, group):
                with eng.Fori(0, NW // 2) as i:
                    group(i * 2, 0, False)
                    group(i * 2 + 1, 1, False)
                group(NW - 1, 0, True)

            @block.sync
            def _(sp):
                def load(g):
                    for part in parts:
                        sp.dma_start(w_raw[part][:, :], d[f"l0_{part}"][:, ds(g * (FW * H), FW * H)]).then_inc(w_in, 16)

                load(0)
                sp.wait_ge(zero_set, 1)
                for t in range(NT):
                    sp.dma_start(d["y6_d"][t * P * 6:(t + 1) * P * 6, :].rearrange("(p k) f -> p (k f)", k=6),
                                 zero[:, :]).then_inc(zeros_out, 16)

                def group(g, s, last):
                    if not last:
                        sp.wait_ge(low_ready, (g + 1) * 3)
                        sp.sem_inc(sp_passed, 1)
                        load(g + 1)

                over_groups(sp, group)
                sp.wait_ge(zeros_out, 16 * NT)

            @block.gpsimd
            def _(pool):
                nc.gpsimd.memset(zero[:, :], 0.0).then_inc(zero_set, 1)
                for g in range(NW):
                    if g:
                        pool.wait_ge(spread_cast, g)
                    pool.dma_start(spread_f[:, :], d["spread"][:, g * FW * P:(g + 1) * FW * P]).then_inc(spread_in, 16)
                    pool.wait_ge(spread_in, 16 * (g + 1))
                    nc.gpsimd.tensor_copy(spread[:, g * FW * P:(g + 1) * FW * P], spread_f[:, :]).then_inc(
                        spread_cast, 1)
                    for n, part in enumerate(parts):
                        pool.wait_ge(cut_done, 3 * g + n + 1)
                        nc.gpsimd.tensor_tensor(w_low[part][:, g % 2, :], w_raw[part][:, :], w_cut[part][:, :],
                                                ALU.subtract).then_inc(low_ready, 1)

            @block.tensor
            def _(pe):
                pe.sem_inc(down_done, FREE)

                def up(g, s, n):
                    cc, f, p = n // FW, n % FW, n % 2
                    rows = slice(cc * S, (cc + 1) * S)
                    if n == 0:
                        pe.wait_ge(low_ready, (g + 1) * 3)
                        pe.wait_ge(high_ready, (g + 1) * 3)
                        pe.wait_ge(spread_cast, g + 1)
                    pe.wait_ge(weighted, g * STEPS + (n + 1))
                    for ps, part in ((ps_g, "w1"), (ps_u, "w3")):
                        for k in range(KH):
                            col = slice(f * H + k * P, f * H + (k + 1) * P)
                            high, low = w_high[part][:, s, col], w_low[part][:, s, col]
                            for m, (w, x) in enumerate(((high, c["xh"]), (high, c["xl"]), (low, c["xh"]))):
                                nc.tensor.matmul(ps[:, p, :], w, x[:, k, rows], start=k == m == 0,
                                                 stop=k == KH - 1 and m == 2)
                    nc.tensor.matmul(ps_w[:, p, :], spread[:, ds(g * (FW * P) + f * P, P)],
                                     weights_t[:, rows], start=True, stop=True).then_inc(up_ready, 1)

                def down(g, s, n):
                    f, p = n % FW, n % 2
                    pe.wait_ge(hidden_high_done, g * STEPS + (n + 1))
                    pe.wait_ge(hidden_low_done, g * STEPS + (n + 1))
                    if f == 0:
                        pe.wait_ge(added, g * B + (n // FW + FREE_Y))
                    for t in range(TB):
                        tok = slice(t * P, (t + 1) * P)
                        high, low = hidden_high[:, p, tok], hidden_low[:, p, tok]
                        for m, (h, w) in enumerate(((high, w_high), (high, w_low), (low, w_high))):
                            op = nc.tensor.matmul(ps_y[:, t, :], h, w["w2"][:, s, f * H:(f + 1) * H],
                                                  start=f == m == t % 2 == 0, stop=f == FW - 1 and m == 2,
                                                  skip_group_check=True)
                    op.then_inc(down_done, 1)

                def group(g, s, last):
                    for n in range(STEPS):
                        if n + 2 < STEPS:
                            up(g, s, n + 2)
                        elif not last:
                            up(g + 1, 1 - s, n + 2 - STEPS)
                        down(g, s, n)

                up(0, 0, 0)
                up(0, 0, 1)
                over_groups(pe, group)

            @block.scalar
            def _(act):
                def group(g, s, last):
                    for n in range(STEPS):
                        act.wait_ge(up_ready, g * STEPS + (n + 1))
                        act.wait_ge(multiplied, g * STEPS + (n + 1))
                        nc.scalar.activation(gate[:, n % 2, :], ps_g[:, n % 2, :], ACT.Silu).then_inc(gated, 1)
                        act.wait_ge(hidden_cut_done, g * STEPS + (n + 1))
                        act.wait_ge(down_done, g * STEPS + (n + 1))
                        nc.scalar.copy(hidden_high[:, n % 2, :], hidden_cut[:, n % 2, :]).then_inc(hidden_high_done, 1)
                        if n - 1 in CUT_AT and not last:
                            high(g + 1, 1 - s, CUT_AT.index(n - 1))

                def high(g, s, part):
                    act.wait_ge(cut_done, g * 3 + (part + 1))
                    nc.scalar.copy(w_high[parts[part]][:, s, :], w_cut[parts[part]][:, :]).then_inc(high_ready, 1)

                for part in range(3):
                    high(0, 0, part)
                over_groups(act, group)

            @block.vector
            def _(dve):
                dve.sem_inc(multiplied, FREE)
                dve.sem_inc(weighted, FREE)
                dve.sem_inc(added, FREE_Y)

                def cut(g, s, part):
                    name = parts[part]
                    if part == 0:
                        dve.wait_ge(w_in, (g + 1) * 48)
                    if not (isinstance(g, int) and g == 0):
                        dve.wait_ge(high_ready, g * 3)
                    cut_bits(nc, w_cut[name][:, :], w_raw[name][:, :]).then_inc(cut_done, 1)

                def hide(g, n):
                    p, done = n % 2, g * STEPS + (n + 1)
                    dve.wait_ge(gated, done)
                    nc.vector.tensor_tensor(product[:, p, :], gate[:, p, :], ps_u[:, p, :], ALU.mult).then_inc(
                        multiplied, 1)
                    dve.wait_ge(multiplied, g * STEPS + (n + 1 + FREE))
                    nc.vector.tensor_tensor(hidden[:, p, :], product[:, p, :], ps_w[:, p, :], ALU.mult).then_inc(
                        weighted, 1)
                    dve.wait_ge(weighted, g * STEPS + (n + 1 + FREE))
                    dve.wait_ge(down_done, done)
                    cut_bits(nc, hidden_cut[:, p, :], hidden[:, p, :]).then_inc(hidden_cut_done, 1)
                    dve.wait_ge(hidden_cut_done, done)
                    nc.vector.tensor_tensor(hidden_low[:, p, :], hidden[:, p, :], hidden_cut[:, p, :],
                                            ALU.subtract).then_inc(hidden_low_done, 1)

                def group(g, s, last):
                    for n in range(STEPS):
                        cc, f = n // FW, n % FW
                        if n + 1 < STEPS:
                            hide(g, n + 1)
                        elif not last:
                            hide(g + 1, 0)
                        if f == FW - 1:
                            dve.wait_ge(down_done, g * STEPS + (n + 1 + FREE))
                            r = c["resid"][:, cc * TB * H:(cc + 1) * TB * H]
                            nc.vector.tensor_tensor(r, r, ps_y[:, :, :].rearrange("p t f -> p (t f)"),
                                                    ALU.add).then_inc(added, 1)
                        if n in CUT_AT and not last:
                            cut(g + 1, 1 - s, CUT_AT.index(n))

                for part in range(3):
                    cut(0, 0, part)
                hide(0, 0)
                over_groups(dve, group)


def sparse_experts(nc, c, d):
    E, G, TOPG, K, F = 64, 8, 4, 6, 96
    CAP, SLOTS = 2 * (256 * K // E), 64
    PAIRS = E // 2
    SCALE = 2.5
    with ExitStack() as outer:
        def sbo(name, shape, dt=F32):
            return outer.enter_context(nc.sbuf_tensor(name, shape, dt))

        c["logits"] = sbo("logits1", [P, NT * E])
        normalised_rows(nc, c, d, "l1", E)
        gather_at = sbo("gather_at", [P, PAIRS], I32)
        scatter_at = sbo("scatter_at", [P, PAIRS], I32)
        wk = sbo("wk", [P, NT, K])

        with ExitStack() as ctx:
            def sb(name, shape, dt=F32):
                return ctx.enter_context(nc.sbuf_tensor(f"{name}_r1", shape, dt))

            logit = c["logits"][:, :].rearrange("p (t e) -> p t e", e=E)
            bias, numbers = sb("bias", [P, E]), sb("numbers", [P, E])
            low, pnum, tnum = sb("low", [P, G, G]), sb("pnum", [P, 1]), sb("tnum", [P, NT])
            sig, tanh, key = sb("sig", [P, NT, E]), sb("tanh", [P, NT, E]), sb("key", [P, NT, E])
            work = sb("work", [P, NT, E])
            gs, keep, second = sb("gs", [P, NT, G]), sb("keep", [P, NT, G]), sb("second", [P, NT, G])
            ge, gt = sb("ge", [P, NT, G, G]), sb("gt", [P, NT, G, G])
            best, place = sb("best", [P, NT, 8]), sb("place", [P, NT, 8], U32)
            placef = sb("placef", [P, NT, 8])
            hot = sb("hot", [P, K, NT, E], BF16)
            mask = sb("mask", [P, NT, E], BF16)
            before = sb("before", [P, NT, E], BF16)
            seat = sb("seat", [P, NT, E])
            total, ck = sb("total", [P, NT, 1]), sb("ck", [P, NT, 1])
            values = sb("values", [P, 2, NT, 3, E], BF16)
            seats = sb("seats", [P, 2, NT, SLOTS], BF16)
            table = sb("table", [P, 3, E])
            ps_p = ctx.enter_context(nc.psum_tensor("ps_p", [P, NT, E], F32))
            ps_s = ctx.enter_context(nc.psum_tensor("ps_s_r1", [P, 512], F32))
            tables_in, scores_done, dve_step, top_done, index_done, before_done, places_done, lists_ready, used = (
                semaphore(nc, c, x + "_r1") for x in (
                    "tables_in", "scores_done", "dve_step", "top_done", "index_done", "before_done", "places_done",
                    "lists_ready", "used"))
            block = ctx.enter_context(nc.Block())

            @block.sync
            def _(sp):
                sp.dma_start(low[:, :, :], d["lower8"]).then_inc(tables_in, 16)
                sp.dma_start(numbers[:, :], d["numbers"]).then_inc(tables_in, 16)
                sp.dma_start(pnum[:, :], d["pnum"]).then_inc(tables_in, 16)
                sp.dma_start(tnum[:, :], d["numbers"][:, 0:NT]).then_inc(tables_in, 16)
                sp.dma_start(bias[:, :], d["l1_bias"].rearrange("(a n) -> a n", a=1).to_broadcast([P, E])).then_inc(
                    tables_in, 16)

            @block.scalar
            def _(act):
                nc.scalar.activation(sig[:, :, :], logit, ACT.Sigmoid).then_inc(scores_done, 1)
                nc.scalar.activation(tanh[:, :, :], logit, ACT.Tanh, scale=0.5).then_inc(scores_done, 1)

            @block.vector
            def _(dve):
                count = [0]

                def step(op):
                    count[0] += 1
                    op.then_inc(dve_step, 1)
                    dve.wait_ge(dve_step, count[0])

                tt, tsc = nc.vector.tensor_tensor, nc.vector.tensor_scalar
                all_ = (slice(None),) * 3
                dve.wait_ge(tables_in, 16 * 5)
                dve.wait_ge(scores_done, 2)
                step(tsc(tanh[all_], tanh[all_], 0.5, 0.5, ALU.mult, ALU.add))
                step(tsc(work[all_], logit, -2.0, None, ALU.is_gt))
                step(tt(tanh[all_], tanh[all_], work[all_], ALU.mult))
                step(tsc(work[all_], logit, -2.0, None, ALU.is_le))
                step(tt(work[all_], work[all_], sig[all_], ALU.mult))
                step(tt(key[all_], tanh[all_], work[all_], ALU.add))
                step(nc.vector.tensor_copy(sig[all_], key[all_]))
                step(tt(key[all_], key[all_], bias[:, :].unsqueeze(1).to_broadcast([P, NT, E]), ALU.add))

                def grouped(x):
                    return x[all_].rearrange("p t (g e) -> p t g e", g=G)

                def spread(x):
                    return x[all_].unsqueeze(3).to_broadcast([P, NT, G, E // G])

                step(nc.vector.tensor_reduce(gs[all_], grouped(key), AX.X, ALU.max))
                step(tt(grouped(work), grouped(key), spread(gs), ALU.is_equal))
                step(nc.vector.tensor_reduce(keep[all_], grouped(work), AX.X, ALU.add))
                step(tsc(work[all_], work[all_], NEG, None, ALU.mult))
                step(tt(work[all_], work[all_], key[all_], ALU.add))
                step(nc.vector.tensor_reduce(second[all_], grouped(work), AX.X, ALU.max))
                step(tsc(keep[all_], keep[all_], 2.0, NEG, ALU.is_lt, ALU.mult))
                step(tt(keep[all_], keep[all_], gs[all_], ALU.add))
                step(tt(second[all_], second[all_], keep[all_], ALU.max))
                step(tt(gs[all_], gs[all_], second[all_], ALU.add))
                chosen_groups(nc, dve, step, gs, ge[:, :, :, :], gt[:, :, :, :], low[all_], keep[all_], G, TOPG)
                step(tt(grouped(key), grouped(key), spread(keep), ALU.add))
                keys = key[all_].rearrange("p t e -> p (t e)")
                bests = best[all_].rearrange("p t e -> p (t e)")
                places = place[all_].rearrange("p t e -> p (t e)")
                for t in range(NT):
                    nc.vector.max(bests[:, t * 8:t * 8 + 8], keys[:, t * E:(t + 1) * E]).then_inc(top_done, 1)
                dve.wait_ge(top_done, NT)
                for t in range(NT):
                    nc.vector.max_index(places[:, t * 8:t * 8 + 8], bests[:, t * 8:t * 8 + 8],
                                        keys[:, t * E:(t + 1) * E]).then_inc(index_done, 1)
                dve.wait_ge(index_done, NT)
                step(nc.vector.tensor_copy(placef[all_], place[all_]))
                for k in range(K):
                    op = tt(hot[:, k, :, :], numbers[:, :].unsqueeze(1).to_broadcast([P, NT, E]),
                            placef[:, :, k:k + 1].to_broadcast([P, NT, E]), ALU.is_equal)
                step(op)
                step(tt(hot_a := work[all_], hot[:, 0], hot[:, 1], ALU.add))
                for k in range(2, K - 1):
                    step(tt(hot_a, hot_a, hot[:, k], ALU.add))
                step(tt(mask[all_], hot_a, hot[:, K - 1], ALU.add))
                step(nc.vector.memset(before[:, 0, :], 0.0))
                for t in range(1, NT):
                    step(tt(before[:, t, :], before[:, t - 1, :], mask[:, t - 1, :], ALU.add))
                nc.vector.tensor_copy(work[all_], mask[all_]).then_inc(before_done, 1)
                dve.wait_ge(before_done, 1)
                step(tt(sig[all_], sig[all_], mask[all_], ALU.mult))
                step(nc.vector.tensor_reduce(total[:, :, 0], sig[all_], AX.X, ALU.add))
                step(nc.vector.reciprocal(total[all_], total[all_]))
                step(tt(sig[all_], sig[all_], total[all_].to_broadcast([P, NT, E]), ALU.mult))
                step(tsc(sig[all_], sig[all_], SCALE, None, ALU.mult))
                dve.wait_ge(places_done, 1)
                step(tsc(work[all_], ps_p[all_], float(CAP), None, ALU.is_lt))
                step(tt(sig[all_], sig[all_], work[all_], ALU.mult))
                step(tsc(seat[all_], ps_p[all_], float(CAP), None, ALU.min))
                step(tsc(work[all_], ps_p[all_], float(CAP), 16.0, ALU.is_ge, ALU.mult))
                step(tt(seat[all_], seat[all_], work[all_], ALU.add))
                for k in range(K):
                    s = k % 2
                    if k >= 2:
                        dve.wait_ge(used, k - 1)
                    step(tt(work[all_], seat[all_], hot[:, k], ALU.mult))
                    step(nc.vector.tensor_reduce(ck[:, :, 0], work[all_], AX.X, ALU.add))
                    step(tt(seats[:, s], numbers[:, :].unsqueeze(1).to_broadcast([P, NT, SLOTS]),
                            ck[all_].to_broadcast([P, NT, SLOTS]), ALU.is_equal))
                    nc.vector.tensor_scalar(values[:, s, :, 0, :], hot[:, k], pnum[:, 0:1], None, ALU.mult)
                    tt(values[:, s, :, 1, :], hot[:, k], tnum[:, :].unsqueeze(2).to_broadcast([P, NT, E]), ALU.mult)
                    tsc(values[:, s, :, 2, :], hot[:, k], float(k + 1), None, ALU.mult).then_inc(lists_ready, 1)
                for k in range(K):
                    step(tt(work[all_], sig[all_], hot[:, k], ALU.mult))
                    step(nc.vector.tensor_reduce(wk[:, :, k], work[all_], AX.X, ALU.add))
                dve.wait_ge(used, K)
                step(nc.vector.tensor_copy(table[all_], ps_s[:, 0:3 * E].rearrange("p (c e) -> p c e", c=3)))
                step(nc.vector.scalar_tensor_tensor(table[:, 1], table[:, 1], float(P), table[:, 0], ALU.mult, ALU.add))
                step(nc.vector.scalar_tensor_tensor(table[:, 0], table[:, 1], float(K), table[:, 2], ALU.mult, ALU.add))
                step(tsc(table[:, 2], table[:, 2], 0.5, 65536.0, ALU.is_lt, ALU.mult))
                step(nc.vector.scalar_tensor_tensor(table[:, 0], table[:, 0], -1.0, table[:, 2], ALU.add, ALU.add))
                step(tsc(table[:, 0], table[:, 0], 0.0, None, ALU.max))
                for half in range(2):
                    rows = slice(half * SLOTS, (half + 1) * SLOTS)
                    for dst, i in ((gather_at, 1), (scatter_at, 0)):
                        src = table[rows, i, :].rearrange("p (n h) -> p n h", h=2)[:, :, half]
                        step(nc.vector.tensor_copy(dst[rows, :], src))

            @block.tensor
            def _(pe):
                pe.wait_ge(before_done, 1)
                for t in range(NT):
                    nc.tensor.matmul(ps_p[:, t, :], c["masks"][:, 3, :], mask[:, t, :], start=True, stop=False)
                    op = nc.tensor.matmul(ps_p[:, t, :], c["masks"][:, 4, :], before[:, t, :], start=False, stop=True)
                op.then_inc(places_done, 1)
                for k in range(K):
                    pe.wait_ge(lists_ready, k + 1)
                    for t in range(NT):
                        for half in range(2):
                            op = nc.tensor.matmul(ps_s[half * SLOTS:(half + 1) * SLOTS, 0:3 * E], seats[:, k % 2, t, :],
                                                  values[:, k % 2, t, :, :].rearrange("p c e -> p (c e)"),
                                                  start=k == 0 and t == 0, stop=k == K - 1 and t == NT - 1)
                    op.then_inc(used, 1)

        expert_pairs(nc, c, d, gather_at, scatter_at)
        combine(nc, c, d, wk)


def expert_pairs(nc, c, d, gather_at, scatter_at):
    PAIRS, SLOTS, F, U = 32, 64, 96, 8
    with ExitStack() as ctx:
        def sb(name, shape, dt=F32):
            return ctx.enter_context(nc.sbuf_tensor(f"{name}_p1", shape, dt))

        def sem(name):
            return semaphore(nc, c, f"{name}_p1")

        w_up = [sb(f"w_up{u}", [P, 2, KH, 2 * F]) for u in range(U)]
        w_down = [sb(f"w_down{u}", [F, 2, H]) for u in range(U)]
        at = [sb(f"at{u}", [P, 1], I32) for u in range(U)]
        to = [sb(f"to{u}", [P, 1], I32) for u in range(U)]
        rows = [sb(f"rows{u}", [P, H]) for u in range(U)]
        rows_t = sb("rows_t", [P, 2, KH, P])
        gate, hidden, hidden_t = sb("gate", [P, 2, F]), sb("hidden", [P, 2, F]), sb("hidden_t", [F, 2, P])
        result = [sb(f"result{u}", [P, H]) for u in range(U)]
        ps_x = [ctx.enter_context(nc.psum_tensor(f"ps_x{i}", [P, KH, P], F32)) for i in range(2)]
        ps_h = [ctx.enter_context(nc.psum_tensor(f"ps_h{i}", [P, 2 * F], F32)) for i in range(2)]
        ps_t = [ctx.enter_context(nc.psum_tensor(f"ps_ht{i}", [F, P], F32)) for i in range(2)]
        ps_o = [ctx.enter_context(nc.psum_tensor(f"ps_o{i}", [P, H], F32)) for i in range(2)]
        w_in = [sem(f"w_in{u}") for u in range(U)]
        gathered = [sem(f"gathered{u}") for u in range(U)]
        scattered = [sem(f"scattered{u}") for u in range(U)]
        at_ready, to_ready, pool_passed = sem("at_ready"), sem("to_ready"), sem("pool_passed")
        x_turned, x_copied, up_done, gated, hidden_done, h_turned, h_copied, down_done, result_done = (
            sem(x) for x in ("x_turned", "x_copied", "up_done", "gated", "hidden_done", "h_turned", "h_copied",
                             "down_done", "result_done"))
        block = ctx.enter_context(nc.Block())

        def steps(eng, one, lag):
            for u in range(U):
                for j in range(lag + 1):
                    if u - j >= 0:
                        one(0, u - j, j, u - j)
            with eng.Fori(1, PAIRS // U) as i:
                for u in range(U):
                    for j in range(lag + 1):
                        one(i if u >= j else i - 1, (u - j) % U, j, 99)
            for u in range(lag):
                for j in range(u + 1, lag + 1):
                    one(PAIRS // U - 1, U + u - j, j, 99)

        @block.sync
        def _(sp):
            def load(i, u):
                sp.dma_start(w_up[u][:, :, :, :], d["l1_w_up"][ds(i * U + u, 1)].rearrange(
                    "o p a k f -> (o p) a k f")).then_inc(w_in[u], 16)
                sp.dma_start(w_down[u][:, :, :], d["l1_w_down"][ds(i * U + u, 1)].rearrange(
                    "o p a f -> (o p) a f")).then_inc(w_in[u], 16)

            for u in range(U):
                load(0, u)
            with sp.Fori(1, PAIRS // U) as i:
                for u in range(U):
                    sp.wait_ge(down_done, i * U + (u - (U - 1)))
                    load(i, u)

        @block.gpsimd
        def _(pool):
            def one(i, u, j, known):
                n = i * U + u
                if j == 0:
                    if known >= U:
                        pool.wait_ge(x_turned, n - (U - 1))
                    nc.gpsimd.tensor_copy(at[u][:, :], gather_at[:, ds(n, 1)]).then_inc(at_ready, 1)
                    pool.wait_ge(at_ready, n + 1)
                    pool.sem_inc(pool_passed, 1)
                    pool.indirect_dma_start(rows[u][:, :], None, d["xn_d"],
                                            bass.IndirectOffsetOnAxis(ap=at[u][:, 0:1], axis=0)).then_inc(
                        gathered[u], 16)
                if j == U:
                    pool.wait_ge(result_done, n + 1)
                    if known >= U:
                        pool.wait_ge(scattered[u], i * 16)
                    nc.gpsimd.tensor_copy(to[u][:, :], scatter_at[:, ds(n, 1)]).then_inc(to_ready, 1)
                    pool.wait_ge(to_ready, n + 1)
                    pool.sem_inc(pool_passed, 1)
                    pool.indirect_dma_start(d["y6_d"], bass.IndirectOffsetOnAxis(ap=to[u][:, 0:1], axis=0),
                                            result[u][:, :], None, bounds_check=T * 6 - 1,
                                            oob_is_err=False).then_inc(scattered[u], 16)

            def both(eng):
                for u in range(U):
                    one(0, u, 0, u)
                with eng.Fori(1, PAIRS // U) as i:
                    for u in range(U):
                        one(i, u, 0, 99)
                        one(i - 1, u, U, 99)
                for u in range(U):
                    one(PAIRS // U - 1, u, U, 99)

            both(pool)
            for u in range(U):
                pool.wait_ge(scattered[u], 16 * (PAIRS // U))

        @block.tensor
        def _(pe):
            def one(i, u, j, known):
                n, s = i * U + u, u % 2
                if j == 0:
                    pe.wait_ge(gathered[u], (i + 1) * 16)
                    if known >= 2:
                        pe.wait_ge(x_copied, n - 1)
                    for k in range(KH):
                        op = nc.tensor.transpose(ps_x[s][:, k, :], rows[u][:, k * P:(k + 1) * P], c["ident"][:, :])
                    op.then_inc(x_turned, 1)
                if j == 1:
                    pe.wait_ge(x_copied, n + 1)
                    pe.wait_ge(w_in[u], (i + 1) * 32)
                    if known >= 2:
                        pe.wait_ge(hidden_done, n - 1)
                    for k in range(KH):
                        for a in range(2):
                            op = nc.tensor.matmul(ps_h[s][a * SLOTS:(a + 1) * SLOTS, :],
                                                  rows_t[:, s, k, a * SLOTS:(a + 1) * SLOTS], w_up[u][:, a, k, :],
                                                  start=k == 0, stop=k == KH - 1)
                    op.then_inc(up_done, 1)
                if j == 2:
                    pe.wait_ge(hidden_done, n + 1)
                    if known >= 2:
                        pe.wait_ge(h_copied, n - 1)
                    nc.tensor.transpose(ps_t[s][:, :], hidden[:, s, :], c["ident"][:, :]).then_inc(h_turned, 1)
                if j == 3:
                    pe.wait_ge(h_copied, n + 1)
                    if known >= 2:
                        pe.wait_ge(result_done, n - 1)
                    for a in range(2):
                        op = nc.tensor.matmul(ps_o[s][a * SLOTS:(a + 1) * SLOTS, :],
                                              hidden_t[:, s, a * SLOTS:(a + 1) * SLOTS], w_down[u][:, a, :],
                                              start=True, stop=True)
                    op.then_inc(down_done, 1)

            steps(pe, one, 3)

        @block.scalar
        def _(act):
            def one(i, u, j, known):
                n, s = i * U + u, u % 2
                if j == 0:
                    act.wait_ge(x_turned, n + 1)
                    if known >= 2:
                        act.wait_ge(up_done, n - 1)
                    nc.scalar.copy(rows_t[:, s, :, :], ps_x[s][:, :, :]).then_inc(x_copied, 1)
                if j == 1:
                    act.wait_ge(up_done, n + 1)
                    if known >= 2:
                        act.wait_ge(hidden_done, n - 1)
                    nc.scalar.activation(gate[:, s, :], ps_h[s][:, 0:F], ACT.Silu).then_inc(gated, 1)

            steps(act, one, 1)

        @block.vector
        def _(dve):
            def one(i, u, j, known):
                n, s = i * U + u, u % 2
                if j == 0:
                    dve.wait_ge(gated, n + 1)
                    if known >= 2:
                        dve.wait_ge(h_turned, n - 1)
                    nc.vector.tensor_tensor(hidden[:, s, :], gate[:, s, :], ps_h[s][:, F:2 * F], ALU.mult).then_inc(
                        hidden_done, 1)
                if j == 1:
                    dve.wait_ge(h_turned, n + 1)
                    if known >= 2:
                        dve.wait_ge(down_done, n - 1)
                    nc.vector.tensor_copy(hidden_t[:, s, :], ps_t[s][:, :]).then_inc(h_copied, 1)
                if j == 2:
                    dve.wait_ge(down_done, n + 1)
                    if known >= U:
                        dve.wait_ge(scattered[u], i * 16)
                    nc.vector.tensor_copy(result[u][:, :], ps_o[s][:, :]).then_inc(result_done, 1)

            steps(dve, one, 2)


def combine(nc, c, d, wk):
    K = 6
    with ExitStack() as ctx:
        R = 8
        M = R // 2
        y = ctx.enter_context(nc.sbuf_tensor("y_choices", [P, R, K, H], F32))
        y_in = [semaphore(nc, c, f"y_in{r}") for r in range(R)]
        y_added = semaphore(nc, c, "y_added")
        stored = semaphore(nc, c, "out_stored")
        block = ctx.enter_context(nc.Block())

        @block.sync
        def _(sp):
            def load(t, r):
                sp.dma_start(y[:, r, :, :].rearrange("p k f -> p (k f)"),
                             d["y6_d"][t * P * K:(t + 1) * P * K, :].rearrange("(p k) f -> p (k f)", k=K)).then_inc(
                    y_in[r], 16)

            for t in range(NT):
                if t >= R and t % M == 0:
                    sp.wait_ge(y_added, (t - R + M) * K)
                load(t, t % R)

        @block.vector
        def _(dve):
            with dve.Fori(0, NT // R) as i:
                for half in range(2):
                    done = i * (R * K) + half * (M * K)
                    for k in range(K):
                        for m in range(M):
                            r = half * M + m
                            if k == 0:
                                dve.wait_ge(y_in[r], (i + 1) * 16)
                            else:
                                dve.wait_ge(y_added, done + ((k - 1) * M + m + 1))
                            x = c["resid"][:, ds((i * R + r) * H, H)]
                            nc.vector.scalar_tensor_tensor(
                                x, y[:, r, k, :],
                                wk[:, :, :].rearrange("p t k -> p (t k)")[:, ds((i * R + r) * K + k, 1)],
                                x, ALU.mult, ALU.add).then_inc(y_added, 1)

        @block.scalar
        def _(act):
            for q in range(NT // M):
                act.wait_ge(y_added, (q + 1) * M * K)
                act.dma_start(d["out"][q * M * P:(q + 1) * M * P, :].rearrange("(t p) f -> p t f", p=P),
                              c["resid"][:, q * M * H:(q + 1) * M * H].rearrange("p (t f) -> p t f", f=H)).then_inc(
                    stored, 16)
            act.wait_ge(stored, 16 * (NT // M))


def build(nc, d, upto=99):
    for L in (L0, L1):
        d[f"{L.name}_qd"] = nc.dram_tensor(f"{L.name}_qd", [3, L.blocks, L.d, HB, S], BF16, kind="Internal").ap()
        d[f"{L.name}_kd"] = nc.dram_tensor(f"{L.name}_kd", [3, L.blocks, L.d, L.kv_of_block, S], BF16,
                                           kind="Internal").ap()
        d[f"{L.name}_vd"] = nc.dram_tensor(f"{L.name}_vd", [L.groups, S, L.vw], F32, kind="Internal").ap()
        d[f"{L.name}_od"] = nc.dram_tensor(f"{L.name}_od", [L.groups * P, S], F32, kind="Internal").ap()
    d["xn_d"] = nc.dram_tensor("xn_d", [T, H], F32, kind="Internal").ap()
    d["y6_d"] = nc.dram_tensor("y6_d", [T * 6, H], F32, kind="Internal").ap()
    d["neg_d"] = nc.dram_tensor("neg_d", [4, P, 4 * HQ * TB], BF16, kind="Internal").ap()
    with ExitStack() as ctx:
        def sb(name, shape, dt=F32):
            return ctx.enter_context(nc.sbuf_tensor(name, shape, dt))

        c = {
            "semaphores": [], "resid": sb("resid_f32", [P, NT * H]), "mean_var": sb("mean_var", [P, NT * 2]), "rstd": sb("rstd", [P, NT]),
            "masks": sb("masks_bf16", [P, 5, P], BF16), "ident": sb("ident_f32", [P, P]), "bo": sb("bo", [P, H]),
        }
        c["FT"] = d["l0_w2"].shape[1] // H
        load_constants(nc, c, d)
        for L in (L0, L1):
            layernorm_statistics(nc, c, f"a{L.name}")
            project(nc, c, d, L)
            attend(nc, c, d, L)
            join(nc, c, d, L)
            if L is L0:
                if upto < 1: break
                layernorm_statistics(nc, c, "f0")
                dense_experts(nc, c, d)
                retire_semaphores(nc, c)
            else:
                if upto < 3: break
                layernorm_statistics(nc, c, "f1")
                sparse_experts(nc, c, d)
            if upto < 2: break
        if upto < 99:
            store_residual(nc, c, d)


def store_residual(nc, c, d):
    with ExitStack() as ctx:
        stored = semaphore(nc, c, "stored")
        block = ctx.enter_context(nc.Block())

        @block.sync
        def _(sp):
            for b in range(B):
                sp.dma_start(d["out"][b * S:(b + 1) * S, :].rearrange("(t p) f -> p t f", p=P),
                             c["resid"][:, b * TB * H:(b + 1) * TB * H].rearrange("p (t f) -> p t f", f=H)).then_inc(
                    stored, 16)
            sp.wait_ge(stored, 16 * B)


def shape_constants():
    half = L0.d // 2
    inv = np.float32(1.0) / (np.float32(10000.0) ** (np.arange(half, dtype=np.float32) / np.float32(half)))
    freq = (np.arange(S, dtype=np.float32)[:, None] * inv[None, :].astype(np.float32)).astype(np.float64)
    dim = (np.arange(P) % L0.d) // 2
    sign = np.where(np.arange(P) % 2 == 0, -1.0, 1.0)[:, None]
    cos = np.cos(freq).T[dim].astype(np.float32)
    sin = (np.sin(freq).T[dim] * sign).astype(np.float32)
    i = np.arange(P)
    masks = np.zeros((P, 5, P), np.float32)
    masks[:, 0] = i[:, None] == i[None, :]
    masks[:, 1] = np.where(i[None, :] > i[:, None], NEG, 0)
    masks[:, 2] = np.where(i[:, None] > i[None, :], NEG, 0)
    masks[:, 3] = i[:, None] < i[None, :]
    masks[:, 4] = 1
    expert = np.minimum(np.arange(25 * P) // 176, 16)
    spread = np.zeros((3, 32, 25 * P), np.float32)
    spread[:, expert, np.arange(25 * P)] = 1

    def lower(n):
        x = np.arange(n)[None, :] < np.arange(n)[:, None]
        return np.broadcast_to(x.astype(np.float32), (P, n, n)).copy()

    return {"cos": cos, "sin": sin, "masks": masks, "ident": np.eye(P, dtype=np.float32),
            "spread": spread.reshape(96, 25 * P), "lower4": lower(4), "lower8": lower(8),
            "numbers": np.broadcast_to(np.arange(64, dtype=np.float32), (P, 64)).copy(),
            "pnum": np.arange(P, dtype=np.float32)[:, None]}


def lay_out(inputs):
    a = {k: np.asarray(v) for k, v in inputs.items()}

    def columns(w):
        return np.ascontiguousarray(w.T.reshape(-1, P, w.shape[0]).transpose(1, 0, 2))

    out = {"x": a["L0_attn_x"].reshape(T, H)}
    for L in (L0, L1):
        for w in "qkvo":
            out[f"{L.name}_w{w}"] = columns(a[f"L{L.name[1]}_attn_W{w}"])
            b = a[f"L{L.name[1]}_attn_b{w}"]
            out[f"{L.name}_b{w}"] = np.ascontiguousarray(b.reshape(-1, min(P, b.size)).T) if w in "qk" else b
    out["l0_router"] = columns(a["L0_ffn_gate_w"])
    out["l1_router"] = np.ascontiguousarray(a["L1_ffn_gate_w"].reshape(KH, P, 64).transpose(1, 0, 2))
    out["l1_bias"] = a["L1_ffn_bias"]
    pad = np.zeros((25 * P - 18 * 176, H), np.float32)
    for dst, w, ws in (("l0_w1", "L0_ffn_W1", "L0_ffn_Ws1"), ("l0_w3", "L0_ffn_W3", "L0_ffn_Ws3")):
        x = np.concatenate([a[w].reshape(-1, H), a[ws], pad])
        out[dst] = np.ascontiguousarray(x.reshape(25, P, KH, P).transpose(3, 0, 2, 1)).reshape(P, 25 * H)
    x = np.concatenate([a["L0_ffn_W2"].transpose(0, 2, 1).reshape(-1, H), a["L0_ffn_Ws2"].T, pad])
    out["l0_w2"] = np.ascontiguousarray(x.reshape(25, P, H).transpose(1, 0, 2)).reshape(P, 25 * H)
    gu = np.concatenate([a["L1_ffn_w_gate"], a["L1_ffn_w_up"]], -1)
    out["l1_w_up"] = np.ascontiguousarray(gu.reshape(32, 2, KH, P, 192).transpose(0, 3, 1, 2, 4))
    out["l1_w_down"] = np.ascontiguousarray(a["L1_ffn_w_down"].reshape(32, 2, 96, H).transpose(0, 2, 1, 3))
    for dst, w in (("l1_wsg", "L1_ffn_ws_gate"), ("l1_wsu", "L1_ffn_ws_up")):
        out[dst] = np.ascontiguousarray(a[w].reshape(KH, P, 96).transpose(1, 0, 2))
    out["l1_wsd"] = a["L1_ffn_ws_down"]
    out.update(shape_constants())
    return out


def kernel(**inputs):
    import concourse.bacc as _bacc
    from concourse.bass_utils import run_bass_kernel_spmd as _run

    nc = _bacc.Bacc("TRN2", target_bir_lowering=False, num_devices=1)
    arrays, d = {}, {}
    for name, a in lay_out(inputs).items():
        a = np.ascontiguousarray(a)
        arrays[f"in_{name}"] = a
        d[name] = nc.dram_tensor(f"in_{name}", a.shape, mybir.dt.from_np(a.dtype), kind="ExternalInput").ap()
    d["out"] = nc.dram_tensor("out_0", [T, H], F32, kind="ExternalOutput").ap()
    build(nc, d)
    r = _run(nc, [arrays], core_ids=[0])
    return r.results[0]["out_0"].reshape(B, S, H)
```

```python
from contextlib import ExitStack

import concourse.bass as bass
import numpy as np
from concourse import mybir

ALU = mybir.AluOpType
ACT = mybir.ActivationFunctionType
AX = mybir.AxisListType
F32 = mybir.dt.float32
BF16 = mybir.dt.bfloat16
I32 = mybir.dt.int32
F32R = mybir.dt.float32r
U32 = mybir.dt.uint32
ds = bass.ds

P = 128
B, S, H = 4, 512, 256
T = B * S
NT = T // P
TB = S // P
KH = H // P
HQ = 4
HB = 16
QUAD = 32
M_ROW = 96
NEG = -1.0e30
HIGH_BITS = -(1 << 12)

PAIRS_L0 = [(0, 0), (0, 1), (0, 2), (1, 0), (1, 1), (2, 0)]
PAIRS_L1 = [(i, j) for i in range(3) for j in range(3)]


class Layer:

    def __init__(self, name, d, nq, nkv, causal, scale, pairs):
        self.name, self.d, self.nq, self.nkv, self.causal, self.scale, self.pairs = (
            name, d, nq, nkv, causal, scale, pairs)
        self.rows = len(pairs) * d
        self.blocks = B * nq // HB
        self.groups = self.blocks * HB // HQ
        self.kv_of_block = HB * nkv // nq
        self.kv_of_group = HQ * nkv // nq
        self.vw = self.kv_of_group * QUAD


L0 = Layer("l0", 16, 16, 16, True, 0.25, PAIRS_L0)
L1 = Layer("l1", 8, 32, 8, False, 8 ** -0.5, PAIRS_L1)


def runs(parts):
    out = []
    for n, p in enumerate(parts):
        if out and out[-1][0] == p:
            out[-1][2] += 1
        else:
            out.append([p, n, 1])
    return out


def climbs(parts):
    out = []
    for n, p in enumerate(parts):
        if p == 0:
            out.append([n, 0])
        out[-1][1] += 1
    return out


def semaphore(nc, c, name):
    s = nc.alloc_semaphore(name=name)
    c["semaphores"].append(s)
    return s


def retire_semaphores(nc, c):
    nc.all_engine_barrier()
    nc.clear_and_free_semaphores(c["semaphores"])
    nc.all_engine_barrier()
    c["semaphores"] = []


def wait_above_zero(eng, sem, value):
    if value > 0:
        eng.wait_ge(sem, value)


def row_statistics(nc, c, b):
    for t in range(b * TB, (b + 1) * TB):
        nc.vector.bn_stats(c["stats"][:, t * 6:(t + 1) * 6], c["resid"][:, t * H:(t + 1) * H])


def layernorm_statistics(nc, c, tag):
    with ExitStack() as ctx:
        var = ctx.enter_context(nc.sbuf_tensor(f"var_{tag}", [P, NT], F32))
        root = ctx.enter_context(nc.sbuf_tensor(f"root_{tag}", [P, NT], F32))
        work = ctx.enter_context(nc.sbuf_tensor(f"work_{tag}", [P, NT], F32))
        mean_done, var_done, root_done, step_done = (
            semaphore(nc, c, f"{n}_{tag}") for n in ("mean_done", "var_done", "root_done", "step_done"))
        block = ctx.enter_context(nc.Block())
        mean_var = c["mean_var"][:, :].rearrange("p (t s) -> p t s", s=2)

        @block.vector
        def _(dve):
            for t in range(NT):
                nc.vector.bn_aggr(c["mean_var"][:, t * 2:t * 2 + 2], c["stats"][:, t * 6:t * 6 + 6]).then_inc(mean_done, 1)
            dve.wait_ge(mean_done, NT)
            nc.vector.tensor_scalar(var[:, :], mean_var[:, :, 1], 1e-5, None, ALU.add).then_inc(var_done, 1)
            dve.wait_ge(root_done, 1)
            nc.vector.reciprocal(c["rstd"][:, :], root[:, :]).then_inc(step_done, 1)
            dve.wait_ge(step_done, 1)
            nc.vector.tensor_tensor(work[:, :], c["rstd"][:, :], c["rstd"][:, :], ALU.mult).then_inc(step_done, 1)
            dve.wait_ge(step_done, 2)
            nc.vector.tensor_tensor(work[:, :], work[:, :], var[:, :], ALU.mult).then_inc(step_done, 1)
            dve.wait_ge(step_done, 3)
            nc.vector.tensor_scalar(work[:, :], work[:, :], -0.5, 1.5, ALU.mult, ALU.add).then_inc(step_done, 1)
            dve.wait_ge(step_done, 4)
            nc.vector.tensor_tensor(c["rstd"][:, :], c["rstd"][:, :], work[:, :], ALU.mult).then_inc(step_done, 1)

        @block.scalar
        def _(act):
            act.wait_ge(var_done, 1)
            nc.scalar.activation(root[:, :], var[:, :], ACT.Sqrt).then_inc(root_done, 1)


def load_constants(nc, c, d):
    with ExitStack() as ctx:
        masks = ctx.enter_context(nc.sbuf_tensor("masks_f32", [P, 5, P], F32))
        x_in = [semaphore(nc, c, f"x_in{b}") for b in range(B)]
        masks_in, ident_in = semaphore(nc, c, "masks_in"), semaphore(nc, c, "ident_in")
        block = ctx.enter_context(nc.Block())

        @block.sync
        def _(sp):
            for b in range(B):
                sp.dma_start(c["resid"][:, b * TB * H:(b + 1) * TB * H].rearrange("p (t f) -> p t f", f=H),
                             d["x"][b * S:(b + 1) * S, :].rearrange("(t p) f -> p t f", p=P)).then_inc(x_in[b], 16)
            sp.dma_start(masks[:, :, :], d["masks"]).then_inc(masks_in, 16)
            sp.dma_start(c["ident"][:, :], d["ident"]).then_inc(ident_in, 16)
            sp.wait_ge(ident_in, 16)

        @block.vector
        def _(dve):
            for b in range(B):
                dve.wait_ge(x_in[b], 16)
                row_statistics(nc, c, b)
            dve.wait_ge(masks_in, 16)
            nc.vector.tensor_copy(c["masks"][:, :, :], masks[:, :, :])


def project(nc, c, d, L):
    rope = L.causal
    n = L.name
    kf = L.nkv * L.d
    KT = -(-kf // P)
    kp = min(kf, P)
    NF = KH + KT
    with ExitStack() as ctx:
        def sb(name, shape, dt=F32):
            return ctx.enter_context(nc.sbuf_tensor(f"{name}_{n}", shape, dt))

        def sem(name):
            return semaphore(nc, c, f"{name}_{n}")

        wq, wk, wv = sb("wq_sb", [P, KH, H]), sb("wk_sb", [P, KH, kf]), sb("wv_sb", [P, KH, kf])
        bqk, bv = sb("bqk_sb", [P, NF]), sb("bv_sb", [P, kf])
        if rope:
            cos, sin = sb("cos_sb", [P, S]), sb("sin_sb", [P, S])
            swapped = sb("swapped", [P, NF, S])
        xn = sb("xn", [P, 2, TB, H])
        xnt = sb("xnt", [P, 2, KH, S])
        qk = sb("qk", [P, NF, S])
        rest = sb("rest", [P, NF, S])
        parts = sb("parts", [P, 2, 3, NF, S], BF16)
        vaug = sb("vaug", [P, TB, L.nkv, QUAD])
        ps_t = ctx.enter_context(nc.psum_tensor(f"ps_t_{n}", [P, KH, S], F32))
        ps_qk = ctx.enter_context(nc.psum_tensor(f"ps_qk_{n}", [P, NF, S], F32))
        ps_v = ctx.enter_context(nc.psum_tensor(f"ps_v_{n}", [P, TB, 256], F32))

        weights_in, xn_ready, t_ready, xnt_ready, qk_ready, v_ready = (
            sem(x) for x in ("weights_in", "xn_ready", "t_ready", "xnt_ready", "qk_ready", "v_ready"))
        qk_biased, rope_swapped, rope_cos, rope_sin, roped = (
            sem(x) for x in ("qk_biased", "rope_swapped", "rope_cos", "rope_sin", "roped"))
        part0, rest1, part1, part2, v_out, v_stored, ones_set = (
            sem(x) for x in ("part0", "rest1", "part1", "part2", "v_out", "v_stored", "ones_set"))
        q_stored, k_stored = [sem("q_stored0"), sem("q_stored1")], [sem("k_stored0"), sem("k_stored1")]
        fixed_set = sem("fixed_set")
        n_weights = 7 + 2 * rope
        q_stores = KH
        k_stores = KT if rope else 2
        hg = L.nkv // L.kv_of_group
        block = ctx.enter_context(nc.Block())

        def store_parts(eng, b, part, keys, stored):
            for m in range(k_stores if keys else q_stores):
                if not keys:
                    blk, h8 = b if rope else b * 2 + m, P // L.d
                    dst = d[f"{n}_qd"][part, ds(blk, 1), :, (m * h8 if rope else 0):(m + 1) * h8 if rope else HB, :]
                    src = parts[:, b % 2, part, m, :]
                elif rope:
                    dst, src = d[f"{n}_kd"][part, ds(b, 1), :, m * 8:(m + 1) * 8, :], parts[:, b % 2, part, KH + m, :]
                else:
                    dst, src = d[f"{n}_kd"][part, ds(b * 2 + m, 1)], parts[m * 32:(m + 1) * 32, b % 2, part, KH, :]
                eng.dma_start(dst.rearrange("o e h t -> (o h) e t"), src).then_inc(stored[b % 2], 16)

        @block.sync
        def _(sp):
            for dst, src in [(wq, "wq"), (wk, "wk"), (wv, "wv")]:
                sp.dma_start(dst[:, :, :], d[f"{n}_{src}"]).then_inc(weights_in, 16)
            sp.dma_start(bqk[:, 0:KH], d[f"{n}_bq"]).then_inc(weights_in, 16)
            sp.dma_start(bqk[0:kp, KH:NF], d[f"{n}_bk"]).then_inc(weights_in, 16)
            sp.dma_start(bv[:, :], d[f"{n}_bv"].rearrange("(a n) -> a n", a=1).to_broadcast([P, kf])).then_inc(
                weights_in, 16)
            sp.dma_start(c["bo"][:, :], d[f"{n}_bo"].rearrange("(a n) -> a n", a=1).to_broadcast([P, H])).then_inc(
                weights_in, 16)
            if rope:
                sp.dma_start(cos[:, :], d["cos"]).then_inc(weights_in, 16)
                sp.dma_start(sin[:, :], d["sin"]).then_inc(weights_in, 16)
            for b in range(B):
                for part, ready in ((0, part0), (1, part1), (2, part2)):
                    sp.wait_ge(ready, b + 1)
                    store_parts(sp, b, part, False, q_stored)
                    store_parts(sp, b, part, True, k_stored)
            for slot in range(2):
                sp.wait_ge(q_stored[slot], 16 * 3 * q_stores * B // 2)
                sp.wait_ge(k_stored[slot], 16 * 3 * k_stores * B // 2)

        @block.gpsimd
        def _(pool):
            fixed = 0
            if L.rows < M_ROW:
                for u in range(4):
                    nc.gpsimd.memset(c["k"][u][64:M_ROW, :], 0.0).then_inc(fixed_set, 1)
                    nc.gpsimd.memset(c["q"][u][64:M_ROW, :, :], 0.0).then_inc(fixed_set, 1)
                fixed = 8
            for u in range(4):
                nc.gpsimd.memset(c["k"][u][M_ROW:M_ROW + 3, :], 1.0).then_inc(fixed_set, 1)
            pool.wait_ge(fixed_set, fixed + 4)
            pool.wait_ge(weights_in, 16 * n_weights)
            for b in range(B):
                if rope:
                    pool.wait_ge(qk_biased, b + 1)
                    wait_above_zero(pool, part1, b)
                    wait_above_zero(pool, part2, b)
                    nc.gpsimd.tensor_tensor(rest[:, :, :], qk[:, :, :],
                                            cos[:, :].unsqueeze(1).to_broadcast([P, NF, S]), ALU.mult).then_inc(
                        rope_cos, 1)
                pool.wait_ge(v_out, b + 1)
                for t in range(TB):
                    pool.dma_start(d[f"{n}_vd"][b * hg:(b + 1) * hg, t * P:(t + 1) * P, :].rearrange("g p w -> p g w"),
                                   vaug[:, t, :, :].rearrange("p (g h) w -> p g (h w)", g=hg)).then_inc(v_stored, 16)
            pool.wait_ge(v_stored, 16 * TB * B)

        def normalise(dve, b):
            wait_above_zero(dve, t_ready, b - 1)
            for t in range(TB):
                at = b * TB + t
                op = nc.vector.tensor_scalar(
                    xn[:, b % 2, t, :], c["resid"][:, ds(at * H, H)], c["mean_var"][:, ds(at * 2, 1)],
                    c["rstd"][:, ds(at, 1)], ALU.subtract, ALU.mult)
            op.then_inc(xn_ready, 1)

        @block.tensor
        def _(pe):
            def turn(b):
                pe.wait_ge(xn_ready, b + 1)
                wait_above_zero(pe, xnt_ready, b)
                for k in range(KH):
                    for t in range(TB):
                        op = nc.tensor.transpose(ps_t[:, k, t * P:(t + 1) * P],
                                                 xn[:, b % 2, t, k * P:(k + 1) * P], c["ident"][:, :])
                op.then_inc(t_ready, 1)

            turn(0)
            pe.wait_ge(weights_in, 16 * n_weights)
            for b in range(B):
                pe.wait_ge(xnt_ready, b + 1)
                wait_above_zero(pe, qk_biased, b)
                for m in range(NF):
                    w, lo, width = (wq, m * P, P) if m < KH else (wk, (m - KH) * P, kp)
                    for k in range(KH):
                        op = nc.tensor.matmul(ps_qk[0:width, m, :], w[:, k, lo:lo + width], xnt[:, b % 2, k, :],
                                              start=k == 0, stop=k == KH - 1)
                op.then_inc(qk_ready, 1)
                if b + 1 < B:
                    turn(b + 1)
                wait_above_zero(pe, v_out, b)
                for t in range(TB):
                    for k in range(KH):
                        op = nc.tensor.matmul(ps_v[:, t, 0:kf], xnt[:, b % 2, k, t * P:(t + 1) * P], wv[:, k, :],
                                              start=k == 0, stop=k == KH - 1)
                op.then_inc(v_ready, 1)

        @block.scalar
        def _(act):
            def keep_turned(b):
                act.wait_ge(t_ready, b + 1)
                wait_above_zero(act, v_ready, b - 1)
                nc.scalar.copy(xnt[:, b % 2, :, :], ps_t[:, :, :]).then_inc(xnt_ready, 1)

            keep_turned(0)
            act.wait_ge(weights_in, 16 * n_weights)
            for b in range(B):
                act.wait_ge(qk_ready, b + 1)
                wait_above_zero(act, rest1, b)
                for m in range(NF):
                    w = P if m < KH else kp
                    op = nc.scalar.activation(qk[0:w, m, :], ps_qk[0:w, m, :], ACT.Identity,
                                              bias=bqk[0:w, m:m + 1])
                op.then_inc(qk_biased, 1)
                if b + 1 < B:
                    keep_turned(b + 1)
                act.wait_ge(roped if rope else qk_biased, b + 1)
                wait_above_zero(act, q_stored[b % 2], 16 * 3 * q_stores * (b // 2))
                wait_above_zero(act, k_stored[b % 2], 16 * 3 * k_stores * (b // 2))
                nc.scalar.copy(parts[:, b % 2, 0, 0:KH, :], qk[:, 0:KH, :])
                nc.scalar.copy(parts[0:kp, b % 2, 0, KH:NF, :], qk[0:kp, KH:NF, :]).then_inc(part0, 1)
                act.wait_ge(rest1, b + 1)
                nc.scalar.copy(parts[:, b % 2, 1, 0:KH, :], rest[:, 0:KH, :])
                nc.scalar.copy(parts[0:kp, b % 2, 1, KH:NF, :], rest[0:kp, KH:NF, :]).then_inc(part1, 1)

        @block.vector
        def _(dve):
            normalise(dve, 0)
            normalise(dve, 1)
            nc.vector.memset(vaug[:, :, :, :], 1.0).then_inc(ones_set, 1)
            dve.wait_ge(ones_set, 1)
            dve.wait_ge(weights_in, 16 * n_weights)
            for b in range(B):
                if rope:
                    dve.wait_ge(qk_biased, b + 1)
                    nc.vector.stream_shuffle(swapped[:, :, :], qk[:, :, :],
                                             [i ^ 1 for i in range(32)]).then_inc(rope_swapped, 1)
                    dve.wait_ge(rope_swapped, b + 1)
                    nc.vector.tensor_tensor(swapped[:, :, :], swapped[:, :, :],
                                            sin[:, :].unsqueeze(1).to_broadcast([P, NF, S]),
                                            ALU.mult).then_inc(rope_sin, 1)
                    dve.wait_ge(rope_sin, b + 1)
                    dve.wait_ge(rope_cos, b + 1)
                    nc.vector.tensor_tensor(qk[:, :, :], rest[:, :, :], swapped[:, :, :], ALU.add).then_inc(
                        roped, 1)
                if b + 2 < B:
                    normalise(dve, b + 2)
                dve.wait_ge(v_ready, b + 1)
                wait_above_zero(dve, v_stored, 16 * TB * b)
                for t in range(TB):
                    op = nc.vector.tensor_tensor(
                        vaug[:, t, :, 0:L.d], ps_v[:, t, 0:kf].rearrange("p (h e) -> p h e", e=L.d),
                        bv[:, :].rearrange("p (h e) -> p h e", e=L.d), ALU.add)
                op.then_inc(v_out, 1)
                dve.wait_ge(part0, b + 1)
                if not rope:
                    wait_above_zero(dve, part1, b)
                    wait_above_zero(dve, part2, b)
                now = parts[:, b % 2]
                nc.vector.tensor_tensor(rest[:, 0:KH, :], qk[:, 0:KH, :], now[:, 0, 0:KH, :], ALU.subtract)
                nc.vector.tensor_tensor(rest[0:kp, KH:NF, :], qk[0:kp, KH:NF, :], now[0:kp, 0, KH:NF, :],
                                        ALU.subtract).then_inc(rest1, 1)
                dve.wait_ge(part1, b + 1)
                wait_above_zero(dve, q_stored[b % 2], 16 * 3 * q_stores * (b // 2))
                wait_above_zero(dve, k_stored[b % 2], 16 * 3 * k_stores * (b // 2))
                nc.vector.tensor_tensor(now[:, 2, 0:KH, :], rest[:, 0:KH, :], now[:, 1, 0:KH, :],
                                        ALU.subtract)
                nc.vector.tensor_tensor(now[0:kp, 2, KH:NF, :], rest[0:kp, KH:NF, :],
                                        now[0:kp, 1, KH:NF, :], ALU.subtract).then_inc(part2, 1)


def attend(nc, c, d, L):
    n = L.name
    G, U = L.groups, 4
    R = L.rows
    q_parts, k_parts = [q for q, _ in L.pairs], [k for _, k in L.pairs]
    q_runs, k_climbs = runs(q_parts), climbs(k_parts)
    q_loads, kv_loads = len(q_runs), len(k_climbs) + 1
    with ExitStack() as ctx:
        def sb(name, shape, dt=F32):
            return ctx.enter_context(nc.sbuf_tensor(f"{name}_{n}", shape, dt))

        def sem(name):
            return semaphore(nc, c, f"{name}_{n}")

        q, k = c["q"], c["k"]
        v = [sb(f"v{u}", [P, TB, L.vw]) for u in range(U)]
        probs = [sb(f"probs{t}", [P, HQ, S]) for t in range(TB)]
        row_max = sb("row_max", [P, 2, HQ * TB])
        neg_rest = sb("neg_rest", [P, 2, HQ * TB])
        neg_parts = sb("neg_parts", [P, 2, 4, HQ * TB], BF16)
        neg_turned = sb("neg_turned", [P, 2, 4 * HQ * TB], BF16)
        mixed = sb("mixed", [P, 2, S])
        ps_max = ctx.enter_context(nc.psum_tensor(f"ps_max_{n}", [P, 3, S], F32))
        ps_s = ctx.enter_context(nc.psum_tensor(f"ps_s_{n}", [P, 2, 2, S], F32))
        ps_o = ctx.enter_context(nc.psum_tensor(f"ps_o_{n}", [P, S], F32))

        q_loaded = [sem(f"q_loaded{u}") for u in range(U)]
        kv_loaded = [sem(f"kv_loaded{u}") for u in range(U)]
        fill_set = sem("fill_set")
        pool_passed = sem("pool_passed")
        max_scores, max_taken = sem("max_scores"), sem("max_taken")
        neg0, neg_r1, neg1, neg_split = sem("neg0"), sem("neg_r1"), sem("neg1"), sem("neg_split")
        turned, neg_stored, neg_loaded = sem("turned"), sem("neg_stored"), sem("neg_loaded")
        scores, exps, values_used, mixed_copied, mixed_stored = (
            sem("scores"), sem("exps"), sem("values_used"), sem("mixed_copied"), sem("mixed_stored"))
        wo_in = sem("wo_in")
        early = Inverses(nc, c, ctx, L, "early", range(B - 1))
        EARLY = G // B * (B - 1)
        block = ctx.enter_context(nc.Block())

        LEAD = 2

        def max_slot(y):
            return 1 if y == U * HQ * TB - 1 else y % 3

        def body_of_groups(eng, one):
            for u in range(U):
                one(eng, 0, u, u)
            with eng.Fori(1, G // U - 1) as i:
                for u in range(U):
                    one(eng, i, u, 99)
            for u in range(U):
                one(eng, G // U - 1, u, G - U + u)

        @block.sync
        def _(sp):
            def load_queries(i, u):
                for part, at, count in q_runs:
                    src = d[f"{n}_qd"][part, ds(i, 1), :, u * HQ:(u + 1) * HQ, :].rearrange(
                        "o e h t -> o e (h t)").to_broadcast([count, L.d, HQ * S])
                    sp.dma_start(q[u][at * L.d:(at + count) * L.d, :, :].rearrange("p h t -> p (h t)"),
                                 src).then_inc(q_loaded[u], 16)

            def store_negated(g, u):
                sp.wait_ge(turned, g + 1)
                sp.dma_start(d["neg_d"][u], neg_turned[:, u % 2, :]).then_inc(neg_stored, 16)

            def load_negated(g, u):
                sp.wait_ge(neg_stored, (g + 1) * 16)
                blocks = d["neg_d"][u].rearrange("(b c) (n e) -> n c b e", b=TB, n=2)
                for part in range(3):
                    c0 = part % 2 * HQ * TB
                    sp.dma_start(q[u][M_ROW + part:M_ROW + part + 1, :, :].rearrange(
                        "o h (t b e) -> o (h t) b e", b=TB, e=QUAD), blocks[part // 2, c0:c0 + HQ * TB]).then_inc(
                        neg_loaded, 16)

            def step(sp, i, u, known):
                g = i * U + u
                if known == 99 or 0 < known < G - 3:
                    sp.wait_ge(scores, g * 8)
                    load_queries(i if u == 0 else i + 1, (u + 3) % U)
                if known < G - 1 or known == 99:
                    store_negated(g + 1, (u + 1) % U)
                    load_negated(g + 1, (u + 1) % U)

            for u in range(U):
                load_queries(0, u)
            store_negated(0, 0)
            load_negated(0, 0)
            sp.dma_start(c["wo"][:, :, :], d[f"{n}_wo"]).then_inc(wo_in, 16)
            body_of_groups(sp, step)
            sp.wait_ge(mixed_stored, EARLY * 16)
            early.load(sp, c, d)
            early.spread(sp, c, d)
            sp.wait_ge(wo_in, 16)

        @block.gpsimd
        def _(pool):


            def load_keys(i, u):
                w = L.kv_of_group
                for at, count in k_climbs:
                    src = d[f"{n}_kd"][0:count, ds(i, 1), :, u * w:(u + 1) * w, :].rearrange(
                        "c o e h t -> (o c) e (h t)")
                    pool.dma_start(k[u][at * L.d:(at + count) * L.d, :], src).then_inc(kv_loaded[u], 16)

            def load_values(i, u):
                pool.dma_start(v[u][:, :, :], d[f"{n}_vd"][ds(i * U + u, 1)].rearrange(
                    "o (t p) w -> p (o t) w", p=P)).then_inc(kv_loaded[u], 16)

            for u in range(U):
                load_keys(0, u)
                load_values(0, u)

            def step(pool, i, u, known):
                g = i * U + u
                if known == 99 or 0 < known < G - 3:
                    pool.wait_ge(scores, g * 8)
                    pool.sem_inc(pool_passed, 1)
                    load_keys(i if u == 0 else i + 1, (u + 3) % U)
                    pool.wait_ge(values_used, g * TB)
                    pool.sem_inc(pool_passed, 1)
                    load_values(i if u == 0 else i + 1, (u + 3) % U)
                if known > 1:
                    pool.wait_ge(mixed_copied, g - 1)
                    pool.wait_ge(mixed_stored, (g - 2) * 16)
                    pool.sem_inc(pool_passed, 1)
                    pool.dma_start(d[f"{n}_od"][ds((g - 2) * P, P), :], mixed[:, u % 2, :]).then_inc(mixed_stored, 16)

            body_of_groups(pool, step)
            for g in (G - 2, G - 1):
                pool.wait_ge(mixed_copied, g + 1)
                pool.wait_ge(mixed_stored, g * 16)
                pool.dma_start(d[f"{n}_od"][g * P:(g + 1) * P, :], mixed[:, g % 2, :]).then_inc(mixed_stored, 16)
            pool.wait_ge(mixed_stored, 16 * G)

        @block.vector
        def _(dve):
            def split(g, s, part, known):
                if part == 0:
                    dve.wait_ge(max_taken, (g + 1) * 16)
                    nc.vector.tensor_scalar(neg_parts[:, s, 0, :], row_max[:, s, :], -1.0, None, ALU.mult).then_inc(
                        neg0, 1)
                if part == 1:
                    dve.wait_ge(neg0, g + 1)
                    nc.vector.scalar_tensor_tensor(neg_rest[:, s, :], row_max[:, s, :], -1.0, neg_parts[:, s, 0, :],
                                                   ALU.mult, ALU.subtract).then_inc(neg_r1, 1)
                if part == 2:
                    dve.wait_ge(neg_r1, g + 1)
                    nc.vector.tensor_copy(neg_parts[:, s, 1, :], neg_rest[:, s, :]).then_inc(neg1, 1)
                if part == 3:
                    dve.wait_ge(neg1, g + 1)
                    nc.vector.tensor_tensor(neg_parts[:, s, 2, :], neg_rest[:, s, :], neg_parts[:, s, 1, :],
                                            ALU.subtract).then_inc(neg_split, 1)
                if part == 4:
                    dve.wait_ge(neg_split, g + 1)
                    if known > 1:
                        dve.wait_ge(neg_stored, (g - 1) * 16)
                    nc.vector.transpose(neg_turned[:, s, :],
                                        neg_parts[:, s, :, :].rearrange("p c n -> p (c n)")).then_inc(turned, 1)

            def step(dve, i, u, known):
                g = i * U + u
                s, first = u % 2, u * HQ * TB
                for t in range(TB):
                    for h in range(HQ):
                        x = t * HQ + h
                        dve.wait_ge(max_scores, g * 16 + x + 1)
                        width = (t + 1) * P if L.causal else S
                        nc.vector.tensor_reduce(row_max[:, s, h * TB + t:h * TB + t + 1],
                                                ps_max[:, max_slot(first + x), 0:width], AX.X, ALU.max).then_inc(
                            max_taken, 1)
                        if known > 0 and x < 5:
                            split(g - 1, 1 - s, x, known - 1)

            nc.vector.memset(neg_parts[:, :, 3, :], 0.0).then_inc(fill_set, 1)
            dve.wait_ge(fill_set, 1)
            body_of_groups(dve, step)
            for part in range(5):
                split(G - 1, 1, part, G - 1)
            early.invert(dve)
            for b in early.rows:
                early.divide(dve, c, b)

        @block.scalar
        def _(act):
            def copy_mixed(g, s):
                act.wait_ge(values_used, (g + 1) * TB)
                if not isinstance(g, int) or g > 1:
                    act.wait_ge(mixed_stored, (g - 1) * 16)
                nc.scalar.copy(mixed[:, s, :], ps_o[:, :]).then_inc(mixed_copied, 1)

            def step(act, i, u, known):
                g = i * U + u
                for x in range(8):
                    kt, pair = x // 2, x % 2
                    lo = kt * P if L.causal else 0
                    act.wait_ge(scores, g * 8 + x + 1)
                    if known > 0 and pair == 0:
                        act.wait_ge(values_used, g * TB + kt - 3)
                    nc.scalar.activation(probs[kt][:, 2 * pair:2 * pair + 2, lo:S], ps_s[:, pair, :, lo:S], ACT.Exp,
                                         scale=L.scale).then_inc(exps, 1)
                    if x == 1 and known > 0:
                        copy_mixed(g - 1, (u + 1) % 2)

            body_of_groups(act, step)
            copy_mixed(G - 1, (G - 1) % 2)

        @block.tensor
        def _(pe):
            def top(g, u, x):
                t, h = x // HQ, x % HQ
                y = u * HQ * TB + x
                slot = max_slot(y)
                back = {0: 4, 1: 2, 2: 4, U * HQ * TB - 1: 2}.get(y, 3)
                if not isinstance(g, int) or g * 16 + x >= 3:
                    pe.wait_ge(max_taken, g * 16 + (x + 1 - back))
                kc = h * S if L.kv_of_group > 1 else 0
                width = (t + 1) * P if L.causal else S
                op = nc.tensor.matmul(ps_max[:, slot, 0:width], q[u][0:R, h, t * P:(t + 1) * P],
                                      k[u][0:R, kc:kc + width], start=True, stop=not L.causal)
                if L.causal:
                    op = nc.tensor.matmul(ps_max[:, slot, t * P:width], c["masks"][:, 0, :], c["masks"][:, 1, :],
                                          start=False, stop=True)
                op.then_inc(max_scores, 1)

            def weigh(g, u, kt):
                pe.wait_ge(exps, g * 8 + 2 * kt + 2)
                if kt == 0 and (not isinstance(g, int) or g > 0):
                    pe.wait_ge(mixed_copied, g)
                lo = kt * P if L.causal else 0
                for h in range(HQ):
                    vc = h * QUAD if L.kv_of_group > 1 else 0
                    op = nc.tensor.matmul(ps_o[h * QUAD:(h + 1) * QUAD, lo:S], v[u][:, kt, vc:vc + QUAD],
                                          probs[kt][:, h, lo:S], start=kt == 0, stop=kt == TB - 1)
                op.then_inc(values_used, 1)

            def step(pe, i, u, known):
                g = i * U + u

                def top_ahead(x):
                    over, x = divmod(x + LEAD, HQ * TB)
                    ahead = 2 + over
                    if known != 99 and known + ahead >= G:
                        return
                    if x == 0:
                        loads = i + ((u + ahead) // U + 1)
                        pe.wait_ge(q_loaded[(u + ahead) % U], loads * (16 * q_loads))
                        pe.wait_ge(kv_loaded[(u + ahead) % U], loads * (16 * kv_loads))
                    top(g + ahead, (u + ahead) % U, x)

                for x in range(8):
                    kt, pair = x // 2, x % 2
                    lo = kt * P if L.causal else 0
                    if x == 0:
                        pe.wait_ge(neg_loaded, (g + 1) * 48)
                    for h in (2 * pair, 2 * pair + 1):
                        top_ahead(2 * x + h % 2)
                        if h % 2 == 0 and (not isinstance(g, int) or g * 8 + x >= 2):
                            pe.wait_ge(exps, g * 8 + x - 1)
                        kc = h * S if L.kv_of_group > 1 else 0
                        op = nc.tensor.matmul(ps_s[:, pair, h % 2, lo:S], k[u][0:M_ROW + 3, kc + kt * P:kc + (kt + 1) * P],
                                              q[u][0:M_ROW + 3, h, lo:S], start=True, stop=not L.causal)
                        if L.causal:
                            op = nc.tensor.matmul(ps_s[:, pair, h % 2, lo:lo + P], c["masks"][:, 0, :],
                                                  c["masks"][:, 2, :], start=False, stop=True)
                    op.then_inc(scores, 1)
                    if x == 1:
                        if known > 0:
                            weigh(g - 1, (u - 1) % U, TB - 1)
                    if x in (3, 5, 7):
                        weigh(g, u, x // 2 - 1)

            for u in range(3):
                pe.wait_ge(q_loaded[u], 16 * q_loads)
                pe.wait_ge(kv_loaded[u], 16 * kv_loads)
                for x in range(HQ * TB if u < 2 else LEAD):
                    top(u, u, x)
            body_of_groups(pe, step)
            weigh(G - 1, U - 1, TB - 1)


class Inverses:

    def __init__(self, nc, c, ctx, L, name, rows):
        self.nc, self.L, self.rows = nc, L, rows
        per_row = P // L.d * KH
        self.h0, self.h1 = rows.start * per_row, rows.stop * per_row
        heads = self.h1 - self.h0
        self.cuts = P // heads
        n = f"{name}_{L.name}"
        self.sums = ctx.enter_context(nc.sbuf_tensor(f"sums_{n}", [heads * self.cuts, S // self.cuts], F32))
        self.sums_in, self.inverted, self.stored = (
            semaphore(nc, c, f"{x}_{n}") for x in ("sums_in", "inverted", "inverse_stored"))
        self.num_in = {b: semaphore(nc, c, f"num_in{b}_{L.name}") for b in rows}
        self.inverse_in = {b: semaphore(nc, c, f"inverse_in{b}_{L.name}") for b in rows}

    def load(self, sp, c, d):
        od = d[f"{self.L.name}_od"].rearrange("(h r) t -> h r t", r=QUAD)
        sp.dma_start(self.sums[:, :], od[self.h0:self.h1, self.L.d, :].rearrange("h (c t) -> h c t", c=self.cuts)
                     ).then_inc(self.sums_in, 16)
        heads = P // self.L.d
        for b in self.rows:
            for m in range(KH):
                h0 = (b * KH + m) * heads
                sp.dma_start(c["num"][:, b, m, :], od[h0:h0 + heads, 0:self.L.d, :]).then_inc(self.num_in[b], 16)

    def invert(self, dve):
        dve.wait_ge(self.sums_in, 16)
        self.nc.vector.reciprocal(self.sums[:, :], self.sums[:, :]).then_inc(self.inverted, 1)

    def spread(self, sp, c, d):
        inv = d["inverse_d"]
        sp.wait_ge(self.inverted, 1)
        sp.dma_start(inv[self.h0:self.h1, :].rearrange("h (c t) -> (h c) t", c=self.cuts), self.sums[:, :]).then_inc(
            self.stored, 16)
        sp.wait_ge(self.stored, 16)
        heads = P // self.L.d
        for b in self.rows:
            for m in range(KH):
                h0 = (b * KH + m) * heads
                sp.dma_start(c["inverse"][:, b, m, :], inv[h0:h0 + heads, :].unsqueeze(1).to_broadcast(
                    [heads, self.L.d, S])).then_inc(self.inverse_in[b], 16)

    def divide(self, dve, c, b):
        dve.wait_ge(self.num_in[b], 16 * KH)
        dve.wait_ge(self.inverse_in[b], 16 * KH)
        num = c["num"][:, b, :, :]
        return self.nc.vector.tensor_tensor(num, num, c["inverse"][:, b, :, :], ALU.mult)


def join(nc, c, d, L):
    n = L.name
    with ExitStack() as ctx:
        def sem(name):
            return semaphore(nc, c, f"{name}_{n}")

        wo = c["wo"]
        ps_y = ctx.enter_context(nc.psum_tensor(f"ps_y_{n}", [P, 2, TB, H], F32))
        biased, divided, projected, added = sem("biased"), sem("divided"), sem("projected"), sem("added")
        last = Inverses(nc, c, ctx, L, "last", range(B - 1, B))
        block = ctx.enter_context(nc.Block())

        @block.sync
        def _(sp):
            last.load(sp, c, d)
            last.spread(sp, c, d)

        @block.gpsimd
        def _(pool):
            for b in range(B):
                r = c["resid"][:, b * TB * H:(b + 1) * TB * H].rearrange("p (t f) -> p t f", f=H)
                nc.gpsimd.tensor_tensor(r, r, c["bo"][:, :].unsqueeze(1).to_broadcast([P, TB, H]),
                                        ALU.add).then_inc(biased, 1)

        @block.vector
        def _(dve):
            def add(b):
                dve.wait_ge(projected, b + 1)
                dve.wait_ge(biased, b + 1)
                r = c["resid"][:, b * TB * H:(b + 1) * TB * H]
                nc.vector.tensor_tensor(r, r, ps_y[:, b % 2, :, :].rearrange("p t f -> p (t f)"),
                                        ALU.add).then_inc(added, 1)

            def row_statistics_after(b):
                dve.wait_ge(added, b + 1)
                row_statistics(nc, c, b)

            last.invert(dve)
            add(0)
            add(1)
            row_statistics_after(0)
            last.divide(dve, c, B - 1).then_inc(divided, 1)
            row_statistics_after(1)
            for b in range(2, B):
                add(b)
                row_statistics_after(b)

        @block.tensor
        def _(pe):
            for b in range(B):
                if b == B - 1:
                    pe.wait_ge(divided, 1)
                wait_above_zero(pe, added, b - 1)
                for t in range(TB):
                    for m in range(KH):
                        op = nc.tensor.matmul(ps_y[:, b % 2, t, :], c["num"][:, b, m, t * P:(t + 1) * P], wo[:, m, :],
                                              start=m == 0, stop=m == KH - 1)
                op.then_inc(projected, 1)


def normalised_rows(nc, c, d, n, experts):
    shared = n == "l1"
    F = 96
    with ExitStack() as ctx:
        def sb(name, shape, dt=F32):
            return ctx.enter_context(nc.sbuf_tensor(f"{name}_{n}f", shape, dt))

        def sem(name):
            return semaphore(nc, c, f"{name}_{n}f")

        wr = sb("wr", [P, KH, experts])
        xn = sb("xn", [P, 2, TB, H])
        xnt, xnt_cut = sb("xnt", [P, 2, KH, S]), sb("xnt_cut", [P, KH, S])
        ps_t = ctx.enter_context(nc.psum_tensor(f"ps_t_{n}f", [P, KH, S], F32))
        ps_l = ctx.enter_context(nc.psum_tensor(f"ps_l_{n}f", [P, TB, experts], F32))
        weights_in, xn_ready, t_ready, xnt_ready, l_ready, l_out, low_kept = (
            sem(x) for x in ("weights_in", "xn_ready", "t_ready", "xnt_ready", "l_ready", "l_out", "low_kept"))
        rows_kept = [sem("rows_kept0"), sem("rows_kept1")]
        if shared:
            wsg, wsu, wsd = sb("wsg", [P, KH, F]), sb("wsu", [P, KH, F]), sb("wsd", [F, H])
            gate, hidden = sb("gate", [F, S]), sb("hidden", [F, S])
            ps_g = ctx.enter_context(nc.psum_tensor("ps_g_sh", [P, 2, S], F32))
            ps_y = ctx.enter_context(nc.psum_tensor("ps_y_sh", [P, TB, H], F32))
            up_ready, gated, hidden_ready, y_ready, y_added = (
                sem(x) for x in ("up_ready", "gated", "hidden_ready", "y_ready", "y_added"))
        cut_done, high_kept = sem("cut_done"), sem("high_kept")
        n_weights = 1 + 3 * shared
        block = ctx.enter_context(nc.Block())

        @block.sync
        def _(sp):
            sp.dma_start(wr[:, :, :], d[f"{n}_router"]).then_inc(weights_in, 16)
            if shared:
                sp.dma_start(wsg[:, :, :], d["l1_wsg"]).then_inc(weights_in, 16)
                sp.dma_start(wsu[:, :, :], d["l1_wsu"]).then_inc(weights_in, 16)
                sp.dma_start(wsd[:, :], d["l1_wsd"]).then_inc(weights_in, 16)
                for b in range(B):
                    sp.wait_ge(xn_ready, b + 1)
                    sp.dma_start(d["xn_d"][b * S:(b + 1) * S, :].rearrange("(t p) f -> p t f", p=P),
                                 xn[:, b % 2, :, :]).then_inc(rows_kept[b % 2], 16)
                for slot in range(2):
                    sp.wait_ge(rows_kept[slot], 16 * B // 2)

        @block.tensor
        def _(pe):
            def turn(b):
                pe.wait_ge(xn_ready, b + 1)
                wait_above_zero(pe, xnt_ready, b)
                for k in range(KH):
                    for t in range(TB):
                        op = nc.tensor.transpose(ps_t[:, k, t * P:(t + 1) * P],
                                                 xn[:, b % 2, t, k * P:(k + 1) * P], c["ident"][:, :])
                op.then_inc(t_ready, 1)

            turn(0)
            pe.wait_ge(weights_in, 16 * n_weights)
            for b in range(B):
                if b + 1 < B:
                    turn(b + 1)
                pe.wait_ge(xnt_ready, b + 1)
                if shared:
                    wait_above_zero(pe, hidden_ready, b)
                    for i, w in enumerate((wsg, wsu)):
                        for k in range(KH):
                            op = nc.tensor.matmul(ps_g[0:F, i, :], w[:, k, :], xnt[:, b % 2, k, :],
                                                  start=k == 0, stop=k == KH - 1)
                    op.then_inc(up_ready, 1)
                wait_above_zero(pe, l_out, b)
                for t in range(TB):
                    for k in range(KH):
                        op = nc.tensor.matmul(ps_l[:, t, :], xnt[:, b % 2, k, t * P:(t + 1) * P], wr[:, k, :],
                                              start=k == 0, stop=k == KH - 1)
                op.then_inc(l_ready, 1)
                if shared:
                    pe.wait_ge(hidden_ready, b + 1)
                    wait_above_zero(pe, y_added, b)
                    for t in range(TB):
                        op = nc.tensor.matmul(ps_y[:, t, :], hidden[:, t * P:(t + 1) * P], wsd[:, :],
                                              start=True, stop=True)
                    op.then_inc(y_ready, 1)

        @block.scalar
        def _(act):
            def keep_turned(b):
                act.wait_ge(t_ready, b + 1)
                wait_above_zero(act, l_ready, b - 1)
                if not shared:
                    wait_above_zero(act, low_kept, b - 1)
                nc.scalar.copy(xnt[:, b % 2, :, :], ps_t[:, :, :]).then_inc(xnt_ready, 1)

            keep_turned(0)
            for b in range(B):
                if b + 1 < B:
                    keep_turned(b + 1)
                if shared:
                    act.wait_ge(up_ready, b + 1)
                    wait_above_zero(act, hidden_ready, b)
                    nc.scalar.activation(gate[:, :], ps_g[0:F, 0, :], ACT.Silu).then_inc(gated, 1)
                else:
                    act.wait_ge(cut_done, b + 1)
                    nc.scalar.copy(c["xh"][:, :, b * S:(b + 1) * S], xnt_cut[:, :, :]).then_inc(high_kept, 1)
                act.wait_ge(l_ready, b + 1)
                nc.scalar.copy(c["logits"][:, b * (TB * experts):(b + 1) * (TB * experts)],
                               ps_l[:, :, :].rearrange("p t e -> p (t e)")).then_inc(l_out, 1)

        @block.gpsimd
        def _(pool):
            if not shared:
                for b in range(B):
                    pool.wait_ge(cut_done, b + 1)
                    nc.gpsimd.tensor_tensor(c["xl"][:, :, b * S:(b + 1) * S], xnt[:, b % 2, :, :], xnt_cut[:, :, :],
                                            ALU.subtract).then_inc(low_kept, 1)

        @block.vector
        def _(dve):
            def normalise(b):
                wait_above_zero(dve, t_ready, b - 1)
                if shared:
                    wait_above_zero(dve, rows_kept[b % 2], 16 * (b // 2))
                for t in range(TB):
                    at = b * TB + t
                    op = nc.vector.tensor_scalar(
                        xn[:, b % 2, t, :], c["resid"][:, at * H:(at + 1) * H], c["mean_var"][:, at * 2:at * 2 + 1],
                        c["rstd"][:, at:at + 1], ALU.subtract, ALU.mult)
                op.then_inc(xn_ready, 1)

            normalise(0)
            normalise(1)
            for b in range(B):
                if shared:
                    dve.wait_ge(gated, b + 1)
                    wait_above_zero(dve, y_ready, b)
                    nc.vector.tensor_tensor(hidden[:, :], gate[:, :], ps_g[0:F, 1, :], ALU.mult).then_inc(
                        hidden_ready, 1)
                else:
                    dve.wait_ge(xnt_ready, b + 1)
                    wait_above_zero(dve, high_kept, b)
                    wait_above_zero(dve, low_kept, b)
                    cut_bits(nc, xnt_cut[:, :, :], xnt[:, b % 2, :, :]).then_inc(cut_done, 1)
                if b + 2 < B:
                    normalise(b + 2)
                if shared:
                    dve.wait_ge(y_ready, b + 1)
                    r = c["resid"][:, b * (TB * H):(b + 1) * (TB * H)]
                    nc.vector.tensor_tensor(r, r, ps_y[:, :, :].rearrange("p t f -> p (t f)"),
                                            ALU.add).then_inc(y_added, 1)


def chosen_groups(nc, dve, step, gs, ge, gt, lower, keep, G, take):
    a = gs[:, :, :].unsqueeze(3).to_broadcast([P, NT, G, G])
    b = gs[:, :, :].unsqueeze(2).to_broadcast([P, NT, G, G])
    low = lower.unsqueeze(1).to_broadcast([P, NT, G, G])
    step(nc.vector.tensor_tensor(ge, b, a, ALU.is_ge))
    step(nc.vector.tensor_tensor(gt, b, a, ALU.is_gt))
    step(nc.vector.tensor_tensor(ge, ge, low, ALU.mult))
    step(nc.vector.tensor_tensor(gt, gt, ge, ALU.max))
    step(nc.vector.tensor_reduce(keep, gt, AX.X, ALU.add))
    step(nc.vector.tensor_scalar(keep, keep, float(take), NEG, ALU.is_ge, ALU.mult))


def cut_bits(nc, out, x):
    return nc.vector.tensor_scalar(out.bitcast(I32), x.bitcast(I32), HIGH_BITS, None, ALU.bitwise_and)


def dense_experts(nc, c, d):
    E, G, TOPG, K = 16, 4, 2, 4
    FT = c["FT"]
    ER = 32
    with ExitStack() as outer:
        def sbo(name, shape, dt=F32):
            return outer.enter_context(nc.sbuf_tensor(name, shape, dt))

        c["xh"], c["xl"] = sbo("xh", [P, KH, T], F32R), sbo("xl", [P, KH, T], F32R)
        c["logits"] = sbo("logits0", [P, NT * E])
        normalised_rows(nc, c, d, "l0", E)
        weights_t = sbo("weights_t", [3 * ER, T], BF16)
        NW = 5
        FW = FT // NW
        PARTS = ("w1", "w3", "w2")
        w_raw = {part: sbo(f"{part}_raw", [P, FW * H]) for part in PARTS}
        spread = sbo("spread_bf16", [3 * ER, FT * P], BF16)
        w_in = semaphore(nc, c, "w_in_e0")

        def load_weights(sp, g):
            for part in PARTS:
                sp.dma_start(w_raw[part][:, :], d[f"l0_{part}"][:, ds(g * (FW * H), FW * H)]).then_inc(w_in, 16)

        with ExitStack() as ctx:
            def sb(name, shape, dt=F32):
                return ctx.enter_context(nc.sbuf_tensor(f"{name}_r0", shape, dt))

            logit = c["logits"][:, :].rearrange("p (t e) -> p t e", e=E)
            key, sig = sb("key", [P, NT, E]), sb("sig", [P, NT, E])
            gs, keep = sb("gs", [P, NT, G]), sb("keep", [P, NT, G])
            ge, gt = sb("ge", [P, NT, G, G]), sb("gt", [P, NT, G, G])
            best, place = sb("best", [P, NT, 8]), sb("place", [P, NT, 8], U32)
            placef = sb("placef", [P, NT, 8])
            hot, mask = sb("hot", [P, K, NT, E]), sb("mask", [P, NT, E])
            total = sb("total", [P, NT, 1])
            weight = sb("weight", [P, NT, ER])
            rest = sb("rest", [P, NT, ER])
            wparts = sb("wparts", [P, NT, 3, ER], BF16)
            low, numbers = sb("low", [P, G, G]), sb("numbers", [P, E])
            spread_f = sb("spread_f", [3 * ER, FT * P])
            spread_in = semaphore(nc, c, "spread_in_r0")
            ps_w = ctx.enter_context(nc.psum_tensor("ps_w", [3 * ER, T], F32))
            tables_in, sigmoid_done, dve_step, split_done, turned, top_done, index_done = (
                semaphore(nc, c, x + "_r0") for x in (
                    "tables_in", "sigmoid_done", "dve_step", "split_done", "turned", "top_done", "index_done"))
            block = ctx.enter_context(nc.Block())

            @block.sync
            def _(sp):
                sp.dma_start(low[:, :, :], d["lower4"]).then_inc(tables_in, 16)
                sp.dma_start(numbers[:, :], d["numbers"][:, 0:E]).then_inc(tables_in, 16)
                sp.dma_start(spread_f[:, :], d["spread"]).then_inc(spread_in, 16)
                load_weights(sp, 0)

            @block.gpsimd
            def _(pool):
                pool.wait_ge(spread_in, 16)
                nc.gpsimd.tensor_copy(spread[:, :], spread_f[:, :])

            @block.scalar
            def _(act):
                nc.scalar.activation(sig[:, :, :], logit, ACT.Sigmoid).then_inc(sigmoid_done, 1)
                act.wait_ge(turned, 1)
                nc.scalar.copy(weights_t[:, :], ps_w[:, :])

            @block.vector
            def _(dve):
                count = [0]

                def step(op):
                    count[0] += 1
                    op.then_inc(dve_step, 1)
                    dve.wait_ge(dve_step, count[0])

                dve.wait_ge(tables_in, 32)
                step(nc.vector.tensor_scalar(key[:, :, :], logit, 17.0, None, ALU.min))
                step(nc.vector.tensor_reduce(gs[:, :, :], key[:, :, :].rearrange("p t (g e) -> p t g e", g=G), AX.X,
                                             ALU.max))
                chosen_groups(nc, dve, step, gs, ge[:, :, :, :], gt[:, :, :, :], low[:, :, :], keep[:, :, :], G, TOPG)
                step(nc.vector.tensor_tensor(key[:, :, :].rearrange("p t (g e) -> p t g e", g=G),
                                             key[:, :, :].rearrange("p t (g e) -> p t g e", g=G),
                                             keep[:, :, :].unsqueeze(3).to_broadcast([P, NT, G, E // G]), ALU.add))
                keys = key[:, :, :].rearrange("p t e -> p (t e)")
                bests = best[:, :, :].rearrange("p t e -> p (t e)")
                places = place[:, :, :].rearrange("p t e -> p (t e)")
                for t in range(NT):
                    nc.vector.max(bests[:, t * 8:t * 8 + 8], keys[:, t * E:(t + 1) * E]).then_inc(top_done, 1)
                dve.wait_ge(top_done, NT)
                for t in range(NT):
                    nc.vector.max_index(places[:, t * 8:t * 8 + 8], bests[:, t * 8:t * 8 + 8],
                                        keys[:, t * E:(t + 1) * E]).then_inc(index_done, 1)
                dve.wait_ge(index_done, NT)
                step(nc.vector.tensor_copy(placef[:, :, :], place[:, :, :]))
                for k in range(K):
                    op = nc.vector.tensor_tensor(hot[:, k, :, :], numbers[:, :].unsqueeze(1).to_broadcast([P, NT, E]),
                                                 placef[:, :, k:k + 1].to_broadcast([P, NT, E]), ALU.is_equal)
                step(op)
                step(nc.vector.tensor_tensor(hot[:, 0:2], hot[:, 0:2], hot[:, 2:4], ALU.add))
                step(nc.vector.tensor_tensor(mask[:, :, :], hot[:, 0], hot[:, 1], ALU.add))
                dve.wait_ge(sigmoid_done, 1)
                step(nc.vector.tensor_tensor(sig[:, :, :], sig[:, :, :], mask[:, :, :], ALU.mult))
                step(nc.vector.tensor_reduce(total[:, :, 0], sig[:, :, :], AX.X, ALU.add))
                step(nc.vector.reciprocal(total[:, :, :], total[:, :, :]))
                step(nc.vector.memset(weight[:, :, :], 0.0))
                step(nc.vector.tensor_tensor(weight[:, :, 0:E], sig[:, :, :],
                                             total[:, :, :].to_broadcast([P, NT, E]), ALU.mult))
                step(nc.vector.memset(weight[:, :, E:E + 1], 1.0))
                step(nc.vector.tensor_copy(wparts[:, :, 0, :], weight[:, :, :]))
                step(nc.vector.tensor_tensor(rest[:, :, :], weight[:, :, :], wparts[:, :, 0, :], ALU.subtract))
                step(nc.vector.tensor_copy(wparts[:, :, 1, :], rest[:, :, :]))
                nc.vector.tensor_tensor(wparts[:, :, 2, :], rest[:, :, :], wparts[:, :, 1, :],
                                        ALU.subtract).then_inc(split_done, 1)

            @block.tensor
            def _(pe):
                pe.wait_ge(split_done, 1)
                for t in range(NT):
                    op = nc.tensor.matmul(ps_w[:, t * P:(t + 1) * P], wparts[:, t, :, :].rearrange("p c e -> p (c e)"),
                                          c["masks"][:, 0, :], start=True, stop=True)
                op.then_inc(turned, 1)

        with ExitStack() as ctx:
            def sb(name, shape, dt=F32):
                return ctx.enter_context(nc.sbuf_tensor(f"{name}_e0", shape, dt))

            def sem(name):
                return semaphore(nc, c, f"{name}_e0")

            STEPS = B * FW
            parts = PARTS
            w_cut = {part: sb(f"{part}_cut", [P, FW * H]) for part in parts}
            w_low = {part: sb(f"{part}_low", [P, 2, FW * H], F32R) for part in parts}
            w_high = {part: sb(f"{part}_high", [P, 2, FW * H], F32R) for part in parts}
            gate, product, hidden = sb("gate", [P, 2, S]), sb("product", [P, 2, S]), sb("hidden", [P, 2, S])
            hidden_cut = sb("hidden_cut", [P, 2, S])
            hidden_high, hidden_low = sb("hidden_high", [P, 2, S], F32R), sb("hidden_low", [P, 2, S], F32R)
            zero = sb("zero", [P, 6 * H])
            ps_g = ctx.enter_context(nc.psum_tensor("ps_g_e0", [P, 2, S], F32))
            ps_u = ctx.enter_context(nc.psum_tensor("ps_u_e0", [P, 2, S], F32))
            ps_w = ctx.enter_context(nc.psum_tensor("ps_w_e0", [P, 2, S], F32))
            ps_y = ctx.enter_context(nc.psum_tensor("ps_y_e0", [P, TB, H], F32))
            cut_done, high_ready, low_ready, first_low_ready, zero_set, zeros_out = (
                sem(x) for x in ("cut_done", "high_ready", "low_ready", "first_low_ready", "zero_set", "zeros_out"))
            up_ready, gated, multiplied, weighted, hidden_cut_done, hidden_high_done, hidden_low_done = (
                sem(x) for x in ("up_ready", "gated", "multiplied", "weighted", "hidden_cut_done",
                                 "hidden_high_done", "hidden_low_done"))
            down_done, added = sem("down_done"), sem("added")
            FREE = 2
            FREE_Y = 1
            CUT_AT = (6, 11, 16)
            block = ctx.enter_context(nc.Block())

            def low_count(g):
                return g * 3 + 2

            def over_groups(eng, group):
                with eng.Fori(0, NW // 2) as i:
                    group(i * 2, 0, False)
                    group(i * 2 + 1, 1, False)
                group(NW - 1, 0, True)

            @block.sync
            def _(sp):
                for g in range(NW - 1):
                    if g == 0:
                        sp.wait_ge(first_low_ready, 1)
                    sp.wait_ge(low_ready, low_count(g))
                    load_weights(sp, g + 1)
                    if g == 0:
                        sp.wait_ge(zero_set, 1)
                        for t in range(NT):
                            sp.dma_start(d["y6_d"][t * P * 6:(t + 1) * P * 6, :].rearrange("(p k) f -> p (k f)", k=6),
                                         zero[:, :]).then_inc(zeros_out, 16)
                sp.wait_ge(zeros_out, 16 * NT)

            @block.gpsimd
            def _(pool):
                for g in range(NW):
                    for n, part in enumerate(parts):
                        if g == n == 0:
                            continue
                        pool.wait_ge(cut_done, 3 * g + n + 1)
                        nc.gpsimd.tensor_tensor(w_low[part][:, g % 2, :], w_raw[part][:, :], w_cut[part][:, :],
                                                ALU.subtract).then_inc(low_ready, 1)
                    if g == 0:
                        nc.gpsimd.memset(zero[:, :], 0.0).then_inc(zero_set, 1)

            @block.tensor
            def _(pe):
                pe.sem_inc(down_done, FREE)

                def up(g, s, n):
                    cc, f, p = n // FW, n % FW, n % 2
                    rows = slice(cc * S, (cc + 1) * S)
                    if n == 0 and isinstance(g, int) and g == 0:
                        pe.wait_ge(first_low_ready, 1)
                        pe.wait_ge(low_ready, 1)
                        pe.wait_ge(high_ready, 2)
                    elif n == 0:
                        pe.wait_ge(low_ready, low_count(g))
                        pe.wait_ge(high_ready, (g + 1) * 3)
                    pe.wait_ge(weighted, g * STEPS + (n + 1))
                    for ps, part in ((ps_g, "w1"), (ps_u, "w3")):
                        for k in range(KH):
                            col = slice(f * H + k * P, f * H + (k + 1) * P)
                            high, low = w_high[part][:, s, col], w_low[part][:, s, col]
                            for m, (w, x) in enumerate(((high, c["xh"]), (high, c["xl"]), (low, c["xh"]))):
                                nc.tensor.matmul(ps[:, p, :], w, x[:, k, rows], start=k == m == 0,
                                                 stop=k == KH - 1 and m == 2)
                    nc.tensor.matmul(ps_w[:, p, :], spread[:, ds(g * (FW * P) + f * P, P)],
                                     weights_t[:, rows], start=True, stop=True).then_inc(up_ready, 1)

                def down(g, s, n):
                    f, p = n % FW, n % 2
                    pe.wait_ge(hidden_high_done, g * STEPS + (n + 1))
                    pe.wait_ge(hidden_low_done, g * STEPS + (n + 1))
                    if f == 0:
                        pe.wait_ge(added, g * B + (n // FW + FREE_Y))
                    for t in range(TB):
                        tok = slice(t * P, (t + 1) * P)
                        high, low = hidden_high[:, p, tok], hidden_low[:, p, tok]
                        for m, (h, w) in enumerate(((high, w_high), (high, w_low), (low, w_high))):
                            op = nc.tensor.matmul(ps_y[:, t, :], h, w["w2"][:, s, f * H:(f + 1) * H],
                                                  start=f == m == t % 2 == 0, stop=f == FW - 1 and m == 2,
                                                  skip_group_check=True)
                    op.then_inc(down_done, 1)

                def group(g, s, last):
                    for n in range(STEPS):
                        if n + 2 < STEPS:
                            up(g, s, n + 2)
                        elif not last:
                            up(g + 1, 1 - s, n + 2 - STEPS)
                        down(g, s, n)

                up(0, 0, 0)
                up(0, 0, 1)
                pe.wait_ge(low_ready, low_count(0))
                pe.wait_ge(high_ready, 3)
                over_groups(pe, group)

            @block.scalar
            def _(act):
                def group(g, s, last):
                    for n in range(STEPS):
                        act.wait_ge(up_ready, g * STEPS + (n + 1))
                        act.wait_ge(multiplied, g * STEPS + (n + 1))
                        nc.scalar.activation(gate[:, n % 2, :], ps_g[:, n % 2, :], ACT.Silu).then_inc(gated, 1)
                        act.wait_ge(hidden_cut_done, g * STEPS + (n + 1))
                        act.wait_ge(down_done, g * STEPS + (n + 1))
                        nc.scalar.copy(hidden_high[:, n % 2, :], hidden_cut[:, n % 2, :]).then_inc(hidden_high_done, 1)
                        if n - 1 in CUT_AT and not last:
                            high(g + 1, 1 - s, CUT_AT.index(n - 1))

                def high(g, s, part):
                    act.wait_ge(cut_done, g * 3 + (part + 1))
                    nc.scalar.copy(w_high[parts[part]][:, s, :], w_cut[parts[part]][:, :]).then_inc(high_ready, 1)

                for part in range(3):
                    high(0, 0, part)
                over_groups(act, group)

            @block.vector
            def _(dve):
                dve.sem_inc(multiplied, FREE)
                dve.sem_inc(weighted, FREE)
                dve.sem_inc(added, FREE_Y)

                def cut(g, part):
                    name = parts[part]
                    if part == 0:
                        dve.wait_ge(w_in, (g + 1) * 48)
                    if not (isinstance(g, int) and g == 0):
                        dve.wait_ge(high_ready, g * 3)
                    cut_bits(nc, w_cut[name][:, :], w_raw[name][:, :]).then_inc(cut_done, 1)

                def hide(g, n):
                    p, done = n % 2, g * STEPS + (n + 1)
                    dve.wait_ge(gated, done)
                    nc.vector.tensor_tensor(product[:, p, :], gate[:, p, :], ps_u[:, p, :], ALU.mult).then_inc(
                        multiplied, 1)
                    dve.wait_ge(multiplied, g * STEPS + (n + 1 + FREE))
                    nc.vector.tensor_tensor(hidden[:, p, :], product[:, p, :], ps_w[:, p, :], ALU.mult).then_inc(
                        weighted, 1)
                    dve.wait_ge(weighted, g * STEPS + (n + 1 + FREE))
                    dve.wait_ge(down_done, done)
                    cut_bits(nc, hidden_cut[:, p, :], hidden[:, p, :]).then_inc(hidden_cut_done, 1)
                    dve.wait_ge(hidden_cut_done, done)
                    nc.vector.tensor_tensor(hidden_low[:, p, :], hidden[:, p, :], hidden_cut[:, p, :],
                                            ALU.subtract).then_inc(hidden_low_done, 1)

                def group(g, s, last):
                    for n in range(STEPS):
                        cc, f = n // FW, n % FW
                        if n + 1 < STEPS:
                            hide(g, n + 1)
                        elif not last:
                            hide(g + 1, 0)
                        if f == FW - 1:
                            dve.wait_ge(down_done, g * STEPS + (n + 1 + FREE))
                            r = c["resid"][:, cc * TB * H:(cc + 1) * TB * H]
                            nc.vector.tensor_tensor(r, r, ps_y[:, :, :].rearrange("p t f -> p (t f)"),
                                                    ALU.add).then_inc(added, 1)
                            if last:
                                dve.wait_ge(added, g * B + cc + 1 + FREE_Y)
                                row_statistics(nc, c, cc)
                        if n in CUT_AT and not last:
                            cut(g + 1, CUT_AT.index(n))

                for part in range(3):
                    cut(0, part)
                dve.wait_ge(cut_done, 1)
                nc.vector.tensor_tensor(w_low[parts[0]][:, 0, :], w_raw[parts[0]][:, :], w_cut[parts[0]][:, :],
                                        ALU.subtract).then_inc(first_low_ready, 1)
                hide(0, 0)
                over_groups(dve, group)


def sparse_experts(nc, c, d):
    E, G, TOPG, K, F = 64, 8, 4, 6, 96
    CAP, SLOTS = 2 * (256 * K // E), 64
    PAIRS = E // 2
    with ExitStack() as outer:
        def sbo(name, shape, dt=F32):
            return outer.enter_context(nc.sbuf_tensor(name, shape, dt))

        c["logits"] = sbo("logits1", [P, NT * E])
        normalised_rows(nc, c, d, "l1", E)
        gather_at = sbo("gather_at", [P, PAIRS], I32)
        scatter_at = sbo("scatter_at", [P, PAIRS], I32)
        wk = sbo("wk", [P, NT, K])
        sig = sbo("sig_r1", [P, NT, E])
        hot = sbo("hot_r1", [P, K, NT, E], BF16)
        mask, seated = sbo("mask_r1", [P, NT, E], BF16), sbo("seated_r1", [P, NT, E], BF16)
        RING = 16
        w_up = [sbo(f"w_up{u}", [P, 2, KH, 2 * F]) for u in range(RING)]
        w_down = [sbo(f"w_down{u}", [F, 2, H]) for u in range(RING)]
        w_in = [semaphore(nc, c, f"w_in{u}_p1") for u in range(RING)]

        def load_weights(sp, i, u):
            sp.dma_start(w_up[u][:, :, :, :], d["l1_w_up"][ds(i * RING + u, 1)].rearrange(
                "o p a k f -> (o p) a k f")).then_inc(w_in[u], 16)
            sp.dma_start(w_down[u][:, :, :], d["l1_w_down"][ds(i * RING + u, 1)].rearrange(
                "o p a f -> (o p) a f")).then_inc(w_in[u], 16)

        with ExitStack() as ctx:
            def sb(name, shape, dt=F32):
                return ctx.enter_context(nc.sbuf_tensor(f"{name}_r1", shape, dt))

            logit = c["logits"][:, :].rearrange("p (t e) -> p t e", e=E)
            bias, numbers = sb("bias", [P, E]), sb("numbers", [P, E])
            low, pnum, tnum = sb("low", [P, G, G]), sb("pnum", [P, 1]), sb("tnum", [P, NT])
            tanh, key = sb("tanh", [P, NT, E]), sb("key", [P, NT, E])
            work = sb("work", [P, NT, E])
            gs, keep, second = sb("gs", [P, NT, G]), sb("keep", [P, NT, G]), sb("second", [P, NT, G])
            ge, gt = sb("ge", [P, NT, G, G]), sb("gt", [P, NT, G, G])
            best, place = sb("best", [P, NT, 8]), sb("place", [P, NT, 8], U32)
            placef = sb("placef", [P, NT, 8])
            before = sb("before", [P, NT, E], BF16)
            seat, chosen = sb("seat", [P, NT, E], BF16), sb("chosen", [P, NT, E], BF16)
            ck = sb("ck", [P, NT, 1])
            values = sb("values", [P, K, NT, 3, E], BF16)
            seats = sb("seats", [P, 2, NT, SLOTS], BF16)
            table = sb("table", [P, 3, E])
            ps_p = ctx.enter_context(nc.psum_tensor("ps_p", [P, NT, E], F32))
            ps_s = ctx.enter_context(nc.psum_tensor("ps_s_r1", [P, 512], F32))
            tables_in, scores_done, dve_step, top_done, index_done, before_done, places_done, seats_ready, used = (
                semaphore(nc, c, x + "_r1") for x in (
                    "tables_in", "scores_done", "dve_step", "top_done", "index_done", "before_done", "places_done",
                    "seats_ready", "used"))
            hot_ready, values_ready = semaphore(nc, c, "hot_ready_r1"), semaphore(nc, c, "values_ready_r1")
            block = ctx.enter_context(nc.Block())

            @block.sync
            def _(sp):
                sp.dma_start(low[:, :, :], d["lower8"]).then_inc(tables_in, 16)
                sp.dma_start(numbers[:, :], d["numbers"]).then_inc(tables_in, 16)
                sp.dma_start(pnum[:, :], d["pnum"]).then_inc(tables_in, 16)
                sp.dma_start(tnum[:, :], d["numbers"][:, 0:NT]).then_inc(tables_in, 16)
                sp.dma_start(bias[:, :], d["l1_bias"].rearrange("(a n) -> a n", a=1).to_broadcast([P, E])).then_inc(
                    tables_in, 16)
                for u in range(RING):
                    load_weights(sp, 0, u)

            @block.scalar
            def _(act):
                nc.scalar.activation(sig[:, :, :], logit, ACT.Sigmoid).then_inc(scores_done, 1)
                nc.scalar.activation(tanh[:, :, :], logit, ACT.Tanh, scale=0.5).then_inc(scores_done, 1)

            @block.vector
            def _(dve):
                count = [0]

                def step(op):
                    count[0] += 1
                    op.then_inc(dve_step, 1)
                    dve.wait_ge(dve_step, count[0])

                tt, tsc = nc.vector.tensor_tensor, nc.vector.tensor_scalar
                all_ = (slice(None),) * 3
                dve.wait_ge(tables_in, 16 * 5)
                dve.wait_ge(scores_done, 2)
                step(tsc(tanh[all_], tanh[all_], 0.5, 0.5, ALU.mult, ALU.add))
                stt = nc.vector.scalar_tensor_tensor
                stt(work[all_], logit, -2.0, sig[all_], ALU.is_le, ALU.mult)
                step(stt(tanh[all_], logit, -2.0, tanh[all_], ALU.is_gt, ALU.mult))
                step(tt(sig[all_], tanh[all_], work[all_], ALU.add))
                step(tt(key[all_], sig[all_], bias[:, :].unsqueeze(1).to_broadcast([P, NT, E]), ALU.add))

                def grouped(x):
                    return x[all_].rearrange("p t (g e) -> p t g e", g=G)

                def spread(x):
                    return x[all_].unsqueeze(3).to_broadcast([P, NT, G, E // G])

                step(nc.vector.tensor_reduce(gs[all_], grouped(key), AX.X, ALU.max))
                step(tt(grouped(work), grouped(key), spread(gs), ALU.is_equal))
                step(nc.vector.tensor_reduce(keep[all_], grouped(work), AX.X, ALU.add))
                step(stt(work[all_], work[all_], NEG, key[all_], ALU.mult, ALU.add))
                step(nc.vector.tensor_reduce(second[all_], grouped(work), AX.X, ALU.max))
                step(tsc(keep[all_], keep[all_], 2.0, NEG, ALU.is_lt, ALU.mult))
                step(tt(keep[all_], keep[all_], gs[all_], ALU.add))
                step(tt(second[all_], second[all_], keep[all_], ALU.max))
                step(tt(gs[all_], gs[all_], second[all_], ALU.add))
                chosen_groups(nc, dve, step, gs, ge[:, :, :, :], gt[:, :, :, :], low[all_], keep[all_], G, TOPG)
                step(tt(grouped(key), grouped(key), spread(keep), ALU.add))
                keys = key[all_].rearrange("p t e -> p (t e)")
                bests = best[all_].rearrange("p t e -> p (t e)")
                places = place[all_].rearrange("p t e -> p (t e)")
                for t in range(NT):
                    nc.vector.max(bests[:, t * 8:t * 8 + 8], keys[:, t * E:(t + 1) * E]).then_inc(top_done, 1)
                dve.wait_ge(top_done, NT)
                for t in range(NT):
                    nc.vector.max_index(places[:, t * 8:t * 8 + 8], bests[:, t * 8:t * 8 + 8],
                                        keys[:, t * E:(t + 1) * E]).then_inc(index_done, 1)
                dve.wait_ge(index_done, NT)
                step(nc.vector.tensor_copy(placef[all_], place[all_]))
                for k in range(K):
                    op = tt(hot[:, k, :, :], numbers[:, :].unsqueeze(1).to_broadcast([P, NT, E]),
                            placef[:, :, k:k + 1].to_broadcast([P, NT, E]), ALU.is_equal)
                step(op)
                dve.sem_inc(hot_ready, 1)
                step(tt(hot_a := chosen[all_], hot[:, 0], hot[:, 1], ALU.add))
                for k in range(2, K - 1):
                    step(tt(hot_a, hot_a, hot[:, k], ALU.add))
                step(tt(mask[all_], hot_a, hot[:, K - 1], ALU.add))
                step(nc.vector.memset(before[:, 0, :], 0.0))
                for t in range(1, NT):
                    step(tt(before[:, t, :], before[:, t - 1, :], mask[:, t - 1, :], ALU.add))
                dve.sem_inc(before_done, 1)
                dve.wait_ge(places_done, 1)
                nc.vector.tensor_scalar(seated[all_], ps_p[all_], float(CAP), None, ALU.is_lt)
                step(tsc(seat[all_], ps_p[all_], float(CAP), None, ALU.min))
                step(tsc(chosen[all_], ps_p[all_], float(CAP), 16.0, ALU.is_ge, ALU.mult))
                step(tt(seat[all_], seat[all_], chosen[all_], ALU.add))
                for k in range(K):
                    s = k % 2
                    if k >= 2:
                        dve.wait_ge(used, k - 1)
                    step(tt(chosen[all_], seat[all_], hot[:, k], ALU.mult))
                    step(nc.vector.tensor_reduce(ck[:, :, 0], chosen[all_], AX.X, ALU.add))
                    tt(seats[:, s], numbers[:, :].unsqueeze(1).to_broadcast([P, NT, SLOTS]),
                       ck[all_].to_broadcast([P, NT, SLOTS]), ALU.is_equal).then_inc(seats_ready, 1)
                dve.wait_ge(used, K)
                step(nc.vector.tensor_copy(table[all_], ps_s[:, 0:3 * E].rearrange("p (c e) -> p c e", c=3)))
                step(nc.vector.scalar_tensor_tensor(table[:, 1], table[:, 1], float(P), table[:, 0], ALU.mult, ALU.add))
                step(nc.vector.scalar_tensor_tensor(table[:, 0], table[:, 1], float(K), table[:, 2], ALU.mult, ALU.add))
                step(tsc(table[:, 2], table[:, 2], 0.5, 65536.0, ALU.is_lt, ALU.mult))
                step(nc.vector.scalar_tensor_tensor(table[:, 0], table[:, 0], -1.0, table[:, 2], ALU.add, ALU.add))
                step(tsc(table[:, 0], table[:, 0], 0.0, None, ALU.max))
                for half in range(2):
                    rows = slice(half * SLOTS, (half + 1) * SLOTS)
                    for dst, i in ((gather_at, 1), (scatter_at, 0)):
                        src = table[rows, i, :].rearrange("p (n h) -> p n h", h=2)[:, :, half]
                        step(nc.vector.tensor_copy(dst[rows, :], src))

            @block.gpsimd
            def _(pool):
                pool.wait_ge(hot_ready, 1)
                for k in range(K):
                    number = numbers[:, k + 1:k + 2]
                    for i, factor in enumerate((pnum[:, 0:1].unsqueeze(2), tnum[:, :].unsqueeze(2),
                                                number.unsqueeze(2))):
                        nc.gpsimd.tensor_tensor(values[:, k, :, i, :], hot[:, k], factor.to_broadcast([P, NT, E]),
                                                ALU.mult).then_inc(values_ready, 1)

            @block.tensor
            def _(pe):
                pe.wait_ge(before_done, 1)
                for t in range(NT):
                    nc.tensor.matmul(ps_p[:, t, :], c["masks"][:, 3, :], mask[:, t, :], start=True, stop=False)
                    op = nc.tensor.matmul(ps_p[:, t, :], c["masks"][:, 4, :], before[:, t, :], start=False, stop=True)
                op.then_inc(places_done, 1)
                for k in range(K):
                    pe.wait_ge(seats_ready, k + 1)
                    pe.wait_ge(values_ready, 3 * (k + 1))
                    for t in range(NT):
                        for half in range(2):
                            op = nc.tensor.matmul(ps_s[half * SLOTS:(half + 1) * SLOTS, 0:3 * E], seats[:, k % 2, t, :],
                                                  values[:, k, t, :, :].rearrange("p c e -> p (c e)"),
                                                  start=k == 0 and t == 0, stop=k == K - 1 and t == NT - 1)
                    op.then_inc(used, 1)

        expert_pairs(nc, c, d, gather_at, scatter_at, w_up, w_down, w_in, load_weights, (sig, hot, mask, seated), wk)
        combine(nc, c, d, wk)


def expert_pairs(nc, c, d, gather_at, scatter_at, w_up, w_down, w_in, load_weights, choices, wk):
    PAIRS, SLOTS, F, U = 32, 64, 96, len(w_up)
    E, TOPK, SCALE = 64, 6, 2.5
    with ExitStack() as ctx:
        def sb(name, shape, dt=F32):
            return ctx.enter_context(nc.sbuf_tensor(f"{name}_p1", shape, dt))

        def sem(name):
            return semaphore(nc, c, f"{name}_p1")

        rows = [sb(f"rows{u}", [P, H]) for u in range(U)]
        rows_t = sb("rows_t", [P, 2, KH, P])
        gate, hidden, hidden_t = sb("gate", [P, 2, F]), sb("hidden", [P, 2, F]), sb("hidden_t", [F, 2, P])
        result = [sb(f"result{u}", [P, H]) for u in range(U)]
        ps_x = [ctx.enter_context(nc.psum_tensor(f"ps_x{i}", [P, KH, P], F32)) for i in range(2)]
        ps_h = [ctx.enter_context(nc.psum_tensor(f"ps_h{i}", [P, 2 * F], F32)) for i in range(2)]
        ps_t = [ctx.enter_context(nc.psum_tensor(f"ps_ht{i}", [F, P], F32)) for i in range(2)]
        ps_o = [ctx.enter_context(nc.psum_tensor(f"ps_o{i}", [P, H], F32)) for i in range(2)]
        gathered = [sem(f"gathered{u}") for u in range(U)]
        scattered = [sem(f"scattered{u}") for u in range(U)]
        total, work = sb("total", [P, NT, 1]), sb("work", [P, NT, E])
        weight_step = sem("weight_step")
        x_turned, x_copied, up_done, gated, hidden_done, h_turned, h_copied, down_done, result_done = (
            sem(x) for x in ("x_turned", "x_copied", "up_done", "gated", "hidden_done", "h_turned", "h_copied",
                             "down_done", "result_done"))
        block = ctx.enter_context(nc.Block())

        def steps(eng, one, lag, beside=None):
            for u in range(U):
                for j in range(lag + 1):
                    if u - j >= 0:
                        one(0, u - j, j, u - j)
                if beside is not None and u % 2 == 1 and u < 2 * TOPK:
                    beside(u // 2)
            with eng.Fori(1, PAIRS // U) as i:
                for u in range(U):
                    for j in range(lag + 1):
                        one(i if u >= j else i - 1, (u - j) % U, j, 99)
            for u in range(lag):
                for j in range(u + 1, lag + 1):
                    one(PAIRS // U - 1, U + u - j, j, 99)

        @block.sync
        def _(sp):
            with sp.Fori(1, PAIRS // U) as i:
                for u in range(U):
                    sp.wait_ge(down_done, i * U + (u - (U - 1)))
                    load_weights(sp, i, u)

        @block.gpsimd
        def _(pool):
            def gather(n):
                wait_above_zero(pool, x_turned, n - (U - 1))
                pool.indirect_dma_start(rows[n % U][:, :], None, d["xn_d"],
                                        bass.IndirectOffsetOnAxis(ap=gather_at[:, n:n + 1], axis=0)).then_inc(
                    gathered[n % U], 16)

            def scatter(n):
                pool.wait_ge(result_done, n + 1)
                wait_above_zero(pool, scattered[n % U], n // U * 16)
                pool.indirect_dma_start(d["y6_d"], bass.IndirectOffsetOnAxis(ap=scatter_at[:, n:n + 1], axis=0),
                                        result[n % U][:, :], None, bounds_check=T * 6 - 1,
                                        oob_is_err=False).then_inc(scattered[n % U], 16)

            LAG = 12
            for n in range(PAIRS):
                gather(n)
                if n >= LAG:
                    scatter(n - LAG)
            for n in range(PAIRS - LAG, PAIRS):
                scatter(n)
            for u in range(U):
                pool.wait_ge(scattered[u], 16 * (PAIRS // U))

        @block.tensor
        def _(pe):
            def one(i, u, j, known):
                n, s = i * U + u, u % 2
                if j == 0:
                    pe.wait_ge(gathered[u], (i + 1) * 16)
                    if known >= 2:
                        pe.wait_ge(x_copied, n - 1)
                    for k in range(KH):
                        op = nc.tensor.transpose(ps_x[s][:, k, :], rows[u][:, k * P:(k + 1) * P], c["ident"][:, :])
                    op.then_inc(x_turned, 1)
                if j == 1:
                    pe.wait_ge(x_copied, n + 1)
                    pe.wait_ge(w_in[u], (i + 1) * 32)
                    if known >= 2:
                        pe.wait_ge(hidden_done, n - 1)
                    for k in range(KH):
                        for a in range(2):
                            op = nc.tensor.matmul(ps_h[s][a * SLOTS:(a + 1) * SLOTS, :],
                                                  rows_t[:, s, k, a * SLOTS:(a + 1) * SLOTS], w_up[u][:, a, k, :],
                                                  start=k == 0, stop=k == KH - 1)
                    op.then_inc(up_done, 1)
                if j == 2:
                    pe.wait_ge(hidden_done, n + 1)
                    if known >= 2:
                        pe.wait_ge(h_copied, n - 1)
                    nc.tensor.transpose(ps_t[s][:, :], hidden[:, s, :], c["ident"][:, :]).then_inc(h_turned, 1)
                if j == 3:
                    pe.wait_ge(h_copied, n + 1)
                    if known >= 2:
                        pe.wait_ge(result_done, n - 1)
                    for a in range(2):
                        op = nc.tensor.matmul(ps_o[s][a * SLOTS:(a + 1) * SLOTS, :],
                                              hidden_t[:, s, a * SLOTS:(a + 1) * SLOTS], w_down[u][:, a, :],
                                              start=True, stop=True)
                    op.then_inc(down_done, 1)

            steps(pe, one, 3)

        @block.scalar
        def _(act):
            def one(i, u, j, known):
                n, s = i * U + u, u % 2
                if j == 0:
                    act.wait_ge(x_turned, n + 1)
                    if known >= 2:
                        act.wait_ge(up_done, n - 1)
                    nc.scalar.copy(rows_t[:, s, :, :], ps_x[s][:, :, :]).then_inc(x_copied, 1)
                if j == 1:
                    act.wait_ge(up_done, n + 1)
                    if known >= 2:
                        act.wait_ge(hidden_done, n - 1)
                    nc.scalar.activation(gate[:, s, :], ps_h[s][:, 0:F], ACT.Silu).then_inc(gated, 1)

            steps(act, one, 1)

        @block.vector
        def _(dve):
            def one(i, u, j, known):
                n, s = i * U + u, u % 2
                if j == 0:
                    dve.wait_ge(gated, n + 1)
                    if known >= 2:
                        dve.wait_ge(h_turned, n - 1)
                    nc.vector.tensor_tensor(hidden[:, s, :], gate[:, s, :], ps_h[s][:, F:2 * F], ALU.mult).then_inc(
                        hidden_done, 1)
                if j == 1:
                    dve.wait_ge(h_turned, n + 1)
                    if known >= 2:
                        dve.wait_ge(down_done, n - 1)
                    nc.vector.tensor_copy(hidden_t[:, s, :], ps_t[s][:, :]).then_inc(h_copied, 1)
                if j == 2:
                    dve.wait_ge(down_done, n + 1)
                    if known >= U:
                        dve.wait_ge(scattered[u], i * 16)
                    nc.vector.tensor_copy(result[u][:, :], ps_o[s][:, :]).then_inc(result_done, 1)

            sig, hot, mask, seated = choices
            tt, all_ = nc.vector.tensor_tensor, (slice(None),) * 3
            count = [0]

            def step(op):
                count[0] += 1
                op.then_inc(weight_step, 1)
                dve.wait_ge(weight_step, count[0])

            def scale_weights():
                step(tt(sig[all_], sig[all_], mask[all_], ALU.mult))
                step(nc.vector.tensor_reduce(total[:, :, 0], sig[all_], AX.X, ALU.add))
                step(nc.vector.reciprocal(total[all_], total[all_]))
                step(tt(sig[all_], sig[all_], total[all_].to_broadcast([P, NT, E]), ALU.mult))
                step(nc.vector.scalar_tensor_tensor(sig[all_], sig[all_], SCALE, seated[all_], ALU.mult, ALU.mult))

            def weight_of_choice(k):
                step(tt(work[all_], sig[all_], hot[:, k], ALU.mult))
                step(nc.vector.tensor_reduce(wk[:, :, k], work[all_], AX.X, ALU.add))

            scale_weights()
            steps(dve, one, 2, weight_of_choice)


def combine(nc, c, d, wk):
    K = 6
    with ExitStack() as ctx:
        R, M = 8, 2
        y = ctx.enter_context(nc.sbuf_tensor("y_choices", [P, R, K, H], F32))
        y_in = [semaphore(nc, c, f"y_in{r}") for r in range(R)]
        y_added = semaphore(nc, c, "y_added")
        stored = semaphore(nc, c, "out_stored")
        block = ctx.enter_context(nc.Block())

        @block.sync
        def _(sp):
            def load(t, r):
                sp.dma_start(y[:, r, :, :].rearrange("p k f -> p (k f)"),
                             d["y6_d"][t * P * K:(t + 1) * P * K, :].rearrange("(p k) f -> p (k f)", k=K)).then_inc(
                    y_in[r], 16)

            for t in range(NT):
                if t >= R and t % M == 0:
                    sp.wait_ge(y_added, (t - R + M) * K)
                load(t, t % R)

        @block.vector
        def _(dve):
            for q in range(NT // M):
                for k in range(K):
                    for t in range(q * M, (q + 1) * M):
                        if k == 0:
                            dve.wait_ge(y_in[t % R], (t // R + 1) * 16)
                        else:
                            dve.wait_ge(y_added, q * M * K + (k - 1) * M + t % M + 1)
                        x = c["resid"][:, t * H:(t + 1) * H]
                        nc.vector.scalar_tensor_tensor(x, y[:, t % R, k, :], wk[:, t, k:k + 1], x, ALU.mult,
                                                       ALU.add).then_inc(y_added, 1)

        @block.scalar
        def _(act):
            for q in range(NT // M):
                act.wait_ge(y_added, (q + 1) * M * K)
                act.dma_start(d["out"][q * M * P:(q + 1) * M * P, :].rearrange("(t p) f -> p t f", p=P),
                              c["resid"][:, q * M * H:(q + 1) * M * H].rearrange("p (t f) -> p t f", f=H)).then_inc(
                    stored, 16)
            act.wait_ge(stored, 16 * (NT // M))


def build(nc, d):
    for L in (L0, L1):
        d[f"{L.name}_qd"] = nc.dram_tensor(f"{L.name}_qd", [3, L.blocks, L.d, HB, S], BF16, kind="Internal").ap()
        d[f"{L.name}_kd"] = nc.dram_tensor(f"{L.name}_kd", [3, L.blocks, L.d, L.kv_of_block, S], BF16,
                                           kind="Internal").ap()
        d[f"{L.name}_vd"] = nc.dram_tensor(f"{L.name}_vd", [L.groups, S, L.vw], F32, kind="Internal").ap()
        d[f"{L.name}_od"] = nc.dram_tensor(f"{L.name}_od", [L.groups * P, S], F32, kind="Internal").ap()
    d["inverse_d"] = nc.dram_tensor("inverse_d", [P, S], F32, kind="Internal").ap()
    d["xn_d"] = nc.dram_tensor("xn_d", [T, H], F32, kind="Internal").ap()
    d["y6_d"] = nc.dram_tensor("y6_d", [T * 6, H], F32, kind="Internal").ap()
    d["neg_d"] = nc.dram_tensor("neg_d", [4, P, 4 * HQ * TB], BF16, kind="Internal").ap()
    with ExitStack() as ctx:
        def sb(name, shape, dt=F32):
            return ctx.enter_context(nc.sbuf_tensor(name, shape, dt))

        c = {
            "semaphores": [], "resid": sb("resid_f32", [P, NT * H]),
            "mean_var": sb("mean_var", [P, NT * 2]), "rstd": sb("rstd", [P, NT]),
            "stats": sb("stats", [P, NT * 6]),
            "masks": sb("masks_bf16", [P, 5, P], BF16), "ident": sb("ident_f32", [P, P]), "bo": sb("bo", [P, H]),
        }
        c["FT"] = d["l0_w2"].shape[1] // H
        load_constants(nc, c, d)
        for L in (L0, L1):
            layernorm_statistics(nc, c, f"a{L.name}")
            with ExitStack() as results:
                for x, shape in (("wo", [P, KH, H]), ("num", [P, B, KH, S]), ("inverse", [P, B, KH, S])):
                    c[x] = results.enter_context(nc.sbuf_tensor(f"{x}_{L.name}_sb", shape, F32))
                with ExitStack() as operands:
                    for x, shape in (("q", [P, HQ, S]), ("k", [P, L.kv_of_group * S])):
                        c[x] = [operands.enter_context(nc.sbuf_tensor(f"{x}{u}_{L.name}", shape, BF16))
                                for u in range(4)]
                    project(nc, c, d, L)
                    attend(nc, c, d, L)
                join(nc, c, d, L)
            if L is L0:
                layernorm_statistics(nc, c, "f0")
                dense_experts(nc, c, d)
                retire_semaphores(nc, c)
            else:
                retire_semaphores(nc, c)
                layernorm_statistics(nc, c, "f1")
                sparse_experts(nc, c, d)


def shape_constants():
    half = L0.d // 2
    inv = np.float32(1.0) / (np.float32(10000.0) ** (np.arange(half, dtype=np.float32) / np.float32(half)))
    freq = (np.arange(S, dtype=np.float32)[:, None] * inv[None, :].astype(np.float32)).astype(np.float64)
    dim = (np.arange(P) % L0.d) // 2
    sign = np.where(np.arange(P) % 2 == 0, -1.0, 1.0)[:, None]
    cos = np.cos(freq).T[dim].astype(np.float32)
    sin = (np.sin(freq).T[dim] * sign).astype(np.float32)
    i = np.arange(P)
    masks = np.zeros((P, 5, P), np.float32)
    masks[:, 0] = i[:, None] == i[None, :]
    masks[:, 1] = np.where(i[None, :] > i[:, None], NEG, 0)
    masks[:, 2] = np.where(i[:, None] > i[None, :], NEG, 0)
    masks[:, 3] = i[:, None] < i[None, :]
    masks[:, 4] = 1
    expert = np.minimum(np.arange(25 * P) // 176, 16)
    spread = np.zeros((3, 32, 25 * P), np.float32)
    spread[:, expert, np.arange(25 * P)] = 1

    def lower(n):
        x = np.arange(n)[None, :] < np.arange(n)[:, None]
        return np.broadcast_to(x.astype(np.float32), (P, n, n)).copy()

    return {"cos": cos, "sin": sin, "masks": masks, "ident": np.eye(P, dtype=np.float32),
            "spread": spread.reshape(96, 25 * P), "lower4": lower(4), "lower8": lower(8),
            "numbers": np.broadcast_to(np.arange(64, dtype=np.float32), (P, 64)).copy(),
            "pnum": np.arange(P, dtype=np.float32)[:, None]}


def lay_out(inputs):
    a = {k: np.asarray(v) for k, v in inputs.items()}

    def columns(w):
        return np.ascontiguousarray(w.T.reshape(-1, P, w.shape[0]).transpose(1, 0, 2))

    out = {"x": a["L0_attn_x"].reshape(T, H)}
    for L in (L0, L1):
        for w in "qkvo":
            out[f"{L.name}_w{w}"] = columns(a[f"L{L.name[1]}_attn_W{w}"])
            b = a[f"L{L.name[1]}_attn_b{w}"]
            out[f"{L.name}_b{w}"] = np.ascontiguousarray(b.reshape(-1, min(P, b.size)).T) if w in "qk" else b
    out["l0_router"] = columns(a["L0_ffn_gate_w"])
    out["l1_router"] = np.ascontiguousarray(a["L1_ffn_gate_w"].reshape(KH, P, 64).transpose(1, 0, 2))
    out["l1_bias"] = a["L1_ffn_bias"]
    pad = np.zeros((25 * P - 18 * 176, H), np.float32)
    for dst, w, ws in (("l0_w1", "L0_ffn_W1", "L0_ffn_Ws1"), ("l0_w3", "L0_ffn_W3", "L0_ffn_Ws3")):
        x = np.concatenate([a[w].reshape(-1, H), a[ws], pad])
        out[dst] = np.ascontiguousarray(x.reshape(25, P, KH, P).transpose(3, 0, 2, 1)).reshape(P, 25 * H)
    x = np.concatenate([a["L0_ffn_W2"].transpose(0, 2, 1).reshape(-1, H), a["L0_ffn_Ws2"].T, pad])
    out["l0_w2"] = np.ascontiguousarray(x.reshape(25, P, H).transpose(1, 0, 2)).reshape(P, 25 * H)
    gu = np.concatenate([a["L1_ffn_w_gate"], a["L1_ffn_w_up"]], -1)
    out["l1_w_up"] = np.ascontiguousarray(gu.reshape(32, 2, KH, P, 192).transpose(0, 3, 1, 2, 4))
    out["l1_w_down"] = np.ascontiguousarray(a["L1_ffn_w_down"].reshape(32, 2, 96, H).transpose(0, 2, 1, 3))
    for dst, w in (("l1_wsg", "L1_ffn_ws_gate"), ("l1_wsu", "L1_ffn_ws_up")):
        out[dst] = np.ascontiguousarray(a[w].reshape(KH, P, 96).transpose(1, 0, 2))
    out["l1_wsd"] = a["L1_ffn_ws_down"]
    out.update(shape_constants())
    return out


def kernel(**inputs):
    import concourse.bacc as _bacc
    from concourse.bass_utils import run_bass_kernel_spmd as _run

    nc = _bacc.Bacc("TRN2", target_bir_lowering=False, num_devices=1)
    arrays, d = {}, {}
    for name, a in lay_out(inputs).items():
        a = np.ascontiguousarray(a)
        arrays[f"in_{name}"] = a
        d[name] = nc.dram_tensor(f"in_{name}", a.shape, mybir.dt.from_np(a.dtype), kind="ExternalInput").ap()
    d["out"] = nc.dram_tensor("out_0", [T, H], F32, kind="ExternalOutput").ap()
    build(nc, d)
    r = _run(nc, [arrays], core_ids=[0])
    return r.results[0]["out_0"].reshape(B, S, H)
```
